# Optimizing a Trainium2 kernel written in Bass

```python
import numpy as np
import jax
import jax.numpy as jnp

def _softmax(x, axis=-1):
    return jax.nn.softmax(x, axis=axis)

def _gelu(x):
    return jax.nn.gelu(x, approximate=True)

def _silu(x):
    return jax.nn.silu(x)

def _sigmoid(x):
    return jax.nn.sigmoid(x)

def _layernorm(x, axis=-1, eps=1e-05):
    m = jnp.mean(x, axis=axis, keepdims=True)
    v = jnp.var(x, axis=axis, keepdims=True)
    return (x - m) / jnp.sqrt(v + eps)

def _scatter_add(tgt, idx, src, axis=0):
    return tgt.at[idx].add(src)

def _segment_sum(src, seg, n):
    return jax.ops.segment_sum(src, seg, n)
kernel_name = 'mk_gnn_preln_d2_gnn_r8_333e82'

def setup_inputs(seed: int=0):
    np.random.seed(seed)
    _w = jnp.asarray

    def _rec_inputs():
        import jax
        import jax.numpy as jnp
        _gk = jax.random.key(seed)
        x = -0.000202 + 1 * jax.random.normal(jax.random.fold_in(_gk, 1), (12500, 64), jnp.float32)
        _s = jax.random.randint(jax.random.fold_in(_gk, 2), (200000,), 0, 12500, jnp.int32)
        _d = jax.random.randint(jax.random.fold_in(_gk, 3), (200000,), 0, 12500, jnp.int32)
        _loop = jnp.arange(12500, dtype=jnp.int32)
        src = jnp.concatenate([_s, _d, _loop])
        dst = jnp.concatenate([_d, _s, _loop])
        _o = jnp.argsort(dst, stable=True)
        src = src[_o]
        dst = dst[_o]
        edge_attr_64 = -8.47137e-05 + 0.99988 * jax.random.normal(jax.random.fold_in(_gk, 12), (412500, 64), jnp.float32)
        return (x, src, dst, edge_attr_64)
    x, src, dst, edge_attr_64 = _rec_inputs()

    def _L0_gnn_setup():
        import jax, jax.numpy as jnp
        import numpy as np
        D = 64
        N_ATOMS = 12500
        N_BONDS = 187500

        def _gated_mlp(x, W1, b1, W2, b2, G1, g1, G2, g2):
            h = jax.nn.silu(x @ W1 + b1)
            h = jax.nn.silu(h @ W2 + b2)
            g = jax.nn.silu(x @ G1 + g1)
            g = jax.nn.sigmoid(g @ G2 + g2)
            return h * g
        key = jax.random.key(seed)
        ks = jax.random.split(key, 8)
        s = 1.0 / np.sqrt(D)
        return {'atom_features': jax.random.normal(ks[0], (N_ATOMS, D), jnp.float32), 'bond_features': jax.random.normal(ks[1], (N_BONDS, D), jnp.float32), 'W1': jax.random.normal(ks[2], (D, D), jnp.float32) * s, 'b1': jnp.zeros((D,), jnp.float32), 'W2': jax.random.normal(ks[3], (D, D), jnp.float32) * s, 'b2': jnp.zeros((D,), jnp.float32), 'G1': jax.random.normal(ks[4], (D, D), jnp.float32) * s, 'g1': jnp.zeros((D,), jnp.float32), 'G2': jax.random.normal(ks[5], (D, D), jnp.float32) * s, 'g2': jnp.zeros((D,), jnp.float32), 'bond_atom_indices': jax.random.randint(ks[6], (N_BONDS, 2), 0, N_ATOMS, jnp.int32)}
    _L0_gnn_all = _L0_gnn_setup()
    _L0_gnn_in = {k: v for k, v in _L0_gnn_all.items() if k in ('W1', 'b1', 'W2', 'b2', 'G1', 'g1', 'G2', 'g2')}
    del _L0_gnn_all

    def _L1_gnn_setup():
        import jax, jax.numpy as jnp
        import numpy as np
        N_NODES = 12500
        N_EDGES = 200000
        EMBED_DIM = 64
        NUM_HEADS = 4
        HEAD_DIM = EMBED_DIM // NUM_HEADS

        def mish(x):
            return x * jnp.tanh(jax.nn.softplus(x))
        key = jax.random.key(seed)
        ks = jax.random.split(key, 8)
        x = jax.random.normal(ks[0], (N_NODES, EMBED_DIM), dtype=jnp.float32)
        senders = jax.random.randint(ks[1], (N_EDGES,), 0, N_NODES, dtype=jnp.int32)
        receivers = jax.random.randint(ks[2], (N_EDGES,), 0, N_NODES, dtype=jnp.int32)
        sc = 1.0 / np.sqrt(EMBED_DIM)
        Ws = jax.random.normal(ks[3], (EMBED_DIM, NUM_HEADS, HEAD_DIM), dtype=jnp.float32) * sc
        bs = jnp.zeros((NUM_HEADS, HEAD_DIM), dtype=jnp.float32)
        Wr = jax.random.normal(ks[4], (EMBED_DIM, NUM_HEADS, HEAD_DIM), dtype=jnp.float32) * sc
        br = jnp.zeros((NUM_HEADS, HEAD_DIM), dtype=jnp.float32)
        aw = jax.random.normal(ks[5], (HEAD_DIM,), dtype=jnp.float32) * (1.0 / np.sqrt(HEAD_DIM))
        ab = jnp.zeros((1,), dtype=jnp.float32)
        return {'x': x, 'Ws': Ws, 'bs': bs, 'Wr': Wr, 'br': br, 'aw': aw, 'ab': ab, 'senders': senders, 'receivers': receivers}
    _L1_gnn_all = _L1_gnn_setup()
    _L1_gnn_in = {k: v for k, v in _L1_gnn_all.items() if k in ('Ws', 'bs', 'Wr', 'br', 'aw', 'ab')}
    del _L1_gnn_all
    return {'x': x, 'src': src, 'dst': dst, 'edge_attr_64': edge_attr_64, 'L0_gnn_W1': _L0_gnn_in['W1'], 'L0_gnn_b1': _L0_gnn_in['b1'], 'L0_gnn_W2': _L0_gnn_in['W2'], 'L0_gnn_b2': _L0_gnn_in['b2'], 'L0_gnn_G1': _L0_gnn_in['G1'], 'L0_gnn_g1': _L0_gnn_in['g1'], 'L0_gnn_G2': _L0_gnn_in['G2'], 'L0_gnn_g2': _L0_gnn_in['g2'], 'L1_gnn_Ws': _L1_gnn_in['Ws'], 'L1_gnn_bs': _L1_gnn_in['bs'], 'L1_gnn_Wr': _L1_gnn_in['Wr'], 'L1_gnn_br': _L1_gnn_in['br'], 'L1_gnn_aw': _L1_gnn_in['aw'], 'L1_gnn_ab': _L1_gnn_in['ab']}

def reference(x, src, dst, edge_attr_64, L0_gnn_W1, L0_gnn_b1, L0_gnn_W2, L0_gnn_b2, L0_gnn_G1, L0_gnn_g1, L0_gnn_G2, L0_gnn_g2, L1_gnn_Ws, L1_gnn_bs, L1_gnn_Wr, L1_gnn_br, L1_gnn_aw, L1_gnn_ab):
    import jax
    import jax.numpy as jnp

    def _L0_gnn_ref(atom_features, bond_features, W1, b1, W2, b2, G1, g1, G2, g2, bond_atom_indices):
        import jax, jax.numpy as jnp
        import numpy as np
        D = 64
        N_ATOMS = 12500
        N_BONDS = 187500

        def _gated_mlp(x, W1, b1, W2, b2, G1, g1, G2, g2):
            h = jax.nn.silu(x @ W1 + b1)
            h = jax.nn.silu(h @ W2 + b2)
            g = jax.nn.silu(x @ G1 + g1)
            g = jax.nn.sigmoid(g @ G2 + g2)
            return h * g
        messages = _gated_mlp(bond_features, W1, b1, W2, b2, G1, g1, G2, g2)
        recv = bond_atom_indices[:, 1]
        summed = jax.ops.segment_sum(messages, recv, num_segments=atom_features.shape[0])
        return atom_features + summed

    def _L1_gnn_ref(x, Ws, bs, Wr, br, aw, ab, senders, receivers):
        import jax, jax.numpy as jnp
        import numpy as np
        N_NODES = 12500
        N_EDGES = 200000
        EMBED_DIM = 64
        NUM_HEADS = 4
        HEAD_DIM = EMBED_DIM // NUM_HEADS

        def mish(x):
            return x * jnp.tanh(jax.nn.softplus(x))
        n = x.shape[0]
        s_proj = jnp.einsum('nf,fhd->nhd', x, Ws) + bs
        r_proj = jnp.einsum('nf,fhd->nhd', x, Wr) + br
        se = s_proj[senders]
        re = r_proj[receivers]
        logits = jnp.einsum('ehd,d->eh', mish(se + re), aw) + ab[0]
        lmax = jax.ops.segment_max(logits, receivers, num_segments=n)
        ex = jnp.exp(logits - lmax[receivers])
        denom = jax.ops.segment_sum(ex, receivers, num_segments=n)
        alpha = ex / denom[receivers]
        out = jax.ops.segment_sum(alpha[..., None] * se, receivers, num_segments=n)
        return out.reshape(n, -1)
    edge_index_t = jnp.stack([src, dst], axis=1)
    h = jnp.maximum(_layernorm(x, axis=-1), 0.0)
    x = x + _L0_gnn_ref(h, edge_attr_64, L0_gnn_W1, L0_gnn_b1, L0_gnn_W2, L0_gnn_b2, L0_gnn_G1, L0_gnn_g1, L0_gnn_G2, L0_gnn_g2, edge_index_t)
    h = jnp.maximum(_layernorm(x, axis=-1), 0.0)
    x = x + _L1_gnn_ref(h, L1_gnn_Ws, L1_gnn_bs, L1_gnn_Wr, L1_gnn_br, L1_gnn_aw, L1_gnn_ab, src, dst)
    return x

_drawn_inputs = setup_inputs


def setup_inputs(seed=0):
    import zlib

    import numpy as np

    out = dict(_drawn_inputs(seed))
    spreads = {'L0_gnn_b1': (0.0, 0.1),
     'L0_gnn_b2': (0.0, 0.1),
     'L0_gnn_g1': (0.0, 0.33),
     'L0_gnn_g2': (0.0, 0.1),
     'L1_gnn_bs': (0.0, 0.314),
     'L1_gnn_br': (0.0, 2.0)}
    factors = {'L1_gnn_Wr': 8.0, 'L1_gnn_aw': 5.338}
    for name, (base, spread) in spreads.items():
        noise = np.random.default_rng([zlib.crc32(name.encode()), seed]).standard_normal(out[name].shape)
        drawn = base * np.exp(spread * noise) if base else spread * noise
        out[name] = jnp.asarray(drawn.astype(out[name].dtype))
    for name, factor in factors.items():
        out[name] = (out[name] * factor).astype(out[name].dtype)
    return out
```

```python
import concourse.bass as bass
from concourse import mybir
from contextlib import ExitStack

f32 = mybir.dt.float32
bf16 = mybir.dt.bfloat16
i32 = mybir.dt.int32
ALU = mybir.AluOpType
ACT = mybir.ActivationFunctionType
AX = mybir.AxisListType.X

P = 128
N = 12500
F = 64
E = 412500
H = 4
HD = F // H
T = 30
CH = -(-E // (T * P))
RUN = CH * T
LAST = (E - (P - 1) * RUN) // T
G = 5
TG = T // G
PAIRS = TG // 2
GC = PAIRS * P
NG = CH * G
QF = T * F
NP, NJ = 125, 100
JB = 10
NS = NJ // JB
SB, SL = 750, 550
ROW = F + 2 * H
BIG = 1e30
EPS = 1e-5


def wait(eng, sem, value):
    if isinstance(value, int) and value <= 0:
        return
    eng.wait_ge(sem, value)


class Order:

    def __init__(self, eng, sem, base=0):
        self.eng, self.sem, self.base, self.n = eng, sem, base, 0

    def __call__(self, ins):
        self.n += 1
        ins.then_inc(self.sem, 1)
        self.eng.wait_ge(self.sem, self.base + self.n)


def last_run_split(view, run_rows):
    body = view[0:(P - 1) * RUN]
    tail = view[(P - 1) * RUN:E]
    if run_rows:
        return (body.rearrange("(p c k) f -> p c (k f)", p=P - 1, c=CH),
                tail.rearrange("(c k) f -> c (k f)", k=T))
    return body.rearrange("(p c k) -> p c k", p=P - 1, c=CH), tail.rearrange("(c k) -> c k", k=T)


def load_chunk(sp, buf, split, chunk, tail_chunk, sem):
    body, tail = split
    sp.dma_start(buf[0:112, :].unsqueeze(1), body[0:112, bass.ds(chunk, 1), :]).then_inc(sem, 16)
    sp.dma_start(buf[112:127, :].unsqueeze(1), body[112:127, bass.ds(chunk, 1), :]).then_inc(sem, 16)
    sp.dma_start(buf[127:128, :], tail[bass.ds(tail_chunk, 1), :]).then_inc(sem, 16)


def setup(nc, R, A, D):
    with ExitStack() as ctx:
        def sb(name, shape, dt=f32):
            return ctx.enter_context(nc.sbuf_tensor(name, shape, dt))

        def sem(name):
            return ctx.enter_context(nc.semaphore(name))

        xt = sb("xt", [NP, NJ, F])
        xc = sb("xc", [NP, NJ, F])
        sq = sb("sq", [NP, NJ, F])
        st1 = sb("st1", [NP, NJ])
        st2 = sb("st2", [NP, NJ])
        dsti = sb("dsti", [P, RUN], i32)
        dstf = sb("dstf", [P, RUN])
        near = sb("near", [P, 2], i32)
        nearf = sb("nearf", [P, 2])
        nid = sb("nid", [NP, NJ + 2], i32)
        nidf = sb("nidf", [NP, NJ + 2])
        smp = sb("smp", [NP, SB // NP], i32)
        smb = sb("smb", [P, SB], i32)
        junk = sb("junk", [P, SB])
        c1 = sb("c1", [NP, NJ + 2])
        blk = sb("blk", [NP, NJ + 2])
        c2 = sb("c2", [NP, NJ + 2])
        bstage = [sb(f"bstage{b}", [NP, 1], i32) for b in range(2)]
        brow = [sb(f"brow{b}", [NP, SL], i32) for b in range(2)]
        fend = sb("fend", [P, 1], i32)
        pid = sb("pid", [P, 1], i32)
        fx = sb("fx", [P, 4])
        b2row = sb("b2row", [P, 2 * F])
        bres = sb("bres", [P, 2 * F])
        bpart = [sb(f"bpart{k}", [P, 2 * F], bf16) for k in range(3)]
        endi = sb("endi", [NP, NJ], i32)
        epst = sb("epst", [P, 1])

        ld_x = sem("ld_x")
        ld_dst = sem("ld_dst")
        ld_w = sem("ld_w")
        ld_smp = sem("ld_smp")
        smp_out = sem("smp_out")
        smp_in = sem("smp_in")
        zeroed = sem("zeroed")
        pool_done = sem("pool_done")
        iotas = sem("iotas")
        staged = sem("staged")
        rowed = [sem(f"rowed{b}") for b in range(2)]
        counted = sem("counted")
        ends_ready = sem("ends_ready")
        ends_out = sem("ends_out")
        fend_in = sem("fend_in")
        var_ready = sem("var_ready")
        std_ready = sem("std_ready")
        chain = sem("chain")
        block = ctx.enter_context(nc.Block())
        samp_d, ends_d = D["samples"], D["ends"]

        @block.sync
        def _(sp):
            sp.dma_start(smp[:, :], A["dst"].rearrange("(p a k) -> p a k", p=NP, k=SL)[:, :, 0],
                         allow_slow_non_contiguous=True).then_inc(ld_smp, 16)
            sp.wait_ge(ld_smp, 16)
            sp.dma_start(samp_d.rearrange("(p a) -> p a", p=NP), smp[:, :]).then_inc(smp_out, 16)
            sp.wait_ge(zeroed, 1)
            body, tail = A["dst"][0:(P - 1) * RUN], A["dst"][(P - 1) * RUN:E]
            sp.dma_start(dsti[0:P - 1, :], body.rearrange("(p k) -> p k", k=RUN)).then_inc(ld_dst, 16)
            sp.dma_start(dsti[P - 1:P, 0:LAST * T], tail.rearrange("(a k) -> a k", a=1)).then_inc(ld_dst, 16)
            sp.dma_start(near[1:P, 0:1], body.rearrange("(p k) -> p k", k=RUN)[:, RUN - 1:RUN],
                         allow_slow_non_contiguous=True).then_inc(ld_dst, 16)
            sp.dma_start(near[0:P - 2, 1:2], body[RUN:].rearrange("(p k) -> p k", k=RUN)[:, 0:1],
                         allow_slow_non_contiguous=True).then_inc(ld_dst, 16)
            sp.dma_start(near[P - 2:P - 1, 1:2], tail[0:1].rearrange("(a k) -> a k", a=1)).then_inc(ld_dst, 16)
            sp.wait_ge(smp_out, 16)
            sp.dma_start(smb[:, :], samp_d.rearrange("(a k) -> a k", a=1).to_broadcast([P, SB])).then_inc(smp_in, 16)
            sp.dma_start(xt[:, :, :], A["x"].rearrange("(p j) f -> p j f", p=NP)).then_inc(ld_x, 16)
            sp.wait_ge(ends_ready, 1)
            sp.dma_start(ends_d.rearrange("(p j) a -> p (j a)", p=NP), endi[:, :]).then_inc(ends_out, 16)
            sp.wait_ge(ends_out, 16)

        @block.scalar
        def _(act):
            act.wait_ge(zeroed, 2)
            for k, (wa, wb) in enumerate((("L0_gnn_W1", "L0_gnn_G1"),) * 2):
                rows = slice(F * k, F * k + F)
                act.dma_start(R["w1g1"][rows, 0:F], A[wa]).then_inc(ld_w, 16)
                act.dma_start(R["w1g1"][rows, F:2 * F], A[wb]).then_inc(ld_w, 16)
            act.dma_start(R["w2g2"][0:F, 0:F], A["L0_gnn_W2"]).then_inc(ld_w, 16)
            act.dma_start(R["w2g2"][F:2 * F, F:2 * F], A["L0_gnn_G2"]).then_inc(ld_w, 16)
            act.dma_start(R["b1g1"][0:F, :], A["L0_gnn_b1"].rearrange("(p a) -> p a", a=1), allow_slow_non_contiguous=True).then_inc(ld_w, 16)
            act.dma_start(R["b1g1"][F:2 * F, :], A["L0_gnn_g1"].rearrange("(p a) -> p a", a=1), allow_slow_non_contiguous=True).then_inc(ld_w, 16)

            def row(ap):
                return ap.rearrange("(a n) -> a n", a=1)

            act.dma_start(b2row[:, 0:F], row(A["L0_gnn_b2"]).to_broadcast([P, F])).then_inc(ld_w, 16)
            act.dma_start(b2row[:, F:2 * F], row(A["L0_gnn_g2"]).to_broadcast([P, F])).then_inc(ld_w, 16)
            act.dma_start(R["wsr"][:, 0:F], A["L1_gnn_Ws"].rearrange("f h d -> f (h d)")).then_inc(ld_w, 16)
            act.dma_start(R["wsr"][:, F:2 * F], A["L1_gnn_Wr"].rearrange("f h d -> f (h d)")).then_inc(ld_w, 16)
            act.dma_start(R["bsr"][:, 0:F], row(A["L1_gnn_bs"].rearrange("h d -> (h d)")).to_broadcast([P, F])).then_inc(ld_w, 16)
            act.dma_start(R["bsr"][:, F:2 * F], row(A["L1_gnn_br"].rearrange("h d -> (h d)")).to_broadcast([P, F])).then_inc(ld_w, 16)
            for h in range(H):
                act.dma_start(R["aw"][:, h * HD:(h + 1) * HD], row(A["L1_gnn_aw"]).to_broadcast([P, HD])).then_inc(ld_w, 16)
            act.dma_start(R["ab"][:, :], row(A["L1_gnn_ab"]).to_broadcast([P, 1])).then_inc(ld_w, 16)
            act.wait_ge(var_ready, 1)
            nc.scalar.activation(st2[:, :], st1[:, :], ACT.Sqrt, bias=epst[0:NP, :], scale=1.0 / F).then_inc(std_ready, 1)
            act.wait_ge(ld_w, 16 * 19)

        @block.gpsimd
        def _(pool):
            nc.gpsimd.memset(R["ident"][:, :], 0.0).then_inc(pool_done, 1)
            nc.gpsimd.iota(nid[:, :], pattern=[[1, NJ + 2]], base=-1, channel_multiplier=NJ).then_inc(iotas, 1)
            nc.gpsimd.iota(pid[:, :], pattern=[[1, 1]], base=0, channel_multiplier=1).then_inc(iotas, 1)
            pool.wait_ge(pool_done, 1)
            nc.gpsimd.affine_select(out=R["ident"][:, :], in_=R["ident"][:, :], compare_op=ALU.not_equal, fill=1.0,
                                    base=0, pattern=[[-1, P]], channel_multiplier=1).then_inc(pool_done, 1)
            dblocks = A["dst"].rearrange("(a k) -> a k", k=SL)

            def fetch(i):
                for b in range(2):
                    pool.wait_ge(staged, i * 2 + b + 1)
                    pool.sem_inc(pool_done, 1)
                    pool.indirect_dma_start(out=brow[b][:, :], out_offset=None, in_=dblocks,
                                            in_offset=bass.IndirectOffsetOnAxis(ap=bstage[b][:, :], axis=0)).then_inc(rowed[b], 16)

            with pool.Fori(0, (NJ + 2) // 2) as i:
                fetch(i)
            pool.wait_ge(ends_out, 16)
            pool.wait_ge(ld_dst, 80)
            pool.indirect_dma_start(out=fend[:, :], out_offset=None, in_=ends_d,
                                    in_offset=bass.IndirectOffsetOnAxis(ap=dsti[:, 0:1], axis=0)).then_inc(fend_in, 16)
            pool.wait_ge(fend_in, 16)
            pool.wait_ge(pool_done, 2)

        @block.vector
        def _(dve):
            do = Order(dve, chain)
            do(nc.vector.memset(near[:, :], -1))
            nc.vector.memset(dsti[96:P, LAST * T:RUN], -1).then_inc(zeroed, 1)
            nc.vector.memset(R["w2g2"][:, :], 0.0).then_inc(zeroed, 1)
            do(nc.vector.memset(R["ones"][:, :], 1.0))
            do(nc.vector.memset(R["b2g2"][:, :, :], 0.0))
            do(nc.vector.memset(epst[:, :], EPS))
            dve.wait_ge(iotas, 2)
            do(nc.vector.tensor_copy(nidf[:, :], nid[:, :]))
            do(nc.vector.tensor_copy(fx[:, 3:4], pid[:, :]))
            dve.wait_ge(smp_in, 16)
            n0 = do.n
            with dve.Fori(0, NJ + 2) as j:
                dve.wait_ge(chain, j + n0)
                nc.vector.tensor_scalar(junk[0:NP, :], smb[0:NP, :], nidf[:, bass.ds(j, 1)], 0.0, ALU.is_le, ALU.add,
                                        accum_out=c1[:, bass.ds(j, 1)]).then_inc(chain, 1)
            do.n = n0 + NJ + 2
            dve.wait_ge(chain, do.n)
            do(nc.vector.tensor_scalar(blk[:, :], c1[:, :], -1.0, 0.0, ALU.add, ALU.max))
            n0 = do.n

            def stage(b, j, first=False):
                if not first:
                    dve.wait_ge(counted, j - 1)
                nc.vector.tensor_copy(bstage[b][:, :], blk[:, bass.ds(j, 1)]).then_inc(staged, 1)

            def count(b, j, rounds):
                dve.wait_ge(rowed[b], rounds)
                nc.vector.tensor_scalar(junk[0:NP, 0:SL], brow[b][:, :], nidf[:, bass.ds(j, 1)], 0.0, ALU.is_le, ALU.add,
                                        accum_out=c2[:, bass.ds(j, 1)]).then_inc(counted, 1)

            stage(0, 0, True)
            stage(1, 1, True)
            with dve.Fori(0, (NJ + 2) // 2 - 1) as i:
                for b in range(2):
                    count(b, i * 2 + b, i * 16 + 16)
                    stage(b, i * 2 + b + 2)
            for b in range(2):
                wait(dve, counted, NJ + b)
                count(b, NJ + b, 8 * (NJ + 2))
            dve.wait_ge(counted, NJ + 2)
            do(nc.vector.scalar_tensor_tensor(c2[:, :], blk[:, :], float(SL), c2[:, :], ALU.mult, ALU.add))
            do(nc.vector.tensor_tensor(R["pres"][:, :], c2[:, 1:NJ + 1], c2[:, 0:NJ], ALU.is_gt))
            do(nc.vector.tensor_scalar(st1[:, :], c2[:, 1:NJ + 1], -1.0, 0.0, ALU.add, ALU.max))
            do(nc.vector.tensor_copy(R["end"][:, :], st1[:, :]))
            nc.vector.tensor_copy(endi[:, :], st1[:, :]).then_inc(ends_ready, 1)
            do(nc.vector.tensor_scalar(fx[0:NP, 0:1], fx[0:NP, 3:4], float(E), None, ALU.add))
            do(nc.vector.tensor_scalar(st1[:, :], c2[:, 0:NJ], fx[0:NP, 0:1], None, ALU.subtract))
            do(nc.vector.tensor_tensor(st1[:, :], st1[:, :], R["pres"][:, :], ALU.mult))
            do(nc.vector.tensor_scalar(R["start"][:, :], st1[:, :], fx[0:NP, 0:1], None, ALU.add))
            dve.wait_ge(ld_dst, 80)
            do(nc.vector.tensor_copy(dstf[:, :], dsti[:, :]))
            do(nc.vector.tensor_copy(nearf[:, :], near[:, :]))
            do(nc.vector.memset(R["keep"][:, 0:1], 0.0))
            do(nc.vector.tensor_tensor(R["keep"][:, 1:RUN], dstf[:, 1:RUN], dstf[:, 0:RUN - 1], ALU.is_equal))
            do(nc.vector.tensor_copy(R["first"][:, :], dsti[:, 0:1]))
            do(nc.vector.tensor_tensor(R["cont"][:, :], dstf[:, 0:1], nearf[:, 0:1], ALU.is_equal))
            do(nc.vector.tensor_tensor(R["onward"][:, :], dstf[:, RUN - 1:RUN], nearf[:, 1:2], ALU.is_equal))
            do(nc.vector.tensor_tensor(R["whole"][:, :], dstf[:, 0:1], dstf[:, RUN - 1:RUN], ALU.is_equal))
            do(nc.vector.tensor_tensor(R["whole"][:, :], R["whole"][:, :], R["onward"][:, :], ALU.mult))
            dve.wait_ge(fend_in, 16)
            do(nc.vector.tensor_copy(fx[:, 0:1], fend[:, :]))
            do(nc.vector.tensor_scalar(fx[:, 1:2], fx[:, 3:4], float(RUN), float(RUN), ALU.mult, ALU.add))
            do(nc.vector.tensor_tensor(fx[:, 1:2], fx[:, 0:1], fx[:, 1:2], ALU.is_lt))
            do(nc.vector.tensor_tensor(fx[:, 1:2], fx[:, 1:2], R["cont"][:, :], ALU.mult))
            do(nc.vector.tensor_scalar(fx[:, 2:3], fx[:, 3:4], float(E), None, ALU.add))
            do(nc.vector.tensor_tensor(fx[:, 0:1], fx[:, 0:1], fx[:, 2:3], ALU.subtract))
            do(nc.vector.tensor_tensor(fx[:, 0:1], fx[:, 0:1], fx[:, 1:2], ALU.mult))
            do(nc.vector.tensor_tensor(R["mend"][:, :], fx[:, 0:1], fx[:, 2:3], ALU.add))
            dve.wait_ge(ld_w, 16 * 19)
            do(nc.vector.tensor_copy(bpart[0][:, :], b2row[:, :]))
            do(nc.vector.tensor_tensor(bres[:, :], b2row[:, :], bpart[0][:, :], ALU.subtract))
            do(nc.vector.tensor_copy(bpart[1][:, :], bres[:, :]))
            do(nc.vector.tensor_tensor(bres[:, :], bres[:, :], bpart[1][:, :], ALU.subtract))
            do(nc.vector.tensor_copy(bpart[2][:, :], bres[:, :]))
            for k in range(3):
                row = slice(32 * k, 32 * k + 1)
                do(nc.vector.tensor_copy(R["b2g2"][row, :, :], bpart[k][row, :].unsqueeze(1).to_broadcast([1, TG // 2, 2 * F])))
            dve.wait_ge(ld_x, 16)
            do(nc.vector.tensor_reduce(st1[:, :], xt[:, :, :], AX, ALU.add))
            do(nc.vector.tensor_scalar(st1[:, :], st1[:, :], 1.0 / F, None, ALU.mult))
            do(nc.vector.tensor_tensor(xc[:, :, :], xt[:, :, :], st1[:, :].unsqueeze(2).to_broadcast([NP, NJ, F]), ALU.subtract))
            do(nc.vector.tensor_tensor(sq[:, :, :], xc[:, :, :], xc[:, :, :], ALU.mult))
            nc.vector.tensor_reduce(st1[:, :], sq[:, :, :], AX, ALU.add).then_inc(var_ready, 1)
            dve.wait_ge(std_ready, 1)
            do(nc.vector.reciprocal(st1[:, :], st2[:, :]))
            do(nc.vector.tensor_tensor(xc[:, :, :], xc[:, :, :], st1[:, :].unsqueeze(2).to_broadcast([NP, NJ, F]), ALU.mult))
            do(nc.vector.scalar_tensor_tensor(R["base"][:, :, :], xc[:, :, :], 0.0, xt[:, :, :], ALU.max, ALU.add))


def edge_mlp(nc, R, A, D):
    with ExitStack() as ctx:
        def sb(name, shape, dt=f32):
            return ctx.enter_context(nc.sbuf_tensor(name, shape, dt))

        def sem(name):
            return ctx.enter_context(nc.semaphore(name))

        edges = [sb(f"edges{b}", [P, QF]) for b in range(2)]
        edges_t = [sb(f"edges_t{b}", [P, GC]) for b in range(2)]
        hidden = [sb(f"hidden{b}", [P, 2, GC]) for b in range(2)]
        value = [sb(f"value{b}", [P, TG, F]) for b in range(2)]
        gate = [sb(f"gate{b}", [P, TG, F]) for b in range(2)]
        msg = [sb(f"msg{b}", [P, F, T]) for b in range(2)]
        keepf = [sb(f"keepf{b}", [P, F, T]) for b in range(2)]
        sums = [sb(f"sums{b}", [P, F, T]) for b in range(2)]
        rows = [sb(f"rows{b}", [P, T, F]) for b in range(2)]
        tr_ps = [ctx.enter_context(nc.psum_tensor(f"tr_ps{b}", [P, 512], f32)) for b in range(2)]
        h_ps = ctx.enter_context(nc.psum_tensor("h_ps", [P, 2, 512], f32))
        o_ps = [ctx.enter_context(nc.psum_tensor(f"o_ps{b}", [P, 2, 512], f32)) for b in range(2)]

        loaded = [sem(f"loaded{b}") for b in range(2)]
        transposed = sem("transposed")
        edges_t_ready = sem("edges_t_ready")
        h_ready = sem("h_ready")
        hidden_ready = sem("hidden_ready")
        o_ready = sem("o_ready")
        gated = sem("gated")
        msg_ready = sem("msg_ready")
        carried = sem("carried")
        scanned = sem("scanned")
        turn = sem("turn")
        keepf_ready = sem("keepf_ready")
        zeroed = sem("zeroed")
        rows_ready = sem("rows_ready")
        stored = [sem(f"stored{b}") for b in range(2)]
        block = ctx.enter_context(nc.Block())
        split = last_run_split(A["edge_attr_64"], True)
        sums_d = D["sums"][0:P * RUN, :].rearrange("(p c k) f -> p c (k f)", p=P, c=CH)
        HALF = CH // 2
        PIECES = 4

        @block.sync
        def _(sp):
            def load(i, b, tail):
                load_chunk(sp, edges[b], split, i * 2 + b, tail, loaded[b])

            def store(c, b):
                sp.wait_ge(rows_ready, c + 1)
                sp.dma_start(sums_d[:, bass.ds(c, 1), :], rows[b][:, :, :].rearrange("p k f -> p (k f)").unsqueeze(1)).then_inc(stored[b], 16)

            def body(i, padded=False, first=False, last=False):
                for b in range(2):
                    if not last:
                        sp.wait_ge(transposed, (i * 2 + b + 1) * G)
                        load(i + 1, b, LAST - 1 if padded else (i + 1) * 2 + b)
                    if not (first and b == 0):
                        store(i * 2 + b - 1, 1 - b)

            load(0, 0, 0)
            load(0, 1, 1)
            body(0, first=True)
            with sp.Fori(1, LAST // 2 - 1) as i:
                body(i)
            with sp.Fori(LAST // 2 - 1, HALF - 1) as i:
                body(i, padded=True)
            body(HALF - 1, last=True)
            store(CH - 1, 1)
            for b in range(2):
                sp.wait_ge(stored[b], 16 * HALF)

        @block.tensor
        def _(pe):
            def transpose(i, s):
                i, s = i + s // (2 * G), s % (2 * G)
                b, g = s // G, s % G
                if g == 0:
                    pe.wait_ge(loaded[b], i * 48 + 48)
                for j in range(PAIRS):
                    at = (g * TG + 2 * j) * F
                    last = nc.tensor.transpose(tr_ps[s % 2][:, j * P:(j + 1) * P], edges[b][:, at:at + 2 * F], R["ident"][:, :])
                last.then_inc(transposed, 1)

            def layer1(i, s):
                n = i * 2 * G + s
                pe.wait_ge(edges_t_ready, n + 1)
                wait(pe, hidden_ready, n)
                for a in range(2):
                    half = slice(F * a, F * a + F)
                    last = nc.tensor.matmul(h_ps[:, a, 0:GC], R["w1g1"][half, :], edges_t[s % 2][half, :], start=True, stop=True)
                last.then_inc(h_ready, 1)

            def layer2(i, s):
                n = i * 2 * G + s
                pe.wait_ge(hidden_ready, n + 1)
                wait(pe, gated, 2 * (n - 1))
                out, hid = o_ps[s % 2], hidden[s % 2]
                for k in range(2):
                    nc.tensor.matmul(out[:, k, 0:GC], R["ones"][:, :], R["b2g2"][:, :, :].rearrange("p a n -> p (a n)"),
                                     start=True, stop=False)
                    for m in range(PAIRS):
                        tile = k * PAIRS + m
                        at = (tile // 2) * P
                        last = nc.tensor.matmul(out[:, k, m * P:(m + 1) * P], hid[:, tile % 2, at:at + P], R["w2g2"][:, :],
                                                start=False, stop=m == PAIRS - 1)
                last.then_inc(o_ready, 1)

            def body(i, last=False):
                for s in range(2 * G):
                    if not (last and s + 1 >= 2 * G):
                        layer1(i + (s + 1) // (2 * G), (s + 1) % (2 * G))
                    if not (last and s + 2 >= 2 * G):
                        transpose(i, s + 2)
                    layer2(i, s)

            transpose(0, 0)
            transpose(0, 1)
            layer1(0, 0)
            body(0)
            with pe.Fori(1, HALF - 1) as i:
                body(i)
            body(HALF - 1, last=True)

        @block.scalar
        def _(act):
            def hid(i, s):
                n = i * 2 * G + s
                act.wait_ge(h_ready, n + 1)
                nc.scalar.activation(hidden[s % 2][:, :, :], h_ps[:, :, 0:GC], ACT.Silu, bias=R["b1g1"][:, :]).then_inc(hidden_ready, 1)

            def outs(i, s):
                n = i * 2 * G + s
                act.wait_ge(o_ready, n + 1)
                wait(act, msg_ready, n - 1)
                o = o_ps[s % 2][:, :, 0:GC].rearrange("p k (m c) -> p k m c", c=P)
                v, g = (x[s % 2][:, :, :].rearrange("p (k m) f -> p k m f", k=2) for x in (value, gate))
                nc.scalar.activation(v, o[:, :, :, 0:F], ACT.Silu).then_inc(gated, 1)
                nc.scalar.activation(g, o[:, :, :, F:2 * F], ACT.Tanh, scale=0.5).then_inc(gated, 1)

            def body(i, last=False):
                for s in range(2 * G):
                    if not (last and s + 1 >= 2 * G):
                        hid(i + (s + 1) // (2 * G), (s + 1) % (2 * G))
                    outs(i, s)

            hid(0, 0)
            body(0)
            with act.Fori(1, HALF - 1) as i:
                body(i)
            body(HALF - 1, last=True)

        @block.vector
        def _(dve):
            def copy_t(i, s):
                n = i * 2 * G + s
                dve.wait_ge(transposed, n + 1)
                nc.vector.tensor_copy(edges_t[s % 2][:, :], tr_ps[s % 2][:, 0:GC]).then_inc(edges_t_ready, 1)

            def product(i, s):
                n = i * 2 * G + s
                b, g = s // G, s % G
                dve.wait_ge(gated, 2 * (n + 1))
                if g == 0:
                    wait(dve, scanned, (i * 2 + b - 1) * PIECES)
                out = msg[b][:, :, g * TG:(g + 1) * TG].rearrange("p f t -> p t f")
                nc.vector.scalar_tensor_tensor(out, gate[s % 2][:, :, :], 1.0, value[s % 2][:, :, :], ALU.add, ALU.mult)\
                    .then_inc(msg_ready, 1)

            def carry(c, b):
                dve.wait_ge(msg_ready, (c + 1) * G)
                wait(dve, scanned, c * PIECES)
                nc.vector.scalar_tensor_tensor(msg[b][:, :, 0], sums[1 - b][:, :, T - 1], R["keep"][:, bass.ds(c * T, 1)],
                                               msg[b][:, :, 0], ALU.mult, ALU.add).then_inc(carried, 1)

            def scan(c, b, k):
                if k == 0:
                    dve.wait_ge(carried, c + 1)
                    dve.wait_ge(keepf_ready, c + 1)
                    wait(dve, rows_ready, c - 1)
                fs = slice(k * F // PIECES, (k + 1) * F // PIECES)
                flat = [x[:, fs, :].rearrange("p f t -> p (f t)") for x in (sums[b], keepf[b], msg[b])]
                nc.vector.tensor_tensor_scan(flat[0], flat[1], flat[2], 0.0, ALU.mult, ALU.add).then_inc(scanned, 1)

            def body(i, first=False, last=False):
                for s in range(2 * G):
                    if not (last and s + 2 >= 2 * G):
                        copy_t(i + (s + 2) // (2 * G), (s + 2) % (2 * G))
                    product(i, s)
                    b, g = s // G, s % G
                    if not (first and b == 0):
                        c = i * 2 + b - 1
                        if g == 0:
                            carry(c, 1 - b)
                        else:
                            scan(c, 1 - b, g - 1)

            nc.vector.memset(sums[1][:, :, :], 0.0).then_inc(zeroed, 1)
            for b in range(2):
                nc.vector.memset(keepf[b][:, :, :], 0.0).then_inc(zeroed, 1)
            dve.wait_ge(zeroed, 3)
            copy_t(0, 0)
            copy_t(0, 1)
            body(0, first=True)
            with dve.Fori(1, HALF - 1) as i:
                body(i)
            body(HALF - 1, last=True)
            carry(CH - 1, 1)
            for k in range(PIECES):
                scan(CH - 1, 1, k)
            dve.wait_ge(scanned, CH * PIECES)
            nc.vector.tensor_copy(R["state"][:, 0:F], sums[1][:, :, T - 1]).then_inc(zeroed, 1)

        @block.gpsimd
        def _(pool):
            def spread_keep(c, b):
                src = R["keep"][:, bass.ds(c * T + 1, T - 1)].unsqueeze(1).to_broadcast([P, F, T - 1])
                pool.sem_inc(turn, 1)
                nc.gpsimd.tensor_copy(keepf[b][:, :, 1:T], src).then_inc(keepf_ready, 1)

            def to_rows(i, b, first=False):
                c = i * 2 + b
                if not first:
                    pool.wait_ge(stored[b], i * 16)
                pool.wait_ge(scanned, (c + 1) * PIECES)
                pool.sem_inc(turn, 1)
                nc.gpsimd.tensor_copy(rows[b][:, :, :], sums[b][:, :, :].rearrange("p f t -> p t f")).then_inc(rows_ready, 1)

            pool.wait_ge(zeroed, 3)
            spread_keep(0, 0)
            spread_keep(1, 1)
            for b in range(2):
                to_rows(0, b, first=True)
                spread_keep(2 + b, b)
            with pool.Fori(1, HALF - 1) as i:
                for b in range(2):
                    to_rows(i, b)
                    spread_keep(i * 2 + b + 2, b)
            for b in range(2):
                to_rows(HALF - 1, b)


def update_nodes(nc, R, A, D):
    with ExitStack() as ctx:
        def sb(name, shape, dt=f32):
            return ctx.enter_context(nc.sbuf_tensor(name, shape, dt))

        def ps(name, shape):
            return ctx.enter_context(nc.psum_tensor(name, shape, f32))

        def sem(name):
            return ctx.enter_context(nc.semaphore(name))

        onw = sb("onw", [P, F])
        whl = sb("whl", [P, F])
        whl_t = sb("whl_t", [F, P])
        cin_t = sb("cin_t", [F, P + 1])
        got = sb("got", [P, F])
        half = sb("half", [NP, NJ])
        ends = [sb(f"ends{b}", [NP, JB], i32) for b in range(2)]
        starts = [sb(f"starts{b}", [NP, JB], i32) for b in range(2)]
        agg = [sb(f"agg{b}", [NP, JB, F]) for b in range(2)]
        x1 = sb("x1", [NP, JB, F])
        xc = sb("xc2", [NP, JB, F])
        sq = sb("sq2", [NP, JB, F])
        st = sb("st", [NP, JB])
        std = sb("std", [NP, JB])
        hh = sb("hh", [NP, JB, F])
        hT = sb("hT", [F, JB, NP])
        sr = [sb(f"sr{b}", [NP, JB, 2 * F]) for b in range(2)]
        epst = sb("epst2", [NP, 1])
        heads = sb("heads", [P, F])
        onw_bank, whl_bank = ps("onw_bank", [P, 512]), ps("whl_bank", [P, 512])
        onw_ps, whl_ps, back_ps = onw_bank[0:F, 0:P], whl_bank[0:F, 0:P], onw_bank[:, 0:F]
        hT_ps = ps("hT_ps", [F, 3, 512])
        pr_ps = ps("pr_ps", [NP, 3, 512])
    
        chain = sem("chain")
        scaled = sem("scaled")
        turned = sem("turned")
        cin_ready = sem("cin_ready")
        cin_back = sem("cin_back")
        got_in = sem("got_in")
        mended = sem("mended")
        mended_out = sem("mended_out")
        staged = sem("staged")
        turn = sem("turn")
        gathered = [sem(f"gathered{b}") for b in range(2)]
        var_ready = sem("var_ready")
        std_ready = sem("std_ready")
        h_ready = sem("h_ready")
        hT_in_ps = sem("hT_in_ps")
        hT_part = sem("hT_part")
        hT_ready = sem("hT_ready")
        pr_in_ps = sem("pr_in_ps")
        sr_ready = sem("sr_ready")
        tabled = [sem(f"tabled{b}") for b in range(2)]
        scattered = [sem(f"scattered{b}") for b in range(2)]
        heads_in = sem("heads_in")
        heads_out = sem("heads_out")
        block = ctx.enter_context(nc.Block())
        sums_d = D["sums"]
        s_tab = D["s_proj"].rearrange("(p j) f -> p j f", p=NP)
        r_tab = D["r_proj"].rearrange("(p j) f -> p j f", p=NP)

        @block.sync
        def _(sp):
            def tables(i):
                for b in range(2):
                    k = i * 2 + b
                    sp.wait_ge(sr_ready, k + 1)
                    sp.dma_start(s_tab[:, bass.ds(k * JB, JB), :], sr[b][:, :, 0:F]).then_inc(tabled[b], 16)
                    sp.dma_start(r_tab[:, bass.ds(k * JB, JB), :], sr[b][:, :, F:2 * F]).then_inc(tabled[b], 16)

            with sp.Fori(0, NS // 2) as i:
                tables(i)
            sp.wait_ge(heads_in, 16)
            for b in range(2):
                sp.wait_ge(scattered[b], 16 * JB * NS // 2)
            sp.dma_start(sums_d[0:P * RUN, :].rearrange("(p k) f -> p k f", p=P)[:, 0:1, :], heads[:, :].unsqueeze(1)).then_inc(heads_out, 16)
            sp.wait_ge(heads_out, 16)

        @block.gpsimd
        def _(pool):
            at = lambda ap: bass.IndirectOffsetOnAxis(ap=ap, axis=0)
            pool.indirect_dma_start(out=got[:, :], out_offset=None, in_=sums_d, in_offset=at(R["mend"][:, :])).then_inc(got_in, 16)
            pool.wait_ge(mended, 1)
            pool.indirect_dma_start(out=sums_d, out_offset=at(R["mend"][:, :]), in_=got[:, :], in_offset=None).then_inc(mended_out, 16)
            pool.wait_ge(mended_out, 16)

            def gather(k, b):
                pool.wait_ge(staged, k + 1)
                pool.sem_inc(turn, 1)
                for m in range(JB):
                    pool.indirect_dma_start(out=agg[b][:, m, :], out_offset=None, in_=sums_d, in_offset=at(ends[b][:, m:m + 1])).then_inc(gathered[b], 16)

            def scatter(k, b):
                pool.wait_ge(sr_ready, k + 1)
                pool.sem_inc(turn, 1)
                for m in range(JB):
                    pool.indirect_dma_start(out=sums_d, out_offset=at(starts[b][:, m:m + 1]), in_=sr[b][:, m, F:2 * F], in_offset=None)\
                        .then_inc(scattered[b], 16)

            gather(0, 0)
            gather(1, 1)
            with pool.Fori(0, NS // 2 - 1) as i:
                for b in range(2):
                    scatter(i * 2 + b, b)
                    gather(i * 2 + b + 2, b)
            for b in range(2):
                scatter(NS - 2 + b, b)
            for b in range(2):
                pool.wait_ge(tabled[b], 32 * NS // 2)
            pool.indirect_dma_start(out=heads[:, :], out_offset=None, in_=D["r_proj"], in_offset=at(R["first"][:, :])).then_inc(heads_in, 16)
            pool.wait_ge(heads_in, 16)

        @block.tensor
        def _(pe):
            pe.wait_ge(scaled, 2)
            nc.tensor.transpose(onw_ps, onw[:, :], R["ident"][:, :])
            nc.tensor.transpose(whl_ps, whl[:, :], R["ident"][:, :]).then_inc(turned, 1)
            pe.wait_ge(cin_ready, 1)
            nc.tensor.transpose(back_ps, cin_t[:, 0:P], R["ident"][0:F, 0:F]).then_inc(cin_back, 1)

            def step(k):
                pe.wait_ge(h_ready, k + 1)
                pe.sem_inc(turn, 1)
                for j in range(JB):
                    last = nc.tensor.transpose(hT_ps[:, j // 4, (j % 4) * NP:(j % 4 + 1) * NP], hh[:, j, :], R["ident"][0:NP, 0:NP])
                last.then_inc(hT_in_ps, 1)
                pe.wait_ge(hT_ready, k + 1)
                wait(pe, sr_ready, k)
                for j in range(JB):
                    last = nc.tensor.matmul(pr_ps[:, j // 4, (j % 4) * P:(j % 4 + 1) * P], hT[:, j, :], R["wsr"][:, :], start=True, stop=True)
                last.then_inc(pr_in_ps, 1)

            step(0)
            with pe.Fori(1, NS) as k:
                step(k)

        @block.scalar
        def _(act):
            def step(k):
                act.wait_ge(var_ready, k + 1)
                nc.scalar.activation(std[:, :], st[:, :], ACT.Sqrt, bias=epst[:, :], scale=1.0 / F).then_inc(std_ready, 1)
                act.wait_ge(hT_in_ps, k + 1)
                for q, w in enumerate((4, 4, 2)):
                    nc.scalar.activation(hT[:, 4 * q:4 * q + w, :], hT_ps[:, q, 0:w * NP].rearrange("f (j n) -> f j n", n=NP), ACT.Copy)\
                        .then_inc(hT_part, 1)
                act.wait_ge(hT_part, k * 3 + 3)
                act.sem_inc(hT_ready, 1)

            act.wait_ge(scaled, 2)
            with act.Fori(0, NS) as k:
                step(k)

        @block.vector
        def _(dve):
            do = Order(dve, chain)
            do(nc.vector.memset(epst[:, :], EPS))
            do(nc.vector.tensor_scalar(half[:, :], R["pres"][:, :], 0.5, None, ALU.mult))
            nc.vector.tensor_scalar(onw[:, :], R["state"][:, 0:F], R["onward"][:, :], None, ALU.mult).then_inc(scaled, 1)
            nc.vector.tensor_copy(whl[:, :], R["whole"][:, :].to_broadcast([P, F])).then_inc(scaled, 1)
            do(nc.vector.memset(cin_t[:, 0:1], 0.0))
            dve.wait_ge(turned, 1)
            do(nc.vector.tensor_copy(whl_t[:, :], whl_ps))
            nc.vector.tensor_tensor_scan(cin_t[:, 1:P + 1], whl_t[:, :], onw_ps, 0.0, ALU.mult, ALU.add).then_inc(cin_ready, 1)
            dve.wait_ge(cin_back, 1)
            dve.wait_ge(got_in, 16)
            nc.vector.tensor_tensor(got[:, :], got[:, :], back_ps, ALU.add).then_inc(mended, 1)

            def stage(k, b):
                nc.vector.tensor_copy(ends[b][:, :], R["end"][:, bass.ds(k * JB, JB)]).then_inc(staged, 1)

            def step(i, b, more=True, first=False):
                k = i * 2 + b
                do = Order(dve, chain, k * STEP + base)
                cols = bass.ds(k * JB, JB)
                wide = [NP, JB, F]
                dve.wait_ge(gathered[b], i * 16 * JB + 16 * JB)
                do(nc.vector.tensor_tensor(x1[:, :, :], agg[b][:, :, :], half[:, cols].unsqueeze(2).to_broadcast(wide), ALU.mult))
                do(nc.vector.tensor_tensor(x1[:, :, :], x1[:, :, :], R["base"][:, cols, :], ALU.add))
                do(nc.vector.tensor_reduce(st[:, :], x1[:, :, :], AX, ALU.add))
                do(nc.vector.tensor_scalar(st[:, :], st[:, :], 1.0 / F, None, ALU.mult))
                do(nc.vector.tensor_tensor(xc[:, :, :], x1[:, :, :], st[:, :].unsqueeze(2).to_broadcast(wide), ALU.subtract))
                do(nc.vector.tensor_tensor(sq[:, :, :], xc[:, :, :], xc[:, :, :], ALU.mult))
                nc.vector.tensor_reduce(st[:, :], sq[:, :, :], AX, ALU.add).then_inc(var_ready, 1)
                dve.wait_ge(std_ready, k + 1)
                do(nc.vector.reciprocal(st[:, :], std[:, :]))
                do(nc.vector.tensor_tensor(xc[:, :, :], xc[:, :, :], st[:, :].unsqueeze(2).to_broadcast(wide), ALU.mult))
                nc.vector.tensor_scalar(hh[:, :, :], xc[:, :, :], 0.0, None, ALU.max).then_inc(h_ready, 1)
                do(nc.vector.tensor_copy(R["base"][:, cols, :], x1[:, :, :]))
                if not first:
                    dve.wait_ge(scattered[b], i * 16 * JB)
                    dve.wait_ge(tabled[b], i * 32)
                do(nc.vector.tensor_copy(starts[b][:, :], R["start"][:, cols]))
                dve.wait_ge(pr_in_ps, k + 1)
                for q, w in enumerate((4, 4, 2)):
                    do(nc.vector.tensor_tensor(sr[b][:, 4 * q:4 * q + w, :], pr_ps[:, q, 0:w * P].rearrange("n (j c) -> n j c", c=P),
                                               R["bsr"][0:NP, :].unsqueeze(1).to_broadcast([NP, w, 2 * F]), ALU.add))
                dve.sem_inc(sr_ready, 1)
                if more:
                    stage(k + 2, b)
                assert do.n == STEP

            base = do.n
            STEP = 13
            stage(0, 0)
            stage(1, 1)
            for b in range(2):
                step(0, b, first=True)
            with dve.Fori(1, NS // 2 - 1) as i:
                for b in range(2):
                    step(i, b)
            for b in range(2):
                step(NS // 2 - 1, b, more=False)


def attention(nc, R, A, D):
    with ExitStack() as ctx:
        def sb(name, shape, dt=f32):
            return ctx.enter_context(nc.sbuf_tensor(name, shape, dt))

        def sem(name):
            return ctx.enter_context(nc.semaphore(name))

        U = 4
        srci = sb("srci", [P, RUN], i32)
        idx = [sb(f"idx{u}", [P, T], i32) for u in range(U)]
        se = [sb(f"se{u}", [P, T, F]) for u in range(U)]
        rs = [sb(f"rs{b}", [P, T, F]) for b in range(2)]
        keepf = [sb(f"akeepf{b}", [P, F, T]) for b in range(2)]
        rnew = sb("rnew", [P, F, T])
        rneg = sb("rneg", [P, F, T])
        z = [sb(f"z{b}", [P, F, T]) for b in range(2)]
        t1 = sb("t1", [P, F, T])
        t2 = sb("t2", [P, F, T])
        decf = sb("decf", [P, F, T])
        wse = sb("wse", [P, F, T])
        num = sb("num", [P, F, T])
        lg = sb("lg", [P, H, T])
        kneg = sb("kneg", [P, T])
        mx = sb("mx", [P, H, T + 1])
        den = sb("den", [P, H, T + 1])
        exin = sb("exin", [P, 2, H, T])
        ex = sb("ex", [P, 2, H, T])
        dec = sb("dec", [P, H, T])
        tmp = sb("tmp", [P, F])
        halfc = sb("halfc", [P, 1])
        rows = [sb(f"arows{b}", [P, T, ROW]) for b in range(2)]

        src_in = sem("src_in")
        padded = sem("padded")
        inited = sem("inited")
        idx_ready = sem("idx_ready")
        turn = sem("turn")
        gathered = [sem(f"agathered{u}") for u in range(U)]
        rs_in = [sem(f"rs_in{b}") for b in range(2)]
        rnew_ready = sem("rnew_ready")
        chain = sem("chain")
        keepf_ready = sem("keepf_ready")
        carried = sem("carried")
        held = sem("held")
        z_ready = sem("z_ready")
        steps = sem("steps")
        q_ready = sem("q_ready")
        rec_ready = sem("rec_ready")
        ratio_ready = sem("ratio_ready")
        exin_ready = sem("exin_ready")
        ex_ready = sem("ex_ready")
        dec_ready = sem("dec_ready")
        decf_ready = sem("decf_ready")
        se_used = sem("se_used")
        summed = sem("summed")
        rows_ready = sem("rows_ready")
        stored = [sem(f"astored{b}") for b in range(2)]
        block = ctx.enter_context(nc.Block())
        NI = CH // U
        rs_d = D["sums"][0:P * RUN, :].rearrange("(p c k) f -> p c (k f)", p=P, c=CH)
        st_d = D["states"][0:P * RUN, :].rearrange("(p c k) f -> p c (k f)", p=P, c=CH)

        @block.sync
        def _(sp):
            sp.wait_ge(padded, 1)
            sp.dma_start(srci[0:P - 1, :], A["src"][0:(P - 1) * RUN].rearrange("(p k) -> p k", k=RUN)).then_inc(src_in, 16)
            sp.dma_start(srci[P - 1:P, 0:LAST * T], A["src"][(P - 1) * RUN:E].rearrange("(a k) -> a k", a=1)).then_inc(src_in, 16)

            def load(c, b):
                sp.dma_start(rs[b][:, :, :].rearrange("p k f -> p (k f)").unsqueeze(1), rs_d[:, bass.ds(c, 1), :]).then_inc(rs_in[b], 16)

            def store(c, b):
                sp.wait_ge(rows_ready, (c + 1) * 3)
                sp.dma_start(st_d[:, bass.ds(c, 1), :], rows[b][:, :, :].rearrange("p k f -> p (k f)").unsqueeze(1)).then_inc(stored[b], 16)

            def body(i, first=False, last=False):
                for u in range(U):
                    c = i * U + u
                    if not (last and u + 2 >= U):
                        sp.wait_ge(rnew_ready, c + 1)
                        load(c + 2, u % 2)
                    if not (first and u == 0):
                        store(c - 1, 1 - u % 2)

            load(0, 0)
            load(1, 1)
            body(0, first=True)
            with sp.Fori(1, NI - 1) as i:
                body(i)
            body(NI - 1, last=True)
            store(CH - 1, 1)
            for b in range(2):
                sp.wait_ge(stored[b], 16 * CH // 2)

        @block.gpsimd
        def _(pool):
            def gather(i, u, first=False):
                c = i * U + u
                if not first:
                    pool.wait_ge(se_used, c - U + 1)
                pool.wait_ge(idx_ready, c + 1)
                pool.sem_inc(turn, 1)
                for k in range(T):
                    pool.indirect_dma_start(out=se[u][:, k, :], out_offset=None, in_=D["s_proj"],
                                            in_offset=bass.IndirectOffsetOnAxis(ap=idx[u][:, k:k + 1], axis=0)).then_inc(gathered[u], 16)

            for u in range(U):
                gather(0, u, first=True)
            with pool.Fori(1, NI) as i:
                for u in range(U):
                    gather(i, u)
            for u in range(U):
                pool.wait_ge(gathered[u], 16 * T * NI)

        @block.scalar
        def _(act):
            def spread(c, b):
                src = R["keep"][:, bass.ds(c * T + 1, T - 1)].unsqueeze(1).to_broadcast([P, F, T - 1])
                nc.scalar.activation(keepf[b][:, :, 1:T], src, ACT.Copy).then_inc(keepf_ready, 1)

            def index(c, u):
                nc.scalar.activation(idx[u][:, :], srci[:, bass.ds(c * T, T)], ACT.Copy).then_inc(idx_ready, 1)

            def body(i, first=False, last=False):
                for u in range(U):
                    b = u % 2
                    c = i * U + u
                    act.wait_ge(z_ready, c + 1)
                    nc.scalar.activation(t1[:, :, :], z[b][:, :, :], ACT.Tanh, scale=0.5).then_inc(steps, 1)
                    act.wait_ge(steps, c * 3 + 1)
                    nc.scalar.activation(t1[:, :, :], t1[:, :, :], ACT.Square, scale=-0.5, bias=halfc[:, :]).then_inc(steps, 1)
                    act.wait_ge(steps, c * 3 + 2)
                    nc.scalar.activation(t1[:, :, :], t1[:, :, :], ACT.Copy, bias=1.0).then_inc(q_ready, 1)
                    if not (last and u + 2 >= U):
                        wait(act, held, c + 1)
                        spread(c + 2, b)
                    if not last:
                        act.wait_ge(gathered[u], i * 16 * T + 16 * T)
                        index(c + U, u)
                    act.wait_ge(rec_ready, c + 1)
                    nc.scalar.activation(t2[:, :, :], t1[:, :, :], ACT.Copy, scale=2.0, bias=-1.0).then_inc(steps, 1)
                    act.wait_ge(steps, c * 3 + 3)
                    act.sem_inc(ratio_ready, 1)
                    act.wait_ge(exin_ready, c + 1)
                    nc.scalar.activation(ex[:, :, :, :], exin[:, :, :, :], ACT.Exp).then_inc(ex_ready, 1)
                    act.wait_ge(dec_ready, c + 1)
                    nc.scalar.activation(decf[:, :, 1:T].rearrange("p (h d) t -> p h d t", h=H),
                                         dec[:, :, 1:T].unsqueeze(2).to_broadcast([P, H, HD, T - 1]), ACT.Copy).then_inc(decf_ready, 1)
                    act.wait_ge(summed, (c + 1) * 2)
                    if not (first and u < 2):
                        act.wait_ge(stored[b], (i * (U // 2) + u // 2) * 16)
                    nc.scalar.activation(rows[b][:, :, 0:F], num[:, :, :].rearrange("p f t -> p t f"), ACT.Copy).then_inc(rows_ready, 1)
                    nc.scalar.activation(rows[b][:, :, F:F + H], den[:, :, 1:T + 1].rearrange("p h t -> p t h"), ACT.Copy).then_inc(rows_ready, 1)
                    nc.scalar.activation(rows[b][:, :, F + H:ROW], mx[:, :, 1:T + 1].rearrange("p h t -> p t h"), ACT.Copy).then_inc(rows_ready, 1)

            act.wait_ge(inited, 8)
            act.wait_ge(src_in, 32)
            for u in range(U):
                index(u, u)
            for b in range(2):
                spread(b, b)
            body(0, first=True)
            with act.Fori(1, NI - 1) as i:
                body(i)
            body(NI - 1, last=True)

        @block.vector
        def _(dve):
            flat = lambda x: x.rearrange("p f t -> p (f t)")
            STEP = 19

            def edge_inputs(i, u):
                i, u = i + u // U, u % U
                c, b = i * U + u, u % 2
                kp = R["keep"][:, bass.ds(c * T, T)].unsqueeze(1).to_broadcast([P, F, T])
                dve.wait_ge(rs_in[b], (i * (U // 2) + u // 2) * 16 + 16)
                nc.vector.scalar_tensor_tensor(rnew[:, :, :], kp, 1.0, rs[b][:, :, :].rearrange("p k f -> p f k"),
                                               ALU.subtract, ALU.mult).then_inc(rnew_ready, 1)
                dve.wait_ge(rnew_ready, c + 1)
                wait(dve, held, c)
                nc.vector.scalar_tensor_tensor(rnew[:, :, 0], rneg[:, :, T - 1], R["keep"][:, bass.ds(c * T, 1)], rnew[:, :, 0],
                                               ALU.mult, ALU.add).then_inc(carried, 1)
                dve.wait_ge(carried, c + 1)
                dve.wait_ge(keepf_ready, c + 1)
                nc.vector.tensor_tensor_scan(flat(rneg[:, :, :]), flat(keepf[b][:, :, :]), flat(rnew[:, :, :]), 0.0, ALU.mult, ALU.add)\
                    .then_inc(held, 1)
                dve.wait_ge(held, c + 1)
                dve.wait_ge(gathered[u], i * 16 * T + 16 * T)
                nc.vector.tensor_tensor(z[b][:, :, :], se[u][:, :, :].rearrange("p k f -> p f k"), rneg[:, :, :], ALU.subtract)\
                    .then_inc(z_ready, 1)

            def body(i, last=False):
                for u in range(U):
                    c, b = i * U + u, u % 2
                    do = Order(dve, chain, c * STEP)
                    if not (last and u + 1 >= U):
                        edge_inputs(i, u + 1)
                    kp = R["keep"][:, bass.ds(c * T, T)]
                    dve.wait_ge(q_ready, c + 1)
                    nc.vector.reciprocal(t1[:, :, :], t1[:, :, :]).then_inc(rec_ready, 1)
                    do(nc.vector.tensor_scalar(kneg[:, :], kp, -1.0, BIG, ALU.add, ALU.mult))
                    dve.wait_ge(ratio_ready, c + 1)
                    do(nc.vector.tensor_tensor(t2[:, :, :], z[b][:, :, :], t2[:, :, :], ALU.mult))
                    do(nc.vector.tensor_tensor(t2[:, :, :], t2[:, :, :], R["aw"][:, :].unsqueeze(2).to_broadcast([P, F, T]), ALU.mult))
                    do(nc.vector.tensor_reduce(lg[:, :, :], t2[:, :, :].rearrange("p (h d) t -> p h t d", h=H), AX, ALU.add))
                    do(nc.vector.tensor_scalar(lg[:, :, :], lg[:, :, :], R["ab"][:, :], None, ALU.add))
                    wait(dve, rows_ready, c * 3)
                    for h in range(H):
                        do(nc.vector.tensor_tensor_scan(mx[:, h, 1:T + 1], kneg[:, :], lg[:, h, :], mx[:, h, 0:1], ALU.add, ALU.max))
                    do(nc.vector.tensor_tensor(exin[:, 0, :, :], mx[:, :, 0:T], mx[:, :, 1:T + 1], ALU.subtract))
                    do(nc.vector.tensor_scalar(exin[:, 0, :, :], exin[:, 0, :, :], 0.0, None, ALU.min))
                    nc.vector.tensor_tensor(exin[:, 1, :, :], lg[:, :, :], mx[:, :, 1:T + 1], ALU.subtract).then_inc(exin_ready, 1)
                    do(nc.vector.tensor_copy(mx[:, :, 0], mx[:, :, T]))
                    dve.wait_ge(ex_ready, c + 1)
                    nc.vector.tensor_tensor(dec[:, :, :], ex[:, 0, :, :], kp.unsqueeze(1).to_broadcast([P, H, T]), ALU.mult).then_inc(dec_ready, 1)
                    nc.vector.tensor_tensor(wse[:, :, :].rearrange("p (h d) t -> p h d t", h=H),
                                            se[u][:, :, :].rearrange("p k (h d) -> p h d k", h=H),
                                            ex[:, 1, :, :].unsqueeze(2).to_broadcast([P, H, HD, T]), ALU.mult).then_inc(se_used, 1)
                    dve.wait_ge(dec_ready, c + 1)
                    for h in range(H):
                        do(nc.vector.tensor_tensor_scan(den[:, h, 1:T + 1], dec[:, h, :], ex[:, 1, h, :], den[:, h, 0:1], ALU.mult, ALU.add))
                    do(nc.vector.tensor_copy(den[:, :, 0], den[:, :, T]))
                    do(nc.vector.tensor_tensor(tmp[:, :].rearrange("p (h d) -> p h d", h=H), num[:, :, T - 1].rearrange("p (h d) -> p h d", h=H),
                                               dec[:, :, 0:1].to_broadcast([P, H, HD]), ALU.mult))
                    dve.wait_ge(se_used, c + 1)
                    do(nc.vector.tensor_tensor(wse[:, :, 0], wse[:, :, 0], tmp[:, :], ALU.add))
                    dve.wait_ge(decf_ready, c + 1)
                    nc.vector.tensor_tensor_scan(flat(num[:, :, :]), flat(decf[:, :, :]), flat(wse[:, :, :]), 0.0, ALU.mult, ALU.add)\
                        .then_inc(summed, 1)
                    dve.wait_ge(summed, c * 2 + 1)
                    dve.sem_inc(summed, 1)
                    assert do.n == STEP, do.n

            nc.vector.memset(srci[96:P, LAST * T:RUN], 0).then_inc(padded, 1)
            for tile, value in ((keepf[0], 0.0), (keepf[1], 0.0), (decf, 0.0), (rneg, 0.0), (num, 0.0), (mx, -BIG), (den, 0.0)):
                nc.vector.memset(tile[:, :, :], value).then_inc(inited, 1)
            nc.vector.memset(halfc[:, :], 0.5).then_inc(inited, 1)
            dve.wait_ge(inited, 8)
            edge_inputs(0, 0)
            body(0)
            with dve.Fori(1, NI - 1) as i:
                body(i)
            body(NI - 1, last=True)
            nc.vector.tensor_copy(R["state"][:, 0:F], num[:, :, T - 1]).then_inc(inited, 1)
            nc.vector.tensor_copy(R["state"][:, F:F + H], den[:, :, T]).then_inc(inited, 1)
            nc.vector.tensor_copy(R["state"][:, F + H:ROW], mx[:, :, T]).then_inc(inited, 1)


def finish(nc, R, A, D, out, ABW=F + H):
    with ExitStack() as ctx:
        def sb(name, shape, dt=f32):
            return ctx.enter_context(nc.sbuf_tensor(name, shape, dt))

        def ps(name, shape):
            return ctx.enter_context(nc.psum_tensor(name, shape, f32))

        def sem(name):
            return ctx.enter_context(nc.semaphore(name))

        drop = sb("drop", [P, H])
        drop_t = sb("drop_t", [H, P])
        mx_t = sb("mx_t", [H, P + 1])
        mio = sb("mio", [P, 2, H])
        e = sb("e", [P, 2, H])
        add = sb("add", [P, ABW])
        mul = sb("mul", [P, ABW])
        mul_t = sb("mul_t", [ABW, P])
        cin_t = sb("fcin_t", [ABW, P + 1])
        cin = sb("cin", [P, ABW])
        got = sb("fgot", [P, ROW])
        mt = sb("mt", [P, H])
        ends = [sb(f"fends{b}", [NP, JB], i32) for b in range(2)]
        q = [sb(f"q{b}", [NP, JB, ROW]) for b in range(2)]
        inv = sb("inv", [NP, JB, H])
        res = [sb(f"res{b}", [NP, JB, F]) for b in range(2)]
        a_ps, b_ps = ps("a_ps", [P, 512]), ps("b_ps", [P, 512])

        chain = sem("chain")
        pe_do = [sem(f"pe_do{k}") for k in range(4)]
        pe_did = [sem(f"pe_did{k}") for k in range(4)]
        act_do = [sem(f"act_do{k}") for k in range(2)]
        act_did = [sem(f"act_did{k}") for k in range(2)]
        got_in = sem("got_in")
        mended = sem("mended")
        mended_out = sem("mended_out")
        staged = sem("staged")
        turn = sem("turn")
        gathered = [sem(f"fgathered{b}") for b in range(2)]
        res_ready = sem("res_ready")
        out_done = [sem(f"out_done{b}") for b in range(2)]
        block = ctx.enter_context(nc.Block())
        out_v = out.rearrange("(p j) f -> p j f", p=NP)

        @block.sync
        def _(sp):
            with sp.Fori(0, NS // 2) as i:
                for b in range(2):
                    sp.wait_ge(res_ready, i * 2 + b + 1)
                    sp.dma_start(out_v[:, bass.ds((i * 2 + b) * JB, JB), :], res[b][:, :, :]).then_inc(out_done[b], 16)
            for b in range(2):
                sp.wait_ge(out_done[b], 16 * NS // 2)

        @block.gpsimd
        def _(pool):
            at = lambda ap: bass.IndirectOffsetOnAxis(ap=ap, axis=0)
            pool.indirect_dma_start(out=got[:, :], out_offset=None, in_=D["states"], in_offset=at(R["mend"][:, :])).then_inc(got_in, 16)
            pool.wait_ge(mended, 1)
            pool.indirect_dma_start(out=D["states"], out_offset=at(R["mend"][:, :]), in_=got[:, :], in_offset=None).then_inc(mended_out, 16)
            pool.wait_ge(mended_out, 16)
            with pool.Fori(0, NS // 2) as i:
                for b in range(2):
                    pool.wait_ge(staged, i * 2 + b + 1)
                    pool.sem_inc(turn, 1)
                    for m in range(JB):
                        pool.indirect_dma_start(out=q[b][:, m, :], out_offset=None, in_=D["states"], in_offset=at(ends[b][:, m:m + 1]))\
                            .then_inc(gathered[b], 16)

        @block.tensor
        def _(pe):
            ident = R["ident"]
            pe.wait_ge(pe_do[0], 1)
            nc.tensor.transpose(a_ps[0:H, 0:P], R["state"][:, F + H:ROW], ident[:, :])
            nc.tensor.transpose(b_ps[0:H, 0:P], drop[:, :], ident[:, :]).then_inc(pe_did[0], 1)
            pe.wait_ge(pe_do[1], 1)
            nc.tensor.transpose(a_ps[:, 0:H], mx_t[:, 0:P], ident[0:H, 0:H])
            nc.tensor.transpose(b_ps[:, 0:H], mx_t[:, 1:P + 1], ident[0:H, 0:H]).then_inc(pe_did[1], 1)
            pe.wait_ge(pe_do[2], 1)
            nc.tensor.transpose(a_ps[0:ABW, 0:P], add[:, :], ident[:, :])
            nc.tensor.transpose(b_ps[0:ABW, 0:P], mul[:, :], ident[:, :]).then_inc(pe_did[2], 1)
            pe.wait_ge(pe_do[3], 1)
            nc.tensor.transpose(a_ps[:, 0:ABW], cin_t[:, 0:P], ident[0:ABW, 0:ABW]).then_inc(pe_did[3], 1)

        @block.scalar
        def _(act):
            for k in range(2):
                act.wait_ge(act_do[k], 1)
                nc.scalar.activation(e[:, :, :], e[:, :, :], ACT.Exp).then_inc(act_did[k], 1)

        @block.vector
        def _(dve):
            do = Order(dve, chain)

            def heads_wide(x):
                return x.unsqueeze(2).to_broadcast([P, H, HD])

            def by_head(x):
                return x.rearrange("p (h d) -> p h d", h=H)

            do(nc.vector.memset(mx_t[:, 0:1], -BIG))
            do(nc.vector.memset(cin_t[:, 0:1], 0.0))
            nc.vector.tensor_scalar(drop[:, :], R["whole"][:, :].to_broadcast([P, H]), -1.0, BIG, ALU.add, ALU.mult).then_inc(pe_do[0], 1)
            dve.wait_ge(pe_did[0], 1)
            do(nc.vector.tensor_copy(drop_t[:, :], b_ps[0:H, 0:P]))
            nc.vector.tensor_tensor_scan(mx_t[:, 1:P + 1], drop_t[:, :], a_ps[0:H, 0:P], -BIG, ALU.add, ALU.max).then_inc(pe_do[1], 1)
            dve.wait_ge(pe_did[1], 1)
            do(nc.vector.tensor_copy(mio[:, 0, :], a_ps[:, 0:H]))
            do(nc.vector.tensor_copy(mio[:, 1, :], b_ps[:, 0:H]))
            do(nc.vector.tensor_tensor(e[:, 0, :], mio[:, 0, :], mio[:, 1, :], ALU.subtract))
            do(nc.vector.tensor_scalar(e[:, 0, :], e[:, 0, :], 0.0, None, ALU.min))
            nc.vector.tensor_tensor(e[:, 1, :], R["state"][:, F + H:ROW], mio[:, 1, :], ALU.subtract).then_inc(act_do[0], 1)
            dve.wait_ge(act_did[0], 1)
            do(nc.vector.tensor_scalar(e[:, 0, :], e[:, 0, :], R["whole"][:, :], None, ALU.mult))
            do(nc.vector.tensor_scalar(e[:, 1, :], e[:, 1, :], R["onward"][:, :], None, ALU.mult))
            do(nc.vector.tensor_copy(by_head(mul[:, 0:F]), heads_wide(e[:, 0, :])))
            do(nc.vector.tensor_copy(mul[:, F:ABW], e[:, 0, :]))
            do(nc.vector.tensor_tensor(by_head(add[:, 0:F]), by_head(R["state"][:, 0:F]), heads_wide(e[:, 1, :]), ALU.mult))
            nc.vector.tensor_tensor(add[:, F:ABW], R["state"][:, F:F + H], e[:, 1, :], ALU.mult).then_inc(pe_do[2], 1)
            dve.wait_ge(pe_did[2], 1)
            do(nc.vector.tensor_copy(mul_t[:, :], b_ps[0:ABW, 0:P]))
            nc.vector.tensor_tensor_scan(cin_t[:, 1:P + 1], mul_t[:, :], a_ps[0:ABW, 0:P], 0.0, ALU.mult, ALU.add).then_inc(pe_do[3], 1)
            dve.wait_ge(pe_did[3], 1)
            do(nc.vector.tensor_copy(cin[:, :], a_ps[:, 0:ABW]))
            dve.wait_ge(got_in, 16)
            do(nc.vector.tensor_tensor(mt[:, :], got[:, F + H:ROW], mio[:, 0, :], ALU.max))
            do(nc.vector.tensor_tensor(e[:, 0, :], got[:, F + H:ROW], mt[:, :], ALU.subtract))
            nc.vector.tensor_tensor(e[:, 1, :], mio[:, 0, :], mt[:, :], ALU.subtract).then_inc(act_do[1], 1)
            dve.wait_ge(act_did[1], 1)
            do(nc.vector.tensor_scalar(e[:, 1, :], e[:, 1, :], R["cont"][:, :], None, ALU.mult))
            do(nc.vector.tensor_tensor(by_head(got[:, 0:F]), by_head(got[:, 0:F]), heads_wide(e[:, 0, :]), ALU.mult))
            do(nc.vector.tensor_tensor(got[:, F:ABW], got[:, F:ABW], e[:, 0, :], ALU.mult))
            do(nc.vector.tensor_tensor(by_head(cin[:, 0:F]), by_head(cin[:, 0:F]), heads_wide(e[:, 1, :]), ALU.mult))
            do(nc.vector.tensor_tensor(cin[:, F:ABW], cin[:, F:ABW], e[:, 1, :], ALU.mult))
            nc.vector.tensor_tensor(got[:, 0:ABW], got[:, 0:ABW], cin[:, :], ALU.add).then_inc(mended, 1)

            def stage(k, b):
                nc.vector.tensor_copy(ends[b][:, :], R["end"][:, bass.ds(k * JB, JB)]).then_inc(staged, 1)

            def step(i, b, first=False, more=True):
                k = i * 2 + b
                do = Order(dve, chain, base + k * 3)
                cols = bass.ds(k * JB, JB)
                dve.wait_ge(gathered[b], i * 16 * JB + 16 * JB)
                do(nc.vector.reciprocal(inv[:, :, :], q[b][:, :, F:F + H]))
                do(nc.vector.tensor_tensor(inv[:, :, :], inv[:, :, :], R["pres"][:, cols].unsqueeze(2).to_broadcast([NP, JB, H]), ALU.mult))
                if not first:
                    dve.wait_ge(out_done[b], i * 16)
                do(nc.vector.tensor_tensor(res[b][:, :, :].rearrange("n j (h d) -> n j h d", h=H),
                                           q[b][:, :, 0:F].rearrange("n j (h d) -> n j h d", h=H),
                                           inv[:, :, :].unsqueeze(3).to_broadcast([NP, JB, H, HD]), ALU.mult))
                nc.vector.tensor_tensor(res[b][:, :, :], res[b][:, :, :], R["base"][:, cols, :], ALU.add).then_inc(res_ready, 1)
                if more:
                    stage(k + 2, b)

            base = do.n
            stage(0, 0)
            stage(1, 1)
            for b in range(2):
                step(0, b, first=True)
            with dve.Fori(1, NS // 2 - 1) as i:
                for b in range(2):
                    step(i, b)
            for b in range(2):
                step(NS // 2 - 1, b, more=False)


def gnn_program(nc, A, out):
    D = {
        "samples": nc.dram_tensor("samples", [SB], i32).ap(),
        "ends": nc.dram_tensor("ends", [N, 1], i32).ap(),
        "sums": nc.dram_tensor("sums", [P * RUN, F], f32).ap(),
        "states": nc.dram_tensor("states", [P * RUN, ROW], f32).ap(),
        "s_proj": nc.dram_tensor("s_proj", [N, F], f32).ap(),
        "r_proj": nc.dram_tensor("r_proj", [N, F], f32).ap(),
    }
    with ExitStack() as ctx:
        shapes = {
            "base": ([NP, NJ, F], f32), "keep": ([P, RUN], f32), "ident": ([P, P], f32),
            "w1g1": ([P, 2 * F], f32), "w2g2": ([P, 2 * F], f32), "b1g1": ([P, 1], f32),
            "ones": ([P, P], bf16), "b2g2": ([P, TG // 2, 2 * F], bf16),
            "wsr": ([F, 2 * F], f32), "bsr": ([P, 2 * F], f32), "aw": ([P, F], f32), "ab": ([P, 1], f32),
            "pres": ([NP, NJ], f32), "end": ([NP, NJ], f32), "start": ([NP, NJ], f32),
            "first": ([P, 1], i32), "mend": ([P, 1], i32), "cont": ([P, 1], f32), "onward": ([P, 1], f32),
            "whole": ([P, 1], f32), "state": ([P, ROW], f32),
        }
        R = {k: ctx.enter_context(nc.sbuf_tensor(f"r_{k}", s, d)) for k, (s, d) in shapes.items()}
        setup(nc, R, A, D)
        edge_mlp(nc, R, A, D)
        update_nodes(nc, R, A, D)
        attention(nc, R, A, D)
        finish(nc, R, A, D, out)


_INS = ["x", "src", "dst", "edge_attr_64", "L0_gnn_W1", "L0_gnn_b1", "L0_gnn_W2", "L0_gnn_b2", "L0_gnn_G1", "L0_gnn_g1",
        "L0_gnn_G2", "L0_gnn_g2", "L1_gnn_Ws", "L1_gnn_bs", "L1_gnn_Wr", "L1_gnn_br", "L1_gnn_aw", "L1_gnn_ab"]


def kernel(**inputs):
    import numpy as np
    import concourse.bacc as bacc
    from concourse.bass_utils import run_bass_kernel_spmd

    nc = bacc.Bacc("TRN2", target_bir_lowering=False, num_devices=1)
    arrays, args = {}, {}
    for name in _INS:
        a = np.ascontiguousarray(inputs[name])
        arrays[f"in_{name}"] = a
        args[name] = nc.dram_tensor(f"in_{name}", a.shape, mybir.dt.from_np(a.dtype), kind="ExternalInput").ap()
    out = nc.dram_tensor("out_0", (N, F), f32, kind="ExternalOutput").ap()
    gnn_program(nc, args, out)
    return run_bass_kernel_spmd(nc, [arrays], core_ids=[0]).results[0]["out_0"]
```

```python
import concourse.bass as bass
from concourse import mybir
from contextlib import ExitStack

f32 = mybir.dt.float32
bf16 = mybir.dt.bfloat16
i32 = mybir.dt.int32
ALU = mybir.AluOpType
ACT = mybir.ActivationFunctionType
AX = mybir.AxisListType.X

P = 128
N = 12500
F = 64
E = 412500
H = 4
HD = F // H
T = 30
CH = -(-E // (T * P))
RUN = CH * T
LAST = (E - (P - 1) * RUN) // T
G = 5
TG = T // G
PAIRS = TG // 2
GC = PAIRS * P
NG = CH * G
QF = T * F
NP, NJ = 125, 100
JB = 10
NS = NJ // JB
SB, SL = 750, 550
NC = CH - 2
ROW = F + 2 * H
BIG = 1e30
EPS = 1e-5


def wait(eng, sem, value):
    if isinstance(value, int) and value <= 0:
        return
    eng.wait_ge(sem, value)


class Order:

    def __init__(self, eng, sem, base=0):
        self.eng, self.sem, self.base, self.n = eng, sem, base, 0

    def __call__(self, ins):
        self.n += 1
        ins.then_inc(self.sem, 1)
        self.eng.wait_ge(self.sem, self.base + self.n)


def last_run_split(view, run_rows):
    body = view[0:(P - 1) * RUN]
    tail = view[(P - 1) * RUN:E]
    if run_rows:
        return (body.rearrange("(p c k) f -> p c (k f)", p=P - 1, c=CH),
                tail.rearrange("(c k) f -> c (k f)", k=T))
    return body.rearrange("(p c k) -> p c k", p=P - 1, c=CH), tail.rearrange("(c k) -> c k", k=T)


def load_chunk(sp, buf, split, chunk, tail_chunk, sem):
    body, tail = split
    sp.dma_start(buf[0:112, :].unsqueeze(1), body[0:112, bass.ds(chunk, 1), :]).then_inc(sem, 16)
    sp.dma_start(buf[112:127, :].unsqueeze(1), body[112:127, bass.ds(chunk, 1), :]).then_inc(sem, 16)
    sp.dma_start(buf[127:128, :], tail[bass.ds(tail_chunk, 1), :]).then_inc(sem, 16)


def setup(nc, R, A, D):
    with ExitStack() as ctx:
        def sb(name, shape, dt=f32):
            return ctx.enter_context(nc.sbuf_tensor(name, shape, dt))

        def sem(name):
            return ctx.enter_context(nc.semaphore(name))

        dsti = sb("dsti", [P, RUN], i32)
        dstf = sb("dstf", [P, RUN])
        near = sb("near", [P, 2], i32)
        nearf = sb("nearf", [P, 2])
        nid = sb("nid", [P, NC], i32)
        smp = sb("smp", [NP, SB // NP], i32)
        pid = sb("pid", [P, 1], i32)

        ld_dst = sem("ld_dst")
        ld_w = sem("ld_w")
        ld_smp = sem("ld_smp")
        smp_out = sem("smp_out")
        smp_in = sem("smp_in")
        zeroed = sem("zeroed")
        pool_done = sem("pool_done")
        iotas = sem("iotas")
        chain = sem("chain")
        block = ctx.enter_context(nc.Block())
        samp_d = D["samples"]

        @block.sync
        def _(sp):
            sp.dma_start(smp[:, :], A["dst"].rearrange("(p a k) -> p a k", p=NP, k=SL)[:, :, 0],
                         allow_slow_non_contiguous=True).then_inc(ld_smp, 16)
            sp.wait_ge(ld_smp, 16)
            sp.dma_start(samp_d.rearrange("(p a) -> p a", p=NP), smp[:, :]).then_inc(smp_out, 16)
            sp.wait_ge(zeroed, 1)
            body, tail = A["dst"][0:(P - 1) * RUN], A["dst"][(P - 1) * RUN:E]
            sp.dma_start(dsti[0:P - 1, :], body.rearrange("(p k) -> p k", k=RUN)).then_inc(ld_dst, 16)
            sp.dma_start(dsti[P - 1:P, 0:LAST * T], tail.rearrange("(a k) -> a k", a=1)).then_inc(ld_dst, 16)
            sp.dma_start(near[1:P, 0:1], body.rearrange("(p k) -> p k", k=RUN)[:, RUN - 1:RUN],
                         allow_slow_non_contiguous=True).then_inc(ld_dst, 16)
            sp.dma_start(near[0:P - 2, 1:2], body[RUN:].rearrange("(p k) -> p k", k=RUN)[:, 0:1],
                         allow_slow_non_contiguous=True).then_inc(ld_dst, 16)
            sp.dma_start(near[P - 2:P - 1, 1:2], tail[0:1].rearrange("(a k) -> a k", a=1)).then_inc(ld_dst, 16)
            sp.wait_ge(smp_out, 16)
            sp.dma_start(R["smb"][:, :], samp_d.rearrange("(a k) -> a k", a=1).to_broadcast([P, SB])).then_inc(smp_in, 16)
            sp.wait_ge(smp_in, 16)

        @block.scalar
        def _(act):
            act.wait_ge(zeroed, 2)
            for k, (wa, wb) in enumerate((("L0_gnn_W1", "L0_gnn_G1"),) * 2):
                rows = slice(F * k, F * k + F)
                act.dma_start(R["w1g1"][rows, 0:F], A[wa]).then_inc(ld_w, 16)
                act.dma_start(R["w1g1"][rows, F:2 * F], A[wb]).then_inc(ld_w, 16)
            act.dma_start(R["w2g2"][0:F, 0:F], A["L0_gnn_W2"]).then_inc(ld_w, 16)
            act.dma_start(R["w2g2"][F:2 * F, F:2 * F], A["L0_gnn_G2"]).then_inc(ld_w, 16)
            act.dma_start(R["b1g1"][0:F, :], A["L0_gnn_b1"].rearrange("(p a) -> p a", a=1), allow_slow_non_contiguous=True).then_inc(ld_w, 16)
            act.dma_start(R["b1g1"][F:2 * F, :], A["L0_gnn_g1"].rearrange("(p a) -> p a", a=1), allow_slow_non_contiguous=True).then_inc(ld_w, 16)

            def row(ap):
                return ap.rearrange("(a n) -> a n", a=1)

            act.dma_start(R["b2g2"][:, 0:F], row(A["L0_gnn_b2"]).to_broadcast([P, F])).then_inc(ld_w, 16)
            act.dma_start(R["b2g2"][:, F:2 * F], row(A["L0_gnn_g2"]).to_broadcast([P, F])).then_inc(ld_w, 16)
            act.dma_start(R["wsr"][:, 0:F], A["L1_gnn_Ws"].rearrange("f h d -> f (h d)")).then_inc(ld_w, 16)
            act.dma_start(R["wsr"][:, F:2 * F], A["L1_gnn_Wr"].rearrange("f h d -> f (h d)")).then_inc(ld_w, 16)
            act.dma_start(R["bsr"][:, 0:F], row(A["L1_gnn_bs"].rearrange("h d -> (h d)")).to_broadcast([P, F])).then_inc(ld_w, 16)
            act.dma_start(R["bsr"][:, F:2 * F], row(A["L1_gnn_br"].rearrange("h d -> (h d)")).to_broadcast([P, F])).then_inc(ld_w, 16)
            for h in range(H):
                act.dma_start(R["aw"][:, h * HD:(h + 1) * HD], row(A["L1_gnn_aw"]).to_broadcast([P, HD])).then_inc(ld_w, 16)
            act.dma_start(R["ab"][:, :], row(A["L1_gnn_ab"]).to_broadcast([P, 1])).then_inc(ld_w, 16)
            act.wait_ge(ld_w, 16 * 19)

        @block.gpsimd
        def _(pool):
            nc.gpsimd.memset(R["ident"][:, :], 0.0).then_inc(pool_done, 1)
            nc.gpsimd.iota(nid[:, :], pattern=[[1, NC]], base=-1, channel_multiplier=NJ).then_inc(iotas, 1)
            nc.gpsimd.iota(pid[:, :], pattern=[[1, 1]], base=0, channel_multiplier=1).then_inc(iotas, 1)
            pool.wait_ge(pool_done, 1)
            nc.gpsimd.affine_select(out=R["ident"][:, :], in_=R["ident"][:, :], compare_op=ALU.not_equal, fill=1.0,
                                    base=0, pattern=[[-1, P]], channel_multiplier=1).then_inc(pool_done, 1)
            pool.wait_ge(pool_done, 2)

        @block.vector
        def _(dve):
            do = Order(dve, chain)
            do(nc.vector.memset(near[:, :], -1))
            nc.vector.memset(dsti[96:P, LAST * T:RUN], -1).then_inc(zeroed, 1)
            nc.vector.memset(R["w2g2"][:, :], 0.0).then_inc(zeroed, 1)
            dve.wait_ge(iotas, 2)
            do(nc.vector.tensor_copy(R["nid"][:, :], nid[:, :]))
            do(nc.vector.tensor_copy(R["pid"][:, :], pid[:, :]))
            dve.wait_ge(ld_dst, 80)
            do(nc.vector.tensor_copy(dstf[:, :], dsti[:, :]))
            do(nc.vector.tensor_copy(nearf[:, :], near[:, :]))
            do(nc.vector.memset(R["keep"][:, 0:1], 0.0))
            do(nc.vector.tensor_tensor(R["keep"][:, 1:RUN], dstf[:, 1:RUN], dstf[:, 0:RUN - 1], ALU.is_equal))
            do(nc.vector.tensor_copy(R["first"][:, :], dsti[:, 0:1]))
            do(nc.vector.tensor_copy(R["nid"][:, NC - 1:NC], dsti[:, 0:1]))
            do(nc.vector.tensor_tensor(R["cont"][:, :], dstf[:, 0:1], nearf[:, 0:1], ALU.is_equal))
            do(nc.vector.tensor_tensor(R["onward"][:, :], dstf[:, RUN - 1:RUN], nearf[:, 1:2], ALU.is_equal))
            do(nc.vector.tensor_tensor(R["whole"][:, :], dstf[:, 0:1], dstf[:, RUN - 1:RUN], ALU.is_equal))
            do(nc.vector.tensor_tensor(R["whole"][:, :], R["whole"][:, :], R["onward"][:, :], ALU.mult))


def edge_mlp(nc, R, A, D):
    with ExitStack() as ctx:
        def sb(name, shape, dt=f32):
            return ctx.enter_context(nc.sbuf_tensor(name, shape, dt))

        def sem(name):
            return ctx.enter_context(nc.semaphore(name))

        edges = [sb(f"edges{b}", [P, QF]) for b in range(2)]
        edges_t = [sb(f"edges_t{b}", [P, GC]) for b in range(2)]
        hidden = [sb(f"hidden{b}", [P, 2, GC]) for b in range(2)]
        value = [sb(f"value{b}", [P, TG, F]) for b in range(2)]
        gate = [sb(f"gate{b}", [P, TG, F]) for b in range(2)]
        msg = [sb(f"msg{b}", [P, F, T]) for b in range(2)]
        keepf = [sb(f"keepf{b}", [P, F, T]) for b in range(2)]
        sums = [sb(f"sums{b}", [P, F, T]) for b in range(2)]
        rows = [sb(f"rows{b}", [P, T, F]) for b in range(2)]
        junk1 = sb("junk1", [P, SB], bf16)
        junk2 = sb("junk2", [P, SL], bf16)
        blocks_upto = sb("blocks_upto", [P, NC])
        upto = sb("upto", [P, NC])
        block_id = [sb(f"block_id{b}", [P, 1], i32) for b in range(2)]
        block_of = [sb(f"block_of{b}", [P, SL], i32) for b in range(2)]
        fx = sb("fx", [P, 3])
        pad = sb("pad", [NP, NJ])
        tr_ps = [ctx.enter_context(nc.psum_tensor(f"tr_ps{b}", [P, 512], f32)) for b in range(2)]
        h_ps = ctx.enter_context(nc.psum_tensor("h_ps", [P, 2, 512], f32))
        o_ps = [ctx.enter_context(nc.psum_tensor(f"o_ps{b}", [P, 2, 512], f32)) for b in range(2)]

        loaded = [sem(f"loaded{b}") for b in range(2)]
        transposed = sem("transposed")
        edges_t_ready = sem("edges_t_ready")
        h_ready = sem("h_ready")
        hidden_ready = sem("hidden_ready")
        o_ready = sem("o_ready")
        biased = sem("biased")
        gated = sem("gated")
        msg_ready = sem("msg_ready")
        carried = sem("carried")
        scanned = sem("scanned")
        turn = sem("turn")
        keepf_ready = sem("keepf_ready")
        zeroed = sem("zeroed")
        rows_ready = sem("rows_ready")
        stored = [sem(f"stored{b}") for b in range(2)]
        chain = sem("chain")
        counted1 = sem("counted1")
        counted2 = sem("counted2")
        block_known = sem("block_known")
        block_in = [sem(f"block_in{b}") for b in range(2)]
        block = ctx.enter_context(nc.Block())
        split = last_run_split(A["edge_attr_64"], True)
        sums_d = D["sums"][0:P * RUN, :].rearrange("(p c k) f -> p c (k f)", p=P, c=CH)
        HALF = CH // 2
        AHEAD = 3
        PIECES = 4

        @block.sync
        def _(sp):
            def load(i, b, tail):
                load_chunk(sp, edges[b], split, i * 2 + b, tail, loaded[b])

            def store(c, b):
                sp.wait_ge(rows_ready, c + 1)
                sp.dma_start(sums_d[:, bass.ds(c, 1), :], rows[b][:, :, :].rearrange("p k f -> p (k f)").unsqueeze(1)).then_inc(stored[b], 16)

            def body(i, padded=False, first=False, last=False):
                for b in range(2):
                    if not last:
                        sp.wait_ge(transposed, (i * 2 + b + 1) * G)
                        load(i + 1, b, LAST - 1 if padded else (i + 1) * 2 + b)
                    if not (first and b == 0):
                        store(i * 2 + b - 1, 1 - b)

            load(0, 0, 0)
            load(0, 1, 1)
            body(0, first=True)
            with sp.Fori(1, LAST // 2 - 1) as i:
                body(i)
            with sp.Fori(LAST // 2 - 1, HALF - 1) as i:
                body(i, padded=True)
            body(HALF - 1, last=True)
            store(CH - 1, 1)
            for b in range(2):
                sp.wait_ge(stored[b], 16 * HALF)

        @block.tensor
        def _(pe):
            def transpose(i, s):
                i, s = i + s // (2 * G), s % (2 * G)
                b, g = s // G, s % G
                if g == 0:
                    pe.wait_ge(loaded[b], i * 48 + 48)
                for j in range(PAIRS):
                    at = (g * TG + 2 * j) * F
                    last = nc.tensor.transpose(tr_ps[s % 2][:, j * P:(j + 1) * P], edges[b][:, at:at + 2 * F], R["ident"][:, :])
                last.then_inc(transposed, 1)

            def layer1(i, s):
                n = i * 2 * G + s
                pe.wait_ge(edges_t_ready, n + 1)
                wait(pe, hidden_ready, n)
                for a in range(2):
                    half = slice(F * a, F * a + F)
                    last = nc.tensor.matmul(h_ps[:, a, 0:GC], R["w1g1"][half, :], edges_t[s % 2][half, :], start=True, stop=True)
                last.then_inc(h_ready, 1)

            def layer2(i, s):
                n = i * 2 * G + s
                pe.wait_ge(hidden_ready, n + 1)
                wait(pe, gated, 2 * (n - 1))
                out, hid = o_ps[s % 2], hidden[s % 2]
                for k in range(2):
                    for m in range(PAIRS):
                        tile = k * PAIRS + m
                        at = (tile // 2) * P
                        last = nc.tensor.matmul(out[:, k, m * P:(m + 1) * P], hid[:, tile % 2, at:at + P], R["w2g2"][:, :],
                                                start=True, stop=True)
                last.then_inc(o_ready, 1)

            def body(i, last=False):
                for s in range(2 * G):
                    if not (last and s + 1 >= 2 * G):
                        layer1(i + (s + 1) // (2 * G), (s + 1) % (2 * G))
                    if not (last and s + AHEAD >= 2 * G):
                        transpose(i, s + AHEAD)
                    layer2(i, s)

            transpose(0, 0)
            transpose(0, 1)
            layer1(0, 0)
            transpose(0, 2)
            body(0)
            with pe.Fori(1, HALF - 1) as i:
                body(i)
            body(HALF - 1, last=True)

        @block.scalar
        def _(act):
            def hid(i, s):
                n = i * 2 * G + s
                act.wait_ge(h_ready, n + 1)
                nc.scalar.activation(hidden[s % 2][:, :, :], h_ps[:, :, 0:GC], ACT.Silu, bias=R["b1g1"][:, :]).then_inc(hidden_ready, 1)

            def outs(i, s):
                n = i * 2 * G + s
                act.wait_ge(biased, n + 1)
                wait(act, msg_ready, n - 1)
                o = o_ps[s % 2][:, :, 0:GC].rearrange("p k (m c) -> p k m c", c=P)
                v, g = (x[s % 2][:, :, :].rearrange("p (k m) f -> p k m f", k=2) for x in (value, gate))
                nc.scalar.activation(v, o[:, :, :, 0:F], ACT.Silu).then_inc(gated, 1)
                nc.scalar.activation(g, o[:, :, :, F:2 * F], ACT.Tanh, scale=0.5).then_inc(gated, 1)

            def body(i, first=False, last=False):
                for s in range(2 * G):
                    if not (last and s + 1 >= 2 * G):
                        hid(i + (s + 1) // (2 * G), (s + 1) % (2 * G))
                    if not (first and s == 0):
                        outs(i + (s - 1) // (2 * G), (s - 1) % (2 * G))

            hid(0, 0)
            body(0, first=True)
            with act.Fori(1, HALF - 1) as i:
                body(i)
            body(HALF - 1, last=True)
            outs(HALF - 1, 2 * G - 1)

        @block.vector
        def _(dve):
            def copy_t(i, s):
                n = i * 2 * G + s
                dve.wait_ge(transposed, n + 1)
                nc.vector.tensor_copy(edges_t[s % 2][:, :], tr_ps[s % 2][:, 0:GC]).then_inc(edges_t_ready, 1)

            def add_bias(i, s):
                dve.wait_ge(o_ready, i * 2 * G + s + 1)
                o = o_ps[s % 2][:, :, 0:GC].rearrange("p k (m c) -> p k m c", c=P)
                bias = R["b2g2"][:, :].unsqueeze(1).unsqueeze(1).to_broadcast([P, 2, PAIRS, P])
                nc.vector.tensor_tensor(o, o, bias, ALU.add).then_inc(biased, 1)

            def product(i, s):
                n = i * 2 * G + s
                b, g = s // G, s % G
                dve.wait_ge(gated, 2 * (n + 1))
                if g == 0:
                    wait(dve, scanned, (i * 2 + b - 1) * PIECES)
                out = msg[b][:, :, g * TG:(g + 1) * TG].rearrange("p f t -> p t f")
                nc.vector.scalar_tensor_tensor(out, gate[s % 2][:, :, :], 1.0, value[s % 2][:, :, :], ALU.add, ALU.mult)\
                    .then_inc(msg_ready, 1)

            def carry(c, b):
                dve.wait_ge(msg_ready, (c + 1) * G)
                wait(dve, scanned, c * PIECES)
                nc.vector.scalar_tensor_tensor(msg[b][:, :, 0], sums[1 - b][:, :, T - 1], R["keep"][:, bass.ds(c * T, 1)],
                                               msg[b][:, :, 0], ALU.mult, ALU.add).then_inc(carried, 1)

            def scan(c, b, k):
                if k == 0:
                    dve.wait_ge(carried, c + 1)
                    dve.wait_ge(keepf_ready, c + 1)
                    wait(dve, rows_ready, c - 1)
                fs = slice(k * F // PIECES, (k + 1) * F // PIECES)
                flat = [x[:, fs, :].rearrange("p f t -> p (f t)") for x in (sums[b], keepf[b], msg[b])]
                nc.vector.tensor_tensor_scan(flat[0], flat[1], flat[2], 0.0, ALU.mult, ALU.add).then_inc(scanned, 1)

            def find_block(i, b):
                q = i * 2 + b
                nc.vector.tensor_scalar(junk1[:, :], R["smb"][:, :], R["nid"][:, bass.ds(q, 1)], 0.0, ALU.is_le, ALU.add,
                                        accum_out=blocks_upto[:, bass.ds(q, 1)]).then_inc(counted1, 1)
                dve.wait_ge(counted1, q + 1)
                nc.vector.tensor_scalar(block_id[b][:, :], blocks_upto[:, bass.ds(q, 1)], -1.0, 0.0, ALU.add, ALU.max).then_inc(block_known, 1)

            def find_edge(i, b):
                q = i * 2 + b
                dve.wait_ge(block_in[b], i * 16 + 16)
                wait(dve, counted2, q)
                nc.vector.tensor_scalar(junk2[:, :], block_of[b][:, :], R["nid"][:, bass.ds(q, 1)], 0.0, ALU.is_le, ALU.add,
                                        accum_out=upto[:, bass.ds(q, 1)]).then_inc(counted2, 1)

            def body(i, first=False, last=False):
                for s in range(2 * G):
                    if s % G == 2:
                        if not first:
                            find_edge(i - 1, s // G)
                        if not last:
                            find_block(i, s // G)
                    if not (last and s + AHEAD >= 2 * G):
                        copy_t(i + (s + AHEAD) // (2 * G), (s + AHEAD) % (2 * G))
                    add_bias(i, s)
                    if not (first and s == 0):
                        product(i + (s - 1) // (2 * G), (s - 1) % (2 * G))
                    b, g = s // G, s % G
                    if g > 0 and not (first and b == 0):
                        c = i * 2 + b - 1
                        if g == 1:
                            carry(c, 1 - b)
                        scan(c, 1 - b, g - 1)

            nc.vector.memset(sums[1][:, :, :], 0.0).then_inc(zeroed, 1)
            for b in range(2):
                nc.vector.memset(keepf[b][:, :, :], 0.0).then_inc(zeroed, 1)
            dve.wait_ge(zeroed, 3)
            for s in range(AHEAD):
                copy_t(0, s)
            body(0, first=True)
            with dve.Fori(1, HALF - 1) as i:
                body(i)
            body(HALF - 1, last=True)
            product(HALF - 1, 2 * G - 1)
            carry(CH - 1, 1)
            for k in range(PIECES):
                scan(CH - 1, 1, k)
            dve.wait_ge(scanned, CH * PIECES)
            nc.vector.tensor_copy(R["state"][:, 0:F], sums[1][:, :, T - 1]).then_inc(zeroed, 1)
            dve.wait_ge(counted2, NC)
            do = Order(dve, chain)
            do(nc.vector.tensor_scalar(blocks_upto[:, :], blocks_upto[:, :], -1.0, 0.0, ALU.add, ALU.max))
            do(nc.vector.scalar_tensor_tensor(upto[:, :], blocks_upto[:, :], float(SL), upto[:, :], ALU.mult, ALU.add))
            before, through = upto[0:NP, 0:NJ], upto[0:NP, 1:NJ + 1]
            do(nc.vector.tensor_tensor(R["pres"][:, :], through, before, ALU.is_gt))
            do(nc.vector.tensor_scalar(R["end"][:, :], through, -1.0, 0.0, ALU.add, ALU.max))
            do(nc.vector.tensor_scalar(fx[:, 2:3], R["pid"][:, :], float(E), None, ALU.add))
            do(nc.vector.tensor_scalar(pad[:, :], before, fx[0:NP, 2:3], None, ALU.subtract))
            do(nc.vector.tensor_tensor(pad[:, :], pad[:, :], R["pres"][:, :], ALU.mult))
            do(nc.vector.tensor_scalar(R["start"][:, :], pad[:, :], fx[0:NP, 2:3], None, ALU.add))
            do(nc.vector.tensor_scalar(fx[:, 0:1], upto[:, NC - 1:NC], -1.0, None, ALU.add))
            do(nc.vector.tensor_scalar(fx[:, 1:2], R["pid"][:, :], float(RUN), float(RUN), ALU.mult, ALU.add))
            do(nc.vector.tensor_tensor(fx[:, 1:2], fx[:, 0:1], fx[:, 1:2], ALU.is_lt))
            do(nc.vector.tensor_tensor(fx[:, 1:2], fx[:, 1:2], R["cont"][:, :], ALU.mult))
            do(nc.vector.tensor_tensor(fx[:, 0:1], fx[:, 0:1], fx[:, 2:3], ALU.subtract))
            do(nc.vector.tensor_tensor(fx[:, 0:1], fx[:, 0:1], fx[:, 1:2], ALU.mult))
            do(nc.vector.tensor_tensor(R["mend"][:, :], fx[:, 0:1], fx[:, 2:3], ALU.add))

        @block.gpsimd
        def _(pool):
            def spread_keep(c, b):
                src = R["keep"][:, bass.ds(c * T + 1, T - 1)].unsqueeze(1).to_broadcast([P, F, T - 1])
                pool.sem_inc(turn, 1)
                nc.gpsimd.tensor_copy(keepf[b][:, :, 1:T], src).then_inc(keepf_ready, 1)

            def to_rows(i, b, first=False):
                c = i * 2 + b
                if not first:
                    pool.wait_ge(stored[b], i * 16)
                pool.wait_ge(scanned, (c + 1) * PIECES)
                pool.sem_inc(turn, 1)
                nc.gpsimd.tensor_copy(rows[b][:, :, :], sums[b][:, :, :].rearrange("p f t -> p t f")).then_inc(rows_ready, 1)

            def fetch_block(q, b):
                pool.wait_ge(block_known, q + 1)
                pool.sem_inc(turn, 1)
                pool.indirect_dma_start(out=block_of[b][:, :], out_offset=None, in_=A["dst"].rearrange("(a k) -> a k", k=SL),
                                        in_offset=bass.IndirectOffsetOnAxis(ap=block_id[b][:, :], axis=0)).then_inc(block_in[b], 16)

            pool.wait_ge(zeroed, 3)
            spread_keep(0, 0)
            spread_keep(1, 1)
            for b in range(2):
                fetch_block(b, b)
                to_rows(0, b, first=True)
                spread_keep(2 + b, b)
            with pool.Fori(1, HALF - 1) as i:
                for b in range(2):
                    fetch_block(i * 2 + b, b)
                    to_rows(i, b)
                    spread_keep(i * 2 + b + 2, b)
            for b in range(2):
                to_rows(HALF - 1, b)


def update_nodes(nc, R, A, D):
    with ExitStack() as ctx:
        def sb(name, shape, dt=f32):
            return ctx.enter_context(nc.sbuf_tensor(name, shape, dt))

        def ps(name, shape):
            return ctx.enter_context(nc.psum_tensor(name, shape, f32))

        def sem(name):
            return ctx.enter_context(nc.semaphore(name))

        onw = sb("onw", [P, F])
        whl = sb("whl", [P, F])
        whl_t = sb("whl_t", [F, P])
        cin_t = sb("cin_t", [F, P + 1])
        got = sb("got", [P, F])
        half = sb("half", [NP, NJ])
        ends = [sb(f"ends{b}", [NP, JB], i32) for b in range(2)]
        starts = [sb(f"starts{b}", [NP, JB], i32) for b in range(2)]
        x = [sb(f"x_tile{b}", [NP, JB, F]) for b in range(2)]
        agg = [sb(f"agg{b}", [NP, JB, F]) for b in range(2)]
        xc = sb("xc", [NP, JB, F])
        sq = sb("sq", [NP, JB, F])
        st = sb("st", [NP, JB])
        std = sb("std", [NP, JB])
        epst = sb("epst", [NP, 1])
        hh = sb("hh", [NP, JB, F])
        hT = sb("hT", [F, JB, NP])
        sr = [sb(f"sr{b}", [NP, JB, 2 * F]) for b in range(2)]
        onw_bank, whl_bank = ps("onw_bank", [P, 512]), ps("whl_bank", [P, 512])
        onw_ps, whl_ps, back_ps = onw_bank[0:F, 0:P], whl_bank[0:F, 0:P], onw_bank[:, 0:F]
        hT_ps = ps("hT_ps", [F, 3, 512])
        pr_ps = ps("pr_ps", [NP, 3, 512])

        chain = sem("chain")
        scaled = sem("scaled")
        turned = sem("turned")
        cin_ready = sem("cin_ready")
        cin_back = sem("cin_back")
        got_in = sem("got_in")
        mended = sem("mended")
        mended_out = sem("mended_out")
        padded = sem("padded")
        src_in = sem("src_in")
        x_in = [sem(f"x_in{b}") for b in range(2)]
        base_ready = sem("base_ready")
        staged = sem("staged")
        turn = sem("turn")
        gathered = [sem(f"gathered{b}") for b in range(2)]
        var_x = sem("var_x")
        std_x = sem("std_x")
        var_h = sem("var_h")
        std_h = sem("std_h")
        h_ready = sem("h_ready")
        hT_in_ps = sem("hT_in_ps")
        hT_part = sem("hT_part")
        hT_ready = sem("hT_ready")
        pr_in_ps = sem("pr_in_ps")
        sr_ready = sem("sr_ready")
        tabled = [sem(f"tabled{b}") for b in range(2)]
        scattered = [sem(f"scattered{b}") for b in range(2)]
        block = ctx.enter_context(nc.Block())
        sums_d = D["sums"]
        x_v = A["x"].rearrange("(p j) f -> p j f", p=NP)
        s_tab = D["s_proj"].rearrange("(p j) f -> p j f", p=NP)
        r_tab = D["r_proj"].rearrange("(p j) f -> p j f", p=NP)
        HALF = NS // 2

        @block.sync
        def _(sp):
            def load_x(k, b):
                sp.dma_start(x[b][:, :, :], x_v[:, bass.ds(k * JB, JB), :]).then_inc(x_in[b], 16)

            def tables(i, more=True):
                for b in range(2):
                    k = i * 2 + b
                    sp.wait_ge(sr_ready, k + 1)
                    if more:
                        load_x(k + 4, b)
                    sp.dma_start(s_tab[:, bass.ds(k * JB, JB), :], sr[b][:, :, 0:F]).then_inc(tabled[b], 16)
                    sp.dma_start(r_tab[:, bass.ds(k * JB, JB), :], sr[b][:, :, F:2 * F]).then_inc(tabled[b], 16)

            load_x(0, 0)
            load_x(1, 1)
            sp.wait_ge(padded, 1)
            src = A["src"][0:(P - 1) * RUN].rearrange("(p k) -> p k", k=RUN)
            sp.dma_start(R["src"][0:112, :], src[0:112, :]).then_inc(src_in, 16)
            sp.dma_start(R["src"][112:P - 1, :], src[112:P - 1, :]).then_inc(src_in, 16)
            sp.dma_start(R["src"][P - 1:P, 0:LAST * T], A["src"][(P - 1) * RUN:E].rearrange("(a k) -> a k", a=1)).then_inc(src_in, 16)
            for b in range(2):
                sp.wait_ge(base_ready, b + 1)
                load_x(2 + b, b)
            with sp.Fori(0, HALF - 2) as i:
                tables(i)
            tables(HALF - 2, more=False)
            tables(HALF - 1, more=False)
            sp.wait_ge(src_in, 48)
            for b in range(2):
                sp.wait_ge(tabled[b], 32 * HALF)

        @block.gpsimd
        def _(pool):
            at = lambda ap: bass.IndirectOffsetOnAxis(ap=ap, axis=0)
            pool.indirect_dma_start(out=got[:, :], out_offset=None, in_=sums_d, in_offset=at(R["mend"][:, :])).then_inc(got_in, 16)
            pool.wait_ge(mended, 1)
            pool.indirect_dma_start(out=sums_d, out_offset=at(R["mend"][:, :]), in_=got[:, :], in_offset=None).then_inc(mended_out, 16)
            pool.wait_ge(mended_out, 16)

            def gather(k, b):
                pool.wait_ge(staged, k + 1)
                pool.sem_inc(turn, 1)
                for m in range(JB):
                    pool.indirect_dma_start(out=agg[b][:, m, :], out_offset=None, in_=sums_d, in_offset=at(ends[b][:, m:m + 1])).then_inc(gathered[b], 16)

            def scatter(k, b):
                pool.wait_ge(sr_ready, k + 1)
                pool.sem_inc(turn, 1)
                for m in range(JB):
                    pool.indirect_dma_start(out=sums_d, out_offset=at(starts[b][:, m:m + 1]), in_=sr[b][:, m, F:2 * F], in_offset=None)\
                        .then_inc(scattered[b], 16)

            for k in range(3):
                gather(k, k % 2)
            with pool.Fori(0, HALF - 2) as i:
                for b in range(2):
                    scatter(i * 2 + b, b)
                    gather(i * 2 + b + 3, 1 - b)
            scatter(NS - 4, 0)
            gather(NS - 1, 1)
            for k in range(NS - 3, NS):
                scatter(k, k % 2)
            for b in range(2):
                pool.wait_ge(scattered[b], 16 * JB * HALF)

        @block.tensor
        def _(pe):
            pe.wait_ge(scaled, 2)
            nc.tensor.transpose(onw_ps, onw[:, :], R["ident"][:, :])
            nc.tensor.transpose(whl_ps, whl[:, :], R["ident"][:, :]).then_inc(turned, 1)
            pe.wait_ge(cin_ready, 1)
            nc.tensor.transpose(back_ps, cin_t[:, 0:P], R["ident"][0:F, 0:F]).then_inc(cin_back, 1)

            def step(k):
                pe.wait_ge(h_ready, k + 1)
                pe.sem_inc(turn, 1)
                for j in range(JB):
                    last = nc.tensor.transpose(hT_ps[:, j // 4, (j % 4) * NP:(j % 4 + 1) * NP], hh[:, j, :], R["ident"][0:NP, 0:NP])
                last.then_inc(hT_in_ps, 1)
                pe.wait_ge(hT_ready, k + 1)
                wait(pe, sr_ready, k)
                for j in range(JB):
                    last = nc.tensor.matmul(pr_ps[:, j // 4, (j % 4) * P:(j % 4 + 1) * P], hT[:, j, :], R["wsr"][:, :], start=True, stop=True)
                last.then_inc(pr_in_ps, 1)

            step(0)
            with pe.Fori(1, NS) as k:
                step(k)

        @block.scalar
        def _(act):
            def root(var_ready, std_ready, n):
                act.wait_ge(var_ready, n + 1)
                nc.scalar.activation(std[:, :], st[:, :], ACT.Sqrt, bias=epst[:, :], scale=1.0 / F).then_inc(std_ready, 1)

            def step(k, more=True):
                root(var_h, std_h, k)
                if more:
                    root(var_x, std_x, k + 2)
                act.wait_ge(hT_in_ps, k + 1)
                for q, w in enumerate((4, 4, 2)):
                    nc.scalar.activation(hT[:, 4 * q:4 * q + w, :], hT_ps[:, q, 0:w * NP].rearrange("f (j n) -> f j n", n=NP), ACT.Copy)\
                        .then_inc(hT_part, 1)
                act.wait_ge(hT_part, k * 3 + 3)
                act.sem_inc(hT_ready, 1)

            act.wait_ge(scaled, 2)
            for k in range(2):
                root(var_x, std_x, k)
            with act.Fori(0, NS - 2) as k:
                step(k)
            for k in range(NS - 2, NS):
                step(k, more=False)

        @block.vector
        def _(dve):
            do = Order(dve, chain)
            wide = [NP, JB, F]
            do(nc.vector.memset(epst[:, :], EPS))
            nc.vector.tensor_scalar(onw[:, :], R["state"][:, 0:F], R["onward"][:, :], None, ALU.mult).then_inc(scaled, 1)
            nc.vector.tensor_copy(whl[:, :], R["whole"][:, :].to_broadcast([P, F])).then_inc(scaled, 1)
            do(nc.vector.memset(cin_t[:, 0:1], 0.0))
            dve.wait_ge(turned, 1)
            do(nc.vector.tensor_copy(whl_t[:, :], whl_ps))
            nc.vector.tensor_tensor_scan(cin_t[:, 1:P + 1], whl_t[:, :], onw_ps, 0.0, ALU.mult, ALU.add).then_inc(cin_ready, 1)
            nc.vector.memset(R["src"][96:P, LAST * T:RUN], 0).then_inc(padded, 1)
            dve.wait_ge(cin_back, 1)
            dve.wait_ge(got_in, 16)
            nc.vector.tensor_tensor(got[:, :], got[:, :], back_ps, ALU.add).then_inc(mended, 1)

            def stage(k, b):
                nc.vector.tensor_copy(ends[b][:, :], R["end"][:, bass.ds(k * JB, JB)]).then_inc(staged, 1)

            def normalize(do, src, var_ready, std_ready, n):
                do(nc.vector.tensor_reduce(st[:, :], src, AX, ALU.add))
                do(nc.vector.tensor_scalar(st[:, :], st[:, :], 1.0 / F, None, ALU.mult))
                do(nc.vector.tensor_tensor(xc[:, :, :], src, st[:, :].unsqueeze(2).to_broadcast(wide), ALU.subtract))
                do(nc.vector.tensor_tensor(sq[:, :, :], xc[:, :, :], xc[:, :, :], ALU.mult))
                nc.vector.tensor_reduce(st[:, :], sq[:, :, :], AX, ALU.add).then_inc(var_ready, 1)
                dve.wait_ge(std_ready, n + 1)
                do(nc.vector.reciprocal(st[:, :], std[:, :]))
                do(nc.vector.tensor_tensor(xc[:, :, :], xc[:, :, :], st[:, :].unsqueeze(2).to_broadcast(wide), ALU.mult))

            def first_part(do, i, b):
                dve.wait_ge(x_in[b], i * 16 + 16)
                normalize(do, x[b][:, :, :], var_x, std_x, i * 2 + b)
                do(nc.vector.scalar_tensor_tensor(R["base"][:, bass.ds((i * 2 + b) * JB, JB), :], xc[:, :, :], 0.0, x[b][:, :, :],
                                                  ALU.max, ALU.add))
                dve.sem_inc(base_ready, 1)

            def step(i, b, count, first=False, last=False):
                k = i * 2 + b
                do = Order(dve, chain, count)
                cols = bass.ds(k * JB, JB)
                base = R["base"][:, cols, :]
                dve.wait_ge(gathered[b], i * 16 * JB + 16 * JB)
                do(nc.vector.tensor_tensor(agg[b][:, :, :], agg[b][:, :, :], half[:, cols].unsqueeze(2).to_broadcast(wide), ALU.mult))
                do(nc.vector.tensor_tensor(base, base, agg[b][:, :, :], ALU.add))
                if not last:
                    stage(k + 2, b)
                normalize(do, base, var_h, std_h, k)
                nc.vector.tensor_scalar(hh[:, :, :], xc[:, :, :], 0.0, None, ALU.max).then_inc(h_ready, 1)
                if not last:
                    dve.wait_ge(h_ready, k + 1)
                    first_part(do, i + 1, b)
                if not first:
                    dve.wait_ge(scattered[b], i * 16 * JB)
                    dve.wait_ge(tabled[b], i * 32)
                do(nc.vector.tensor_copy(starts[b][:, :], R["start"][:, cols]))
                dve.wait_ge(pr_in_ps, k + 1)
                for q, w in enumerate((4, 4, 2)):
                    do(nc.vector.tensor_tensor(sr[b][:, 4 * q:4 * q + w, :], pr_ps[:, q, 0:w * P].rearrange("n (j c) -> n j c", c=P),
                                               R["bsr"][0:NP, :].unsqueeze(1).to_broadcast([NP, w, 2 * F]), ALU.add))
                dve.sem_inc(sr_ready, 1)
                assert do.n == (12 if last else STEP), do.n

            STEP = 19
            do(nc.vector.tensor_scalar(half[:, :], R["pres"][:, :], 0.5, None, ALU.mult))
            stage(0, 0)
            stage(1, 1)
            for b in range(2):
                first_part(do, 0, b)
            done = do.n
            for b in range(2):
                step(0, b, done + b * STEP, first=True)
            with dve.Fori(1, HALF - 1) as i:
                for b in range(2):
                    step(i, b, i * (2 * STEP) + (done + b * STEP))
            for b in range(2):
                step(HALF - 1, b, done + (NS - 2) * STEP + 12 * b, last=True)


def attention(nc, R, A, D):
    with ExitStack() as ctx:
        def sb(name, shape, dt=f32):
            return ctx.enter_context(nc.sbuf_tensor(name, shape, dt))

        def sem(name):
            return ctx.enter_context(nc.semaphore(name))

        U = 4
        idx = [sb(f"idx{u}", [P, T], i32) for u in range(U)]
        se = [sb(f"se{u}", [P, T, F]) for u in range(U)]
        rs = [sb(f"rs{b}", [P, T, F]) for b in range(2)]
        keepf = [sb(f"akeepf{b}", [P, F, T]) for b in range(2)]
        rnew = sb("rnew", [P, F, T])
        rneg = sb("rneg", [P, F, T])
        z = [sb(f"z{b}", [P, F, T]) for b in range(2)]
        t1 = sb("t1", [P, F, T])
        t2 = sb("t2", [P, F, T])
        decf = sb("decf", [P, F, T])
        wse = sb("wse", [P, F, T])
        num = sb("num", [P, F, T])
        lg = sb("lg", [P, H, T])
        kneg = sb("kneg", [P, T])
        mx = sb("mx", [P, H, T + 1])
        den = sb("den", [P, H, T + 1])
        exin = sb("exin", [P, 2, H, T])
        ex = sb("ex", [P, 2, H, T])
        dec = sb("dec", [P, H, T])
        tmp = sb("tmp", [P, F])
        heads = sb("heads", [P, F])
        rows = [sb(f"arows{b}", [P, T, ROW]) for b in range(2)]

        heads_in = sem("heads_in")
        heads_out = sem("heads_out")
        inited = sem("inited")
        idx_ready = sem("idx_ready")
        turn = sem("turn")
        gathered = [sem(f"agathered{u}") for u in range(U)]
        rs_in = [sem(f"rs_in{b}") for b in range(2)]
        rnew_ready = sem("rnew_ready")
        chain = sem("chain")
        keepf_ready = sem("keepf_ready")
        carried = sem("carried")
        held = sem("held")
        z_ready = sem("z_ready")
        expz_ready = sem("expz_ready")
        bounded = sem("bounded")
        softplus_ready = sem("softplus_ready")
        tanh_ready = sem("tanh_ready")
        exin_ready = sem("exin_ready")
        ex_ready = sem("ex_ready")
        dec_ready = sem("dec_ready")
        decf_ready = sem("decf_ready")
        se_used = sem("se_used")
        summed = sem("summed")
        rows_ready = sem("rows_ready")
        stored = [sem(f"astored{b}") for b in range(2)]
        block = ctx.enter_context(nc.Block())
        NI = CH // U
        rs_d = D["sums"][0:P * RUN, :].rearrange("(p c k) f -> p c (k f)", p=P, c=CH)
        st_d = D["states"][0:P * RUN, :].rearrange("(p c k) f -> p c (k f)", p=P, c=CH)

        @block.sync
        def _(sp):
            def load(c, b):
                sp.dma_start(rs[b][:, :, :].rearrange("p k f -> p (k f)").unsqueeze(1), rs_d[:, bass.ds(c, 1), :]).then_inc(rs_in[b], 16)

            def store(c, b):
                sp.wait_ge(rows_ready, (c + 1) * 3)
                sp.dma_start(st_d[:, bass.ds(c, 1), :], rows[b][:, :, :].rearrange("p k f -> p (k f)").unsqueeze(1)).then_inc(stored[b], 16)

            def body(i, first=False, last=False):
                for u in range(U):
                    c = i * U + u
                    if not (last and u + 2 >= U):
                        sp.wait_ge(rnew_ready, c + 1)
                        load(c + 2, u % 2)
                    if not (first and u == 0):
                        store(c - 1, 1 - u % 2)

            sp.wait_ge(heads_in, 16)
            sp.dma_start(D["sums"][0:P * RUN, :].rearrange("(p k) f -> p k f", p=P)[:, 0:1, :], heads[:, :].unsqueeze(1)).then_inc(heads_out, 16)
            load(1, 1)
            sp.wait_ge(heads_out, 16)
            load(0, 0)
            body(0, first=True)
            with sp.Fori(1, NI - 1) as i:
                body(i)
            body(NI - 1, last=True)
            store(CH - 1, 1)
            for b in range(2):
                sp.wait_ge(stored[b], 16 * CH // 2)

        @block.gpsimd
        def _(pool):
            def gather(i, u, first=False):
                c = i * U + u
                if not first:
                    pool.wait_ge(se_used, c - U + 1)
                    pool.wait_ge(idx_ready, c - U + 1)
                    pool.sem_inc(turn, 1)
                node = R["src"][:, u * T:(u + 1) * T] if first else idx[u][:, :]
                for k in range(T):
                    pool.indirect_dma_start(out=se[u][:, k, :], out_offset=None, in_=D["s_proj"],
                                            in_offset=bass.IndirectOffsetOnAxis(ap=node[:, k:k + 1], axis=0)).then_inc(gathered[u], 16)

            pool.indirect_dma_start(out=heads[:, :], out_offset=None, in_=D["r_proj"],
                                    in_offset=bass.IndirectOffsetOnAxis(ap=R["first"][:, :], axis=0)).then_inc(heads_in, 16)
            for u in range(U):
                gather(0, u, first=True)
            with pool.Fori(1, NI) as i:
                for u in range(U):
                    gather(i, u)
            for u in range(U):
                pool.wait_ge(gathered[u], 16 * T * NI)

        @block.scalar
        def _(act):
            def spread(c, b):
                src = R["keep"][:, bass.ds(c * T + 1, T - 1)].unsqueeze(1).to_broadcast([P, F, T - 1])
                nc.scalar.activation(keepf[b][:, :, 1:T], src, ACT.Copy).then_inc(keepf_ready, 1)

            def index(c, u):
                nc.scalar.activation(idx[u][:, :], R["src"][:, bass.ds(c * T, T)], ACT.Copy).then_inc(idx_ready, 1)

            def body(i, first=False, last=False):
                for u in range(U):
                    b = u % 2
                    c = i * U + u
                    act.wait_ge(z_ready, c + 1)
                    nc.scalar.activation(t1[:, :, :], z[b][:, :, :], ACT.Exp).then_inc(expz_ready, 1)
                    act.wait_ge(bounded, c + 1)
                    nc.scalar.activation(t1[:, :, :], t1[:, :, :], ACT.Ln, bias=1.0).then_inc(softplus_ready, 1)
                    act.wait_ge(softplus_ready, c + 1)
                    nc.scalar.activation(t2[:, :, :], t1[:, :, :], ACT.Tanh).then_inc(tanh_ready, 1)
                    if not (last and u + 2 >= U):
                        wait(act, held, c + 1)
                        spread(c + 2, b)
                    if not last:
                        act.wait_ge(gathered[u], i * 16 * T + 16 * T)
                        index(c + U, u)
                    act.wait_ge(exin_ready, c + 1)
                    nc.scalar.activation(ex[:, :, :, :], exin[:, :, :, :], ACT.Exp).then_inc(ex_ready, 1)
                    act.wait_ge(dec_ready, c + 1)
                    nc.scalar.activation(decf[:, :, 1:T].rearrange("p (h d) t -> p h d t", h=H),
                                         dec[:, :, 1:T].unsqueeze(2).to_broadcast([P, H, HD, T - 1]), ACT.Copy).then_inc(decf_ready, 1)
                    act.wait_ge(summed, (c + 1) * 2)
                    if not (first and u < 2):
                        act.wait_ge(stored[b], (i * (U // 2) + u // 2) * 16)
                    nc.scalar.activation(rows[b][:, :, 0:F], num[:, :, :].rearrange("p f t -> p t f"), ACT.Copy).then_inc(rows_ready, 1)
                    nc.scalar.activation(rows[b][:, :, F:F + H], den[:, :, 1:T + 1].rearrange("p h t -> p t h"), ACT.Copy).then_inc(rows_ready, 1)
                    nc.scalar.activation(rows[b][:, :, F + H:ROW], mx[:, :, 1:T + 1].rearrange("p h t -> p t h"), ACT.Copy).then_inc(rows_ready, 1)

            act.wait_ge(inited, 7)
            for b in range(2):
                spread(b, b)
            body(0, first=True)
            with act.Fori(1, NI - 1) as i:
                body(i)
            body(NI - 1, last=True)

        @block.vector
        def _(dve):
            flat = lambda x: x.rearrange("p f t -> p (f t)")
            STEP = 19

            def edge_inputs(i, u):
                i, u = i + u // U, u % U
                c, b = i * U + u, u % 2
                kp = R["keep"][:, bass.ds(c * T, T)].unsqueeze(1).to_broadcast([P, F, T])
                dve.wait_ge(rs_in[b], (i * (U // 2) + u // 2) * 16 + 16)
                nc.vector.scalar_tensor_tensor(rnew[:, :, :], kp, 1.0, rs[b][:, :, :].rearrange("p k f -> p f k"),
                                               ALU.subtract, ALU.mult).then_inc(rnew_ready, 1)
                dve.wait_ge(rnew_ready, c + 1)
                wait(dve, held, c)
                nc.vector.scalar_tensor_tensor(rnew[:, :, 0], rneg[:, :, T - 1], R["keep"][:, bass.ds(c * T, 1)], rnew[:, :, 0],
                                               ALU.mult, ALU.add).then_inc(carried, 1)
                dve.wait_ge(carried, c + 1)
                dve.wait_ge(keepf_ready, c + 1)
                nc.vector.tensor_tensor_scan(flat(rneg[:, :, :]), flat(keepf[b][:, :, :]), flat(rnew[:, :, :]), 0.0, ALU.mult, ALU.add)\
                    .then_inc(held, 1)
                dve.wait_ge(held, c + 1)
                dve.wait_ge(gathered[u], i * 16 * T + 16 * T)
                nc.vector.tensor_tensor(z[b][:, :, :], se[u][:, :, :].rearrange("p k f -> p f k"), rneg[:, :, :], ALU.subtract)\
                    .then_inc(z_ready, 1)

            def body(i, last=False):
                for u in range(U):
                    c, b = i * U + u, u % 2
                    do = Order(dve, chain, c * STEP)
                    dve.wait_ge(expz_ready, c + 1)
                    nc.vector.tensor_scalar(t1[:, :, :], t1[:, :, :], 2.0 ** 60, None, ALU.min).then_inc(bounded, 1)
                    if not (last and u + 1 >= U):
                        edge_inputs(i, u + 1)
                    kp = R["keep"][:, bass.ds(c * T, T)]
                    do(nc.vector.tensor_scalar(kneg[:, :], kp, -1.0, BIG, ALU.add, ALU.mult))
                    dve.wait_ge(tanh_ready, c + 1)
                    do(nc.vector.tensor_tensor(t2[:, :, :], z[b][:, :, :], t2[:, :, :], ALU.mult))
                    do(nc.vector.tensor_tensor(t2[:, :, :], t2[:, :, :], R["aw"][:, :].unsqueeze(2).to_broadcast([P, F, T]), ALU.mult))
                    do(nc.vector.tensor_reduce(lg[:, :, :], t2[:, :, :].rearrange("p (h d) t -> p h t d", h=H), AX, ALU.add))
                    do(nc.vector.tensor_scalar(lg[:, :, :], lg[:, :, :], R["ab"][:, :], None, ALU.add))
                    wait(dve, rows_ready, c * 3)
                    for h in range(H):
                        do(nc.vector.tensor_tensor_scan(mx[:, h, 1:T + 1], kneg[:, :], lg[:, h, :], mx[:, h, 0:1], ALU.add, ALU.max))
                    do(nc.vector.tensor_tensor(exin[:, 0, :, :], mx[:, :, 0:T], mx[:, :, 1:T + 1], ALU.subtract))
                    do(nc.vector.tensor_scalar(exin[:, 0, :, :], exin[:, 0, :, :], 0.0, None, ALU.min))
                    nc.vector.tensor_tensor(exin[:, 1, :, :], lg[:, :, :], mx[:, :, 1:T + 1], ALU.subtract).then_inc(exin_ready, 1)
                    do(nc.vector.tensor_copy(mx[:, :, 0], mx[:, :, T]))
                    dve.wait_ge(ex_ready, c + 1)
                    nc.vector.tensor_tensor(dec[:, :, :], ex[:, 0, :, :], kp.unsqueeze(1).to_broadcast([P, H, T]), ALU.mult).then_inc(dec_ready, 1)
                    nc.vector.tensor_tensor(wse[:, :, :].rearrange("p (h d) t -> p h d t", h=H),
                                            se[u][:, :, :].rearrange("p k (h d) -> p h d k", h=H),
                                            ex[:, 1, :, :].unsqueeze(2).to_broadcast([P, H, HD, T]), ALU.mult).then_inc(se_used, 1)
                    dve.wait_ge(dec_ready, c + 1)
                    for h in range(H):
                        do(nc.vector.tensor_tensor_scan(den[:, h, 1:T + 1], dec[:, h, :], ex[:, 1, h, :], den[:, h, 0:1], ALU.mult, ALU.add))
                    do(nc.vector.tensor_copy(den[:, :, 0], den[:, :, T]))
                    do(nc.vector.tensor_tensor(tmp[:, :].rearrange("p (h d) -> p h d", h=H), num[:, :, T - 1].rearrange("p (h d) -> p h d", h=H),
                                               dec[:, :, 0:1].to_broadcast([P, H, HD]), ALU.mult))
                    dve.wait_ge(se_used, c + 1)
                    do(nc.vector.tensor_tensor(wse[:, :, 0], wse[:, :, 0], tmp[:, :], ALU.add))
                    dve.wait_ge(decf_ready, c + 1)
                    nc.vector.tensor_tensor_scan(flat(num[:, :, :]), flat(decf[:, :, :]), flat(wse[:, :, :]), 0.0, ALU.mult, ALU.add)\
                        .then_inc(summed, 1)
                    dve.wait_ge(summed, c * 2 + 1)
                    dve.sem_inc(summed, 1)
                    assert do.n == STEP, do.n

            for tile, value in ((keepf[0], 0.0), (keepf[1], 0.0), (decf, 0.0), (rneg, 0.0), (num, 0.0), (mx, -BIG), (den, 0.0)):
                nc.vector.memset(tile[:, :, :], value).then_inc(inited, 1)
            dve.wait_ge(inited, 7)
            edge_inputs(0, 0)
            body(0)
            with dve.Fori(1, NI - 1) as i:
                body(i)
            body(NI - 1, last=True)
            nc.vector.tensor_copy(R["state"][:, 0:F], num[:, :, T - 1]).then_inc(inited, 1)
            nc.vector.tensor_copy(R["state"][:, F:F + H], den[:, :, T]).then_inc(inited, 1)
            nc.vector.tensor_copy(R["state"][:, F + H:ROW], mx[:, :, T]).then_inc(inited, 1)


def finish(nc, R, A, D, out, ABW=F + H):
    with ExitStack() as ctx:
        def sb(name, shape, dt=f32):
            return ctx.enter_context(nc.sbuf_tensor(name, shape, dt))

        def ps(name, shape):
            return ctx.enter_context(nc.psum_tensor(name, shape, f32))

        def sem(name):
            return ctx.enter_context(nc.semaphore(name))

        drop = sb("drop", [P, H])
        drop_t = sb("drop_t", [H, P])
        mx_t = sb("mx_t", [H, P + 1])
        mio = sb("mio", [P, 2, H])
        e = sb("e", [P, 2, H])
        add = sb("add", [P, ABW])
        mul = sb("mul", [P, ABW])
        mul_t = sb("mul_t", [ABW, P])
        cin_t = sb("fcin_t", [ABW, P + 1])
        cin = sb("cin", [P, ABW])
        got = sb("fgot", [P, ROW])
        mt = sb("mt", [P, H])
        ends = [sb(f"fends{b}", [NP, JB], i32) for b in range(2)]
        q = [sb(f"q{b}", [NP, JB, ROW]) for b in range(2)]
        inv = sb("inv", [NP, JB, H])
        res = [sb(f"res{b}", [NP, JB, F]) for b in range(2)]
        a_ps, b_ps = ps("a_ps", [P, 512]), ps("b_ps", [P, 512])

        chain = sem("chain")
        pe_do = [sem(f"pe_do{k}") for k in range(4)]
        pe_did = [sem(f"pe_did{k}") for k in range(4)]
        act_do = [sem(f"act_do{k}") for k in range(2)]
        act_did = [sem(f"act_did{k}") for k in range(2)]
        got_in = sem("got_in")
        mended = sem("mended")
        mended_out = sem("mended_out")
        staged = sem("staged")
        turn = sem("turn")
        gathered = [sem(f"fgathered{b}") for b in range(2)]
        res_ready = sem("res_ready")
        out_done = [sem(f"out_done{b}") for b in range(2)]
        block = ctx.enter_context(nc.Block())
        out_v = out.rearrange("(p j) f -> p j f", p=NP)

        @block.sync
        def _(sp):
            with sp.Fori(0, NS // 2) as i:
                for b in range(2):
                    sp.wait_ge(res_ready, i * 2 + b + 1)
                    sp.dma_start(out_v[:, bass.ds((i * 2 + b) * JB, JB), :], res[b][:, :, :]).then_inc(out_done[b], 16)
            for b in range(2):
                sp.wait_ge(out_done[b], 16 * NS // 2)

        @block.gpsimd
        def _(pool):
            at = lambda ap: bass.IndirectOffsetOnAxis(ap=ap, axis=0)
            pool.indirect_dma_start(out=got[:, :], out_offset=None, in_=D["states"], in_offset=at(R["mend"][:, :])).then_inc(got_in, 16)
            pool.wait_ge(mended, 1)
            pool.indirect_dma_start(out=D["states"], out_offset=at(R["mend"][:, :]), in_=got[:, :], in_offset=None).then_inc(mended_out, 16)
            pool.wait_ge(mended_out, 16)
            with pool.Fori(0, NS // 2) as i:
                for b in range(2):
                    pool.wait_ge(staged, i * 2 + b + 1)
                    pool.sem_inc(turn, 1)
                    for m in range(JB):
                        pool.indirect_dma_start(out=q[b][:, m, :], out_offset=None, in_=D["states"], in_offset=at(ends[b][:, m:m + 1]))\
                            .then_inc(gathered[b], 16)

        @block.tensor
        def _(pe):
            ident = R["ident"]
            pe.wait_ge(pe_do[0], 1)
            nc.tensor.transpose(a_ps[0:H, 0:P], R["state"][:, F + H:ROW], ident[:, :])
            nc.tensor.transpose(b_ps[0:H, 0:P], drop[:, :], ident[:, :]).then_inc(pe_did[0], 1)
            pe.wait_ge(pe_do[1], 1)
            nc.tensor.transpose(a_ps[:, 0:H], mx_t[:, 0:P], ident[0:H, 0:H])
            nc.tensor.transpose(b_ps[:, 0:H], mx_t[:, 1:P + 1], ident[0:H, 0:H]).then_inc(pe_did[1], 1)
            pe.wait_ge(pe_do[2], 1)
            nc.tensor.transpose(a_ps[0:ABW, 0:P], add[:, :], ident[:, :])
            nc.tensor.transpose(b_ps[0:ABW, 0:P], mul[:, :], ident[:, :]).then_inc(pe_did[2], 1)
            pe.wait_ge(pe_do[3], 1)
            nc.tensor.transpose(a_ps[:, 0:ABW], cin_t[:, 0:P], ident[0:ABW, 0:ABW]).then_inc(pe_did[3], 1)

        @block.scalar
        def _(act):
            for k in range(2):
                act.wait_ge(act_do[k], 1)
                nc.scalar.activation(e[:, :, :], e[:, :, :], ACT.Exp).then_inc(act_did[k], 1)

        @block.vector
        def _(dve):
            do = Order(dve, chain)

            def heads_wide(x):
                return x.unsqueeze(2).to_broadcast([P, H, HD])

            def by_head(x):
                return x.rearrange("p (h d) -> p h d", h=H)

            do(nc.vector.memset(mx_t[:, 0:1], -BIG))
            do(nc.vector.memset(cin_t[:, 0:1], 0.0))
            nc.vector.tensor_scalar(drop[:, :], R["whole"][:, :].to_broadcast([P, H]), -1.0, BIG, ALU.add, ALU.mult).then_inc(pe_do[0], 1)
            dve.wait_ge(pe_did[0], 1)
            do(nc.vector.tensor_copy(drop_t[:, :], b_ps[0:H, 0:P]))
            nc.vector.tensor_tensor_scan(mx_t[:, 1:P + 1], drop_t[:, :], a_ps[0:H, 0:P], -BIG, ALU.add, ALU.max).then_inc(pe_do[1], 1)
            dve.wait_ge(pe_did[1], 1)
            do(nc.vector.tensor_copy(mio[:, 0, :], a_ps[:, 0:H]))
            do(nc.vector.tensor_copy(mio[:, 1, :], b_ps[:, 0:H]))
            do(nc.vector.tensor_tensor(e[:, 0, :], mio[:, 0, :], mio[:, 1, :], ALU.subtract))
            do(nc.vector.tensor_scalar(e[:, 0, :], e[:, 0, :], 0.0, None, ALU.min))
            nc.vector.tensor_tensor(e[:, 1, :], R["state"][:, F + H:ROW], mio[:, 1, :], ALU.subtract).then_inc(act_do[0], 1)
            dve.wait_ge(act_did[0], 1)
            do(nc.vector.tensor_scalar(e[:, 0, :], e[:, 0, :], R["whole"][:, :], None, ALU.mult))
            do(nc.vector.tensor_scalar(e[:, 1, :], e[:, 1, :], R["onward"][:, :], None, ALU.mult))
            do(nc.vector.tensor_copy(by_head(mul[:, 0:F]), heads_wide(e[:, 0, :])))
            do(nc.vector.tensor_copy(mul[:, F:ABW], e[:, 0, :]))
            do(nc.vector.tensor_tensor(by_head(add[:, 0:F]), by_head(R["state"][:, 0:F]), heads_wide(e[:, 1, :]), ALU.mult))
            nc.vector.tensor_tensor(add[:, F:ABW], R["state"][:, F:F + H], e[:, 1, :], ALU.mult).then_inc(pe_do[2], 1)
            dve.wait_ge(pe_did[2], 1)
            do(nc.vector.tensor_copy(mul_t[:, :], b_ps[0:ABW, 0:P]))
            nc.vector.tensor_tensor_scan(cin_t[:, 1:P + 1], mul_t[:, :], a_ps[0:ABW, 0:P], 0.0, ALU.mult, ALU.add).then_inc(pe_do[3], 1)
            dve.wait_ge(pe_did[3], 1)
            do(nc.vector.tensor_copy(cin[:, :], a_ps[:, 0:ABW]))
            dve.wait_ge(got_in, 16)
            do(nc.vector.tensor_tensor(mt[:, :], got[:, F + H:ROW], mio[:, 0, :], ALU.max))
            do(nc.vector.tensor_tensor(e[:, 0, :], got[:, F + H:ROW], mt[:, :], ALU.subtract))
            nc.vector.tensor_tensor(e[:, 1, :], mio[:, 0, :], mt[:, :], ALU.subtract).then_inc(act_do[1], 1)
            dve.wait_ge(act_did[1], 1)
            do(nc.vector.tensor_scalar(e[:, 1, :], e[:, 1, :], R["cont"][:, :], None, ALU.mult))
            do(nc.vector.tensor_tensor(by_head(got[:, 0:F]), by_head(got[:, 0:F]), heads_wide(e[:, 0, :]), ALU.mult))
            do(nc.vector.tensor_tensor(got[:, F:ABW], got[:, F:ABW], e[:, 0, :], ALU.mult))
            do(nc.vector.tensor_tensor(by_head(cin[:, 0:F]), by_head(cin[:, 0:F]), heads_wide(e[:, 1, :]), ALU.mult))
            do(nc.vector.tensor_tensor(cin[:, F:ABW], cin[:, F:ABW], e[:, 1, :], ALU.mult))
            nc.vector.tensor_tensor(got[:, 0:ABW], got[:, 0:ABW], cin[:, :], ALU.add).then_inc(mended, 1)

            def stage(k, b):
                nc.vector.tensor_copy(ends[b][:, :], R["end"][:, bass.ds(k * JB, JB)]).then_inc(staged, 1)

            def step(i, b, first=False, more=True):
                k = i * 2 + b
                do = Order(dve, chain, base + k * 3)
                cols = bass.ds(k * JB, JB)
                dve.wait_ge(gathered[b], i * 16 * JB + 16 * JB)
                do(nc.vector.reciprocal(inv[:, :, :], q[b][:, :, F:F + H]))
                do(nc.vector.tensor_tensor(inv[:, :, :], inv[:, :, :], R["pres"][:, cols].unsqueeze(2).to_broadcast([NP, JB, H]), ALU.mult))
                if not first:
                    dve.wait_ge(out_done[b], i * 16)
                do(nc.vector.tensor_tensor(res[b][:, :, :].rearrange("n j (h d) -> n j h d", h=H),
                                           q[b][:, :, 0:F].rearrange("n j (h d) -> n j h d", h=H),
                                           inv[:, :, :].unsqueeze(3).to_broadcast([NP, JB, H, HD]), ALU.mult))
                nc.vector.tensor_tensor(res[b][:, :, :], res[b][:, :, :], R["base"][:, cols, :], ALU.add).then_inc(res_ready, 1)
                if more:
                    stage(k + 2, b)

            base = do.n
            stage(0, 0)
            stage(1, 1)
            for b in range(2):
                step(0, b, first=True)
            with dve.Fori(1, NS // 2 - 1) as i:
                for b in range(2):
                    step(i, b)
            for b in range(2):
                step(NS // 2 - 1, b, more=False)


def gnn_program(nc, A, out):
    D = {
        "samples": nc.dram_tensor("samples", [SB], i32).ap(),
        "sums": nc.dram_tensor("sums", [P * RUN, F], f32).ap(),
        "states": nc.dram_tensor("states", [P * RUN, ROW], f32).ap(),
        "s_proj": nc.dram_tensor("s_proj", [N, F], f32).ap(),
        "r_proj": nc.dram_tensor("r_proj", [N, F], f32).ap(),
    }
    with ExitStack() as ctx:
        shapes = {
            "base": ([NP, NJ, F], f32), "src": ([P, RUN], i32), "keep": ([P, RUN], f32), "ident": ([P, P], f32),
            "w1g1": ([P, 2 * F], f32), "w2g2": ([P, 2 * F], f32), "b1g1": ([P, 1], f32),
            "b2g2": ([P, 2 * F], f32),
            "wsr": ([F, 2 * F], f32), "bsr": ([P, 2 * F], f32), "aw": ([P, F], f32), "ab": ([P, 1], f32),
            "pres": ([NP, NJ], f32), "end": ([NP, NJ], f32), "start": ([NP, NJ], f32),
            "first": ([P, 1], i32), "mend": ([P, 1], i32), "cont": ([P, 1], f32), "onward": ([P, 1], f32),
            "whole": ([P, 1], f32), "state": ([P, ROW], f32),
        }
        R = {k: ctx.enter_context(nc.sbuf_tensor(f"r_{k}", s, d)) for k, (s, d) in shapes.items()}
        with ExitStack() as early:
            shapes = {"nid": ([P, NC], f32), "pid": ([P, 1], f32), "smb": ([P, SB], i32)}
            early_tiles = {k: early.enter_context(nc.sbuf_tensor(f"r_{k}", s, d)) for k, (s, d) in shapes.items()}
            setup(nc, R | early_tiles, A, D)
            edge_mlp(nc, R | early_tiles, A, D)
        update_nodes(nc, R, A, D)
        attention(nc, R, A, D)
        finish(nc, R, A, D, out)


_INS = ["x", "src", "dst", "edge_attr_64", "L0_gnn_W1", "L0_gnn_b1", "L0_gnn_W2", "L0_gnn_b2", "L0_gnn_G1", "L0_gnn_g1",
        "L0_gnn_G2", "L0_gnn_g2", "L1_gnn_Ws", "L1_gnn_bs", "L1_gnn_Wr", "L1_gnn_br", "L1_gnn_aw", "L1_gnn_ab"]


def kernel(**inputs):
    import numpy as np
    import concourse.bacc as bacc
    from concourse.bass_utils import run_bass_kernel_spmd

    nc = bacc.Bacc("TRN2", target_bir_lowering=False, num_devices=1)
    arrays, args = {}, {}
    for name in _INS:
        a = np.ascontiguousarray(inputs[name])
        arrays[f"in_{name}"] = a
        args[name] = nc.dram_tensor(f"in_{name}", a.shape, mybir.dt.from_np(a.dtype), kind="ExternalInput").ap()
    out = nc.dram_tensor("out_0", (N, F), f32, kind="ExternalOutput").ap()
    gnn_program(nc, args, out)
    return run_bass_kernel_spmd(nc, [arrays], core_ids=[0]).results[0]["out_0"]
```

```python
import concourse.bass as bass
from concourse import mybir
from contextlib import ExitStack

f32 = mybir.dt.float32
bf16 = mybir.dt.bfloat16
i32 = mybir.dt.int32
ALU = mybir.AluOpType
ACT = mybir.ActivationFunctionType
AX = mybir.AxisListType.X

P = 128
N = 12500
F = 64
E = 412500
H = 4
HD = F // H
T = 30
CH = -(-E // (T * P))
RUN = CH * T
LAST = (E - (P - 1) * RUN) // T
G = 5
TG = T // G
PAIRS = TG // 2
GC = PAIRS * P
NG = CH * G
QF = T * F
NP, NJ = 125, 100
JB = 10
NS = NJ // JB
SB, SL = 750, 550
NC = CH - 2
ROW = F + 2 * H
BIG = 1e30
EPS = 1e-5


def wait(eng, sem, value):
    if isinstance(value, int) and value <= 0:
        return
    eng.wait_ge(sem, value)


class Order:

    def __init__(self, eng, sem, base=0):
        self.eng, self.sem, self.base, self.n = eng, sem, base, 0

    def __call__(self, ins):
        self.n += 1
        ins.then_inc(self.sem, 1)
        self.eng.wait_ge(self.sem, self.base + self.n)


def last_run_split(view):
    return (view[0:(P - 1) * RUN].rearrange("(p c k) f -> p c (k f)", p=P - 1, c=CH),
            view[(P - 1) * RUN:E].rearrange("(c k) f -> c (k f)", k=T))


def load_chunk(sp, buf, split, chunk, tail_chunk, sem):
    body, tail = split
    sp.dma_start(buf[0:112, :].unsqueeze(1), body[0:112, bass.ds(chunk, 1), :]).then_inc(sem, 16)
    sp.dma_start(buf[112:127, :].unsqueeze(1), body[112:127, bass.ds(chunk, 1), :]).then_inc(sem, 16)
    sp.dma_start(buf[127:128, :], tail[bass.ds(tail_chunk, 1), :]).then_inc(sem, 16)


def edge_mlp(nc, R, A, D):
    with ExitStack() as ctx:
        def sb(name, shape, dt=f32):
            return ctx.enter_context(nc.sbuf_tensor(name, shape, dt))

        def sem(name):
            return ctx.enter_context(nc.semaphore(name))

        dsti = sb("dsti", [P, RUN], i32)
        near = sb("near", [P, 2], i32)
        nidi = sb("nidi", [P, NC], i32)
        nid = sb("nid", [P, NC])
        pidi = sb("pidi", [P, 1], i32)
        pid = sb("pid", [P, 1])
        sample = sb("sample", [NP, SB // NP], i32)
        samples = sb("samples_tile", [P, SB], i32)
        edges = [sb(f"edges{b}", [P, QF]) for b in range(2)]
        edges_t = [sb(f"edges_t{b}", [P, GC]) for b in range(2)]
        hidden = [sb(f"hidden{b}", [P, 2, GC]) for b in range(2)]
        value = [sb(f"value{b}", [P, TG, F]) for b in range(2)]
        gate = [sb(f"gate{b}", [P, TG, F]) for b in range(2)]
        msg = [sb(f"msg{b}", [P, F, T]) for b in range(2)]
        keepf = [sb(f"keepf{b}", [P, F, T]) for b in range(2)]
        sums = [sb(f"sums{b}", [P, F, T]) for b in range(2)]
        rows = [sb(f"rows{b}", [P, T, F]) for b in range(2)]
        junk1 = sb("junk1", [P, SB], bf16)
        junk2 = sb("junk2", [P, SL], bf16)
        blocks_upto = sb("blocks_upto", [P, NC])
        upto = sb("upto", [P, NC])
        block_id = [sb(f"block_id{b}", [P, 1], i32) for b in range(2)]
        block_of = [sb(f"block_of{b}", [P, SL], i32) for b in range(2)]
        fx = sb("fx", [P, 3])
        spare = sb("spare", [NP, NJ])
        tr_ps = [ctx.enter_context(nc.psum_tensor(f"tr_ps{b}", [P, 512], f32)) for b in range(2)]
        h_ps = ctx.enter_context(nc.psum_tensor("h_ps", [P, 2, 512], f32))
        o_ps = [ctx.enter_context(nc.psum_tensor(f"o_ps{b}", [P, 2, 512], f32)) for b in range(2)]

        padded = sem("padded")
        diag_zeroed = sem("diag_zeroed")
        dst_in = sem("dst_in")
        weights_in = sem("weights_in")
        later_in = sem("later_in")
        sample_in = sem("sample_in")
        sample_out = sem("sample_out")
        samples_in = sem("samples_in")
        iotas = sem("iotas")
        ident_steps = sem("ident_steps")
        keep_ready = sem("keep_ready")
        init = sem("init")
        loaded = [sem(f"loaded{b}") for b in range(2)]
        transposed = sem("transposed")
        edges_t_ready = sem("edges_t_ready")
        h_ready = sem("h_ready")
        hidden_ready = sem("hidden_ready")
        o_ready = sem("o_ready")
        biased = sem("biased")
        gated = sem("gated")
        msg_ready = sem("msg_ready")
        carried = sem("carried")
        scanned = sem("scanned")
        turn = sem("turn")
        keepf_ready = sem("keepf_ready")
        keepf_zeroed = sem("keepf_zeroed")
        state_ready = sem("state_ready")
        last_rows = sem("last_rows")
        rows_ready = sem("rows_ready")
        stored = [sem(f"stored{b}") for b in range(2)]
        chain = sem("chain")
        counted1 = sem("counted1")
        counted2 = sem("counted2")
        block_known = sem("block_known")
        block_in = [sem(f"block_in{b}") for b in range(2)]
        block = ctx.enter_context(nc.Block())
        split = last_run_split(A["edge_attr_64"])
        sums_d = D["sums"][0:P * RUN, :].rearrange("(p c k) f -> p c (k f)", p=P, c=CH)
        HALF = CH // 2
        AHEAD = 3
        PIECES = 4
        SHARE = 8
        WEIGHTS = 10

        def row(ap):
            return ap.rearrange("(a n) -> a n", a=1)

        dst = A["dst"]

        @block.sync
        def _(sp):
            def load(i, b, tail):
                load_chunk(sp, edges[b], split, i * 2 + b, tail, loaded[b])

            def store(c, b, last=False):
                if last:
                    sp.wait_ge(last_rows, 2)
                else:
                    sp.wait_ge(rows_ready, c + 1)
                sp.dma_start(sums_d[:, bass.ds(c, 1), :], rows[b][:, :, :].rearrange("p k f -> p (k f)").unsqueeze(1)).then_inc(stored[b], 16)

            def body(i, padded=False, first=False, last=False):
                for b in range(2):
                    if not last:
                        sp.wait_ge(transposed, (i * 2 + b + 1) * G)
                        load(i + 1, b, LAST - 1 if padded else (i + 1) * 2 + b)
                    if not (first and b == 0):
                        store(i * 2 + b - 1, 1 - b)

            one = dict(allow_slow_non_contiguous=True)
            load(0, 0, 0)
            sp.dma_start(sample[:, :], dst.rearrange("(p a k) -> p a k", p=NP, k=SL)[:, :, 0], **one).then_inc(sample_in, 16)
            sp.wait_ge(padded, 2)
            dst_body, dst_tail = dst[0:(P - 1) * RUN].rearrange("(p k) -> p k", k=RUN), dst[(P - 1) * RUN:E]
            sp.dma_start(dsti[0:112, :], dst_body[0:112, :]).then_inc(dst_in, 16)
            sp.dma_start(dsti[112:P - 1, :], dst_body[112:P - 1, :]).then_inc(dst_in, 16)
            sp.dma_start(dsti[P - 1:P, 0:LAST * T], dst_tail.rearrange("(a k) -> a k", a=1)).then_inc(dst_in, 16)
            sp.dma_start(near[1:P, 0:1], dst_body[:, RUN - 1:RUN], **one).then_inc(dst_in, 16)
            sp.dma_start(near[0:P - 2, 1:2], dst_body[1:, 0:1], **one).then_inc(dst_in, 16)
            sp.dma_start(near[P - 2:P - 1, 1:2], dst_tail[0:1].rearrange("(a k) -> a k", a=1)).then_inc(dst_in, 16)
            load(0, 1, 1)
            sp.wait_ge(sample_in, 16)
            sp.dma_start(D["samples"].rearrange("(p a) -> p a", p=NP), sample[:, :]).then_inc(sample_out, 16)
            sp.wait_ge(sample_out, 16)
            sp.dma_start(samples[:, :], row(D["samples"]).to_broadcast([P, SB])).then_inc(samples_in, 16)
            body(0, first=True)
            with sp.Fori(1, LAST // 2 - 1) as i:
                body(i)
            with sp.Fori(LAST // 2 - 1, HALF - 1) as i:
                body(i, padded=True)
            body(HALF - 1, last=True)
            store(CH - 1, 1, last=True)
            for b in range(2):
                sp.wait_ge(stored[b], 16 * HALF)

        @block.tensor
        def _(pe):
            def transpose(i, s):
                i, s = i + s // (2 * G), s % (2 * G)
                b, g = s // G, s % G
                if g == 0:
                    pe.wait_ge(loaded[b], i * 48 + 48)
                for j in range(PAIRS):
                    at = (g * TG + 2 * j) * F
                    last = nc.tensor.transpose(tr_ps[s % 2][:, j * P:(j + 1) * P], edges[b][:, at:at + 2 * F], R["ident"][:, :])
                last.then_inc(transposed, 1)

            def layer1(i, s):
                n = i * 2 * G + s
                pe.wait_ge(edges_t_ready, n + 1)
                wait(pe, hidden_ready, n)
                for a in range(2):
                    half = slice(F * a, F * a + F)
                    last = nc.tensor.matmul(h_ps[:, a, 0:GC], R["w1g1"][half, :], edges_t[s % 2][half, :], start=True, stop=True)
                last.then_inc(h_ready, 1)

            def layer2(i, s):
                n = i * 2 * G + s
                pe.wait_ge(hidden_ready, n + 1)
                wait(pe, gated, 2 * (n - 1))
                out, hid = o_ps[s % 2], hidden[s % 2]
                for k in range(2):
                    for m in range(PAIRS):
                        tile = k * PAIRS + m
                        at = (tile // 2) * P
                        last = nc.tensor.matmul(out[:, k, m * P:(m + 1) * P], hid[:, tile % 2, at:at + P], R["w2g2"][:, :],
                                                start=True, stop=True)
                last.then_inc(o_ready, 1)

            def body(i, last=False):
                for s in range(2 * G):
                    if not (last and s + 1 >= 2 * G):
                        layer1(i + (s + 1) // (2 * G), (s + 1) % (2 * G))
                    if not (last and s + AHEAD >= 2 * G):
                        transpose(i, s + AHEAD)
                    layer2(i, s)

            pe.wait_ge(ident_steps, 2)
            transpose(0, 0)
            transpose(0, 1)
            pe.wait_ge(weights_in, 16 * WEIGHTS)
            layer1(0, 0)
            transpose(0, 2)
            body(0)
            with pe.Fori(1, HALF - 1) as i:
                body(i)
            body(HALF - 1, last=True)

        @block.scalar
        def _(act):
            def hid(i, s):
                n = i * 2 * G + s
                act.wait_ge(h_ready, n + 1)
                nc.scalar.activation(hidden[s % 2][:, :, :], h_ps[:, :, 0:GC], ACT.Silu, bias=R["b1g1"][:, :]).then_inc(hidden_ready, 1)

            def outs(i, s):
                n = i * 2 * G + s
                act.wait_ge(biased, n + 1)
                wait(act, msg_ready, n - 1)
                o = o_ps[s % 2][:, :, 0:GC].rearrange("p k (m c) -> p k m c", c=P)
                v, g = (x[s % 2][:, :, :].rearrange("p (k m) f -> p k m f", k=2) for x in (value, gate))
                nc.scalar.activation(v, o[:, :, :, 0:F], ACT.Silu).then_inc(gated, 1)
                nc.scalar.activation(g, o[:, :, :, F:2 * F], ACT.Tanh, scale=0.5).then_inc(gated, 1)

            def body(i, first=False, last=False):
                for s in range(2 * G):
                    if not (last and s + 1 >= 2 * G):
                        hid(i + (s + 1) // (2 * G), (s + 1) % (2 * G))
                    if not (first and s == 0):
                        outs(i + (s - 1) // (2 * G), (s - 1) % (2 * G))

            for k in range(2):
                rows_k = slice(F * k, F * k + F)
                act.dma_start(R["w1g1"][rows_k, 0:F], A["L0_gnn_W1"]).then_inc(weights_in, 16)
                act.dma_start(R["w1g1"][rows_k, F:2 * F], A["L0_gnn_G1"]).then_inc(weights_in, 16)
            act.dma_start(R["b1g1"][0:F, :], A["L0_gnn_b1"].rearrange("(p a) -> p a", a=1), allow_slow_non_contiguous=True).then_inc(weights_in, 16)
            act.dma_start(R["b1g1"][F:2 * F, :], A["L0_gnn_g1"].rearrange("(p a) -> p a", a=1), allow_slow_non_contiguous=True).then_inc(weights_in, 16)
            act.wait_ge(diag_zeroed, 1)
            act.dma_start(R["w2g2"][0:F, 0:F], A["L0_gnn_W2"]).then_inc(weights_in, 16)
            act.dma_start(R["w2g2"][F:2 * F, F:2 * F], A["L0_gnn_G2"]).then_inc(weights_in, 16)
            act.dma_start(R["b2g2"][:, 0:F], row(A["L0_gnn_b2"]).to_broadcast([P, F])).then_inc(weights_in, 16)
            act.dma_start(R["b2g2"][:, F:2 * F], row(A["L0_gnn_g2"]).to_broadcast([P, F])).then_inc(weights_in, 16)
            act.dma_start(R["wsr"][:, 0:F], A["L1_gnn_Ws"].rearrange("f h d -> f (h d)")).then_inc(later_in, 16)
            act.dma_start(R["wsr"][:, F:2 * F], A["L1_gnn_Wr"].rearrange("f h d -> f (h d)")).then_inc(later_in, 16)
            act.dma_start(R["bsr"][:, 0:F], row(A["L1_gnn_bs"].rearrange("h d -> (h d)")).to_broadcast([P, F])).then_inc(later_in, 16)
            act.dma_start(R["bsr"][:, F:2 * F], row(A["L1_gnn_br"].rearrange("h d -> (h d)")).to_broadcast([P, F])).then_inc(later_in, 16)
            for h in range(H):
                act.dma_start(R["aw"][:, h * HD:(h + 1) * HD], row(A["L1_gnn_aw"]).to_broadcast([P, HD])).then_inc(later_in, 16)
            act.dma_start(R["ab"][:, :], row(A["L1_gnn_ab"]).to_broadcast([P, 1])).then_inc(later_in, 16)

            act.wait_ge(weights_in, 16 * WEIGHTS)
            hid(0, 0)
            body(0, first=True)
            with act.Fori(1, HALF - 1) as i:
                body(i)
            body(HALF - 1, last=True)
            outs(HALF - 1, 2 * G - 1)
            act.wait_ge(later_in, 16 * 9)
            act.wait_ge(stored[1], (HALF - 1) * 16)
            act.wait_ge(scanned, CH * PIECES)
            nc.scalar.activation(rows[1][:, SHARE:T, :], sums[1][:, :, SHARE:T].rearrange("p f t -> p t f"), ACT.Copy).then_inc(last_rows, 1)

        @block.vector
        def _(dve):
            def copy_t(i, s):
                n = i * 2 * G + s
                dve.wait_ge(transposed, n + 1)
                nc.vector.tensor_copy(edges_t[s % 2][:, :], tr_ps[s % 2][:, 0:GC]).then_inc(edges_t_ready, 1)

            def add_bias(i, s):
                dve.wait_ge(o_ready, i * 2 * G + s + 1)
                o = o_ps[s % 2][:, :, 0:GC].rearrange("p k (m c) -> p k m c", c=P)
                bias = R["b2g2"][:, :].unsqueeze(1).unsqueeze(1).to_broadcast([P, 2, PAIRS, P])
                nc.vector.tensor_tensor(o, o, bias, ALU.add).then_inc(biased, 1)

            def product(i, s):
                n = i * 2 * G + s
                b, g = s // G, s % G
                dve.wait_ge(gated, 2 * (n + 1))
                if g == 0:
                    wait(dve, scanned, (i * 2 + b - 1) * PIECES)
                out = msg[b][:, :, g * TG:(g + 1) * TG].rearrange("p f t -> p t f")
                nc.vector.scalar_tensor_tensor(out, gate[s % 2][:, :, :], 1.0, value[s % 2][:, :, :], ALU.add, ALU.mult)\
                    .then_inc(msg_ready, 1)

            def carry(c, b):
                dve.wait_ge(msg_ready, (c + 1) * G)
                wait(dve, scanned, c * PIECES)
                nc.vector.scalar_tensor_tensor(msg[b][:, :, 0], sums[1 - b][:, :, T - 1], R["keep"][:, bass.ds(c * T, 1)],
                                               msg[b][:, :, 0], ALU.mult, ALU.add).then_inc(carried, 1)

            def scan(c, b, k):
                if k == 0:
                    dve.wait_ge(keepf_zeroed, 2)
                    dve.wait_ge(carried, c + 1)
                    dve.wait_ge(keepf_ready, c + 1)
                    wait(dve, rows_ready, c - 1)
                fs = slice(k * F // PIECES, (k + 1) * F // PIECES)
                flat = [x[:, fs, :].rearrange("p f t -> p (f t)") for x in (sums[b], keepf[b], msg[b])]
                nc.vector.tensor_tensor_scan(flat[0], flat[1], flat[2], 0.0, ALU.mult, ALU.add).then_inc(scanned, 1)

            def find_block(i, b):
                q = i * 2 + b
                dve.wait_ge(samples_in, 16)
                nc.vector.tensor_scalar(junk1[:, :], samples[:, :], nid[:, bass.ds(q, 1)], 0.0, ALU.is_le, ALU.add,
                                        accum_out=blocks_upto[:, bass.ds(q, 1)]).then_inc(counted1, 1)
                dve.wait_ge(counted1, q + 1)
                nc.vector.tensor_scalar(block_id[b][:, :], blocks_upto[:, bass.ds(q, 1)], -1.0, 0.0, ALU.add, ALU.max).then_inc(block_known, 1)

            def find_edge(i, b):
                q = i * 2 + b
                dve.wait_ge(block_in[b], i * 16 + 16)
                wait(dve, counted2, q)
                nc.vector.tensor_scalar(junk2[:, :], block_of[b][:, :], nid[:, bass.ds(q, 1)], 0.0, ALU.is_le, ALU.add,
                                        accum_out=upto[:, bass.ds(q, 1)]).then_inc(counted2, 1)

            def body(i, first=False, last=False):
                for s in range(2 * G):
                    if s % G == 2:
                        if not first:
                            find_edge(i - 1, s // G)
                        if not last:
                            find_block(i, s // G)
                    if not (last and s + AHEAD >= 2 * G):
                        copy_t(i + (s + AHEAD) // (2 * G), (s + AHEAD) % (2 * G))
                    add_bias(i, s)
                    if not (first and s == 0):
                        product(i + (s - 1) // (2 * G), (s - 1) % (2 * G))
                    b, g = s // G, s % G
                    if g > 0 and not (first and b == 0):
                        c = i * 2 + b - 1
                        if g == 1:
                            carry(c, 1 - b)
                        scan(c, 1 - b, g - 1)

            nc.vector.memset(near[:, :], -1).then_inc(padded, 1)
            nc.vector.memset(dsti[96:P, LAST * T:RUN], -1).then_inc(padded, 1)
            nc.vector.memset(R["w2g2"][:, :], 0.0).then_inc(diag_zeroed, 1)
            do = Order(dve, init)
            do(nc.vector.memset(sums[1][:, :, T - 1], 0.0))
            do(nc.vector.memset(R["keep"][:, 0:1], 0.0))
            dve.wait_ge(iotas, 2)
            do(nc.vector.tensor_copy(nid[:, :], nidi[:, :]))
            do(nc.vector.tensor_copy(pid[:, :], pidi[:, :]))
            for s in range(AHEAD):
                copy_t(0, s)
            dve.wait_ge(dst_in, 16 * 6)
            nc.vector.tensor_tensor(R["keep"][:, 1:RUN], dsti[:, 1:RUN], dsti[:, 0:RUN - 1], ALU.is_equal).then_inc(keep_ready, 1)
            do(nc.vector.tensor_copy(R["first"][:, :], dsti[:, 0:1]))
            do(nc.vector.tensor_copy(nid[:, NC - 1:NC], dsti[:, 0:1]))
            do(nc.vector.tensor_tensor(R["cont"][:, :], dsti[:, 0:1], near[:, 0:1], ALU.is_equal))
            do(nc.vector.tensor_tensor(R["onward"][:, :], dsti[:, RUN - 1:RUN], near[:, 1:2], ALU.is_equal))
            do(nc.vector.tensor_tensor(R["whole"][:, :], dsti[:, 0:1], dsti[:, RUN - 1:RUN], ALU.is_equal))
            do(nc.vector.tensor_tensor(R["whole"][:, :], R["whole"][:, :], R["onward"][:, :], ALU.mult))
            dve.wait_ge(keep_ready, 1)
            dve.wait_ge(weights_in, 16 * WEIGHTS)
            body(0, first=True)
            with dve.Fori(1, HALF - 1) as i:
                body(i)
            body(HALF - 1, last=True)
            product(HALF - 1, 2 * G - 1)
            carry(CH - 1, 1)
            for k in range(PIECES):
                scan(CH - 1, 1, k)
            dve.wait_ge(scanned, CH * PIECES)
            nc.vector.tensor_copy(R["state"][:, 0:F], sums[1][:, :, T - 1]).then_inc(state_ready, 1)
            dve.wait_ge(counted2, NC)
            do = Order(dve, chain)
            do(nc.vector.tensor_scalar(blocks_upto[:, :], blocks_upto[:, :], -1.0, 0.0, ALU.add, ALU.max))
            do(nc.vector.scalar_tensor_tensor(upto[:, :], blocks_upto[:, :], float(SL), upto[:, :], ALU.mult, ALU.add))
            before, through = upto[0:NP, 0:NJ], upto[0:NP, 1:NJ + 1]
            do(nc.vector.tensor_tensor(R["pres"][:, :], through, before, ALU.is_gt))
            do(nc.vector.tensor_scalar(R["end"][:, :], through, -1.0, 0.0, ALU.add, ALU.max))
            do(nc.vector.tensor_scalar(fx[:, 2:3], pid[:, :], float(E), None, ALU.add))
            do(nc.vector.tensor_scalar(spare[:, :], nid[0:NP, 1:NJ + 1], float(P * RUN), None, ALU.add))
            do(nc.vector.tensor_tensor(R["start"][:, :], before, spare[:, :], ALU.subtract))
            do(nc.vector.tensor_tensor(R["start"][:, :], R["start"][:, :], R["pres"][:, :], ALU.mult))
            do(nc.vector.tensor_tensor(R["start"][:, :], R["start"][:, :], spare[:, :], ALU.add))
            do(nc.vector.tensor_scalar(fx[:, 0:1], upto[:, NC - 1:NC], -1.0, None, ALU.add))
            do(nc.vector.tensor_scalar(fx[:, 1:2], pid[:, :], float(RUN), float(RUN), ALU.mult, ALU.add))
            do(nc.vector.tensor_tensor(fx[:, 1:2], fx[:, 0:1], fx[:, 1:2], ALU.is_lt))
            do(nc.vector.tensor_tensor(fx[:, 1:2], fx[:, 1:2], R["cont"][:, :], ALU.mult))
            do(nc.vector.tensor_tensor(fx[:, 0:1], fx[:, 0:1], fx[:, 2:3], ALU.subtract))
            do(nc.vector.tensor_tensor(fx[:, 0:1], fx[:, 0:1], fx[:, 1:2], ALU.mult))
            do(nc.vector.tensor_tensor(R["mend"][:, :], fx[:, 0:1], fx[:, 2:3], ALU.add))

        @block.gpsimd
        def _(pool):
            def spread_keep(c, b):
                src = R["keep"][:, bass.ds(c * T + 1, T - 1)].unsqueeze(1).to_broadcast([P, F, T - 1])
                pool.sem_inc(turn, 1)
                nc.gpsimd.tensor_copy(keepf[b][:, :, 1:T], src).then_inc(keepf_ready, 1)

            def to_rows(i, b, first=False):
                c = i * 2 + b
                if not first:
                    pool.wait_ge(stored[b], i * 16)
                pool.wait_ge(scanned, (c + 1) * PIECES)
                pool.sem_inc(turn, 1)
                nc.gpsimd.tensor_copy(rows[b][:, :, :], sums[b][:, :, :].rearrange("p f t -> p t f")).then_inc(rows_ready, 1)

            def fetch_block(q, b):
                pool.wait_ge(block_known, q + 1)
                pool.sem_inc(turn, 1)
                pool.indirect_dma_start(out=block_of[b][:, :], out_offset=None, in_=A["dst"].rearrange("(a k) -> a k", k=SL),
                                        in_offset=bass.IndirectOffsetOnAxis(ap=block_id[b][:, :], axis=0)).then_inc(block_in[b], 16)

            nc.gpsimd.memset(R["ident"][:, :], 0.0).then_inc(ident_steps, 1)
            nc.gpsimd.iota(nidi[:, :], pattern=[[1, NC]], base=-1, channel_multiplier=NJ).then_inc(iotas, 1)
            nc.gpsimd.iota(pidi[:, :], pattern=[[1, 1]], base=0, channel_multiplier=1).then_inc(iotas, 1)
            pool.wait_ge(ident_steps, 1)
            nc.gpsimd.affine_select(out=R["ident"][:, :], in_=R["ident"][:, :], compare_op=ALU.not_equal, fill=1.0,
                                    base=0, pattern=[[-1, P]], channel_multiplier=1).then_inc(ident_steps, 1)
            for b in range(2):
                nc.gpsimd.memset(keepf[b][:, :, 0:1], 0.0).then_inc(keepf_zeroed, 1)
            pool.wait_ge(keep_ready, 1)
            spread_keep(0, 0)
            spread_keep(1, 1)
            for b in range(2):
                fetch_block(b, b)
                to_rows(0, b, first=True)
                spread_keep(2 + b, b)
            with pool.Fori(1, HALF - 1) as i:
                for b in range(2):
                    fetch_block(i * 2 + b, b)
                    to_rows(i, b)
                    spread_keep(i * 2 + b + 2, b)
            to_rows(HALF - 1, 0)
            pool.wait_ge(stored[1], (HALF - 1) * 16)
            pool.wait_ge(scanned, CH * PIECES)
            nc.gpsimd.tensor_copy(rows[1][:, 0:SHARE, :], sums[1][:, :, 0:SHARE].rearrange("p f t -> p t f")).then_inc(last_rows, 1)


def update_nodes(nc, R, A, D):
    with ExitStack() as ctx:
        def sb(name, shape, dt=f32):
            return ctx.enter_context(nc.sbuf_tensor(name, shape, dt))

        def ps(name, shape):
            return ctx.enter_context(nc.psum_tensor(name, shape, f32))

        def sem(name):
            return ctx.enter_context(nc.semaphore(name))

        onw = sb("onw", [P, F])
        whl = sb("whl", [P, F])
        whl_t = sb("whl_t", [F, P])
        cin_t = sb("cin_t", [F, P + 1])
        got = sb("got", [P, F])
        half = sb("half", [NP, NJ])
        ends = [sb(f"ends{b}", [NP, JB], i32) for b in range(2)]
        starts = [sb(f"starts{b}", [NP, JB], i32) for b in range(2)]
        x = [sb(f"x_tile{b}", [NP, JB, F]) for b in range(2)]
        agg = [sb(f"agg{b}", [NP, JB, F]) for b in range(2)]
        xc = sb("xc", [NP, JB, F])
        sq = sb("sq", [NP, JB, F])
        st = sb("st", [NP, JB])
        std = sb("std", [NP, JB])
        epst = sb("epst", [NP, 1])
        hh = sb("hh", [NP, JB, F])
        hT = sb("hT", [F, JB, NP])
        sr = [sb(f"sr{b}", [NP, JB, 2 * F]) for b in range(2)]
        onw_bank, whl_bank = ps("onw_bank", [P, 512]), ps("whl_bank", [P, 512])
        onw_ps, whl_ps, back_ps = onw_bank[0:F, 0:P], whl_bank[0:F, 0:P], onw_bank[:, 0:F]
        hT_ps = ps("hT_ps", [F, 3, 512])
        pr_ps = ps("pr_ps", [NP, 3, 512])

        chain = sem("chain")
        scaled = sem("scaled")
        turned = sem("turned")
        cin_ready = sem("cin_ready")
        cin_back = sem("cin_back")
        got_in = sem("got_in")
        mended = sem("mended")
        mended_out = sem("mended_out")
        padded = sem("padded")
        src_in = sem("src_in")
        x_in = [sem(f"x_in{b}") for b in range(2)]
        base_ready = sem("base_ready")
        staged = sem("staged")
        turn = sem("turn")
        gathered = [sem(f"gathered{b}") for b in range(2)]
        var_x = sem("var_x")
        std_x = sem("std_x")
        var_h = sem("var_h")
        std_h = sem("std_h")
        h_ready = sem("h_ready")
        hT_in_ps = sem("hT_in_ps")
        hT_part = sem("hT_part")
        hT_ready = sem("hT_ready")
        pr_in_ps = sem("pr_in_ps")
        sr_ready = sem("sr_ready")
        tabled = [sem(f"tabled{b}") for b in range(2)]
        scattered = [sem(f"scattered{b}") for b in range(2)]
        block = ctx.enter_context(nc.Block())
        sums_d = D["sums"]
        edge_rows = sums_d[0:P * RUN, :]
        x_v = A["x"].rearrange("(p j) f -> p j f", p=NP)
        s_tab = D["s_proj"].rearrange("(p j) f -> p j f", p=NP)
        r_tab = D["r_proj"].rearrange("(p j) f -> p j f", p=NP)
        HALF = NS // 2

        @block.sync
        def _(sp):
            def load_x(k, b):
                sp.dma_start(x[b][:, :, :], x_v[:, bass.ds(k * JB, JB), :]).then_inc(x_in[b], 16)

            def tables(i, more=True):
                for b in range(2):
                    k = i * 2 + b
                    sp.wait_ge(sr_ready, k + 1)
                    if more:
                        load_x(k + 4, b)
                    sp.dma_start(s_tab[:, bass.ds(k * JB, JB), :], sr[b][:, :, 0:F]).then_inc(tabled[b], 16)
                    sp.dma_start(r_tab[:, bass.ds(k * JB, JB), :], sr[b][:, :, F:2 * F]).then_inc(tabled[b], 16)

            load_x(0, 0)
            load_x(1, 1)
            sp.wait_ge(padded, 1)
            src = A["src"][0:(P - 1) * RUN].rearrange("(p k) -> p k", k=RUN)
            sp.dma_start(R["src"][0:112, :], src[0:112, :]).then_inc(src_in, 16)
            sp.dma_start(R["src"][112:P - 1, :], src[112:P - 1, :]).then_inc(src_in, 16)
            sp.dma_start(R["src"][P - 1:P, 0:LAST * T], A["src"][(P - 1) * RUN:E].rearrange("(a k) -> a k", a=1)).then_inc(src_in, 16)
            for b in range(2):
                sp.wait_ge(base_ready, b + 1)
                load_x(2 + b, b)
            with sp.Fori(0, HALF - 2) as i:
                tables(i)
            tables(HALF - 2, more=False)
            tables(HALF - 1, more=False)
            sp.wait_ge(src_in, 48)
            for b in range(2):
                sp.wait_ge(tabled[b], 32 * HALF)

        @block.gpsimd
        def _(pool):
            at = lambda ap: bass.IndirectOffsetOnAxis(ap=ap, axis=0)
            pool.indirect_dma_start(out=got[:, :], out_offset=None, in_=edge_rows, in_offset=at(R["mend"][:, :])).then_inc(got_in, 16)
            pool.wait_ge(mended, 1)
            pool.indirect_dma_start(out=sums_d, out_offset=at(R["mend"][:, :]), in_=got[:, :], in_offset=None).then_inc(mended_out, 16)
            pool.wait_ge(mended_out, 16)

            def gather(k, b):
                pool.wait_ge(staged, k + 1)
                pool.sem_inc(turn, 1)
                for m in range(JB):
                    pool.indirect_dma_start(out=agg[b][:, m, :], out_offset=None, in_=edge_rows, in_offset=at(ends[b][:, m:m + 1])).then_inc(gathered[b], 16)

            def scatter(k, b):
                pool.wait_ge(sr_ready, k + 1)
                pool.sem_inc(turn, 1)
                for m in range(JB):
                    pool.indirect_dma_start(out=sums_d, out_offset=at(starts[b][:, m:m + 1]), in_=sr[b][:, m, F:2 * F], in_offset=None)\
                        .then_inc(scattered[b], 16)

            for k in range(3):
                gather(k, k % 2)
            with pool.Fori(0, HALF - 2) as i:
                for b in range(2):
                    scatter(i * 2 + b, b)
                    gather(i * 2 + b + 3, 1 - b)
            scatter(NS - 4, 0)
            gather(NS - 1, 1)
            for k in range(NS - 3, NS):
                scatter(k, k % 2)
            for b in range(2):
                pool.wait_ge(scattered[b], 16 * JB * HALF)

        @block.tensor
        def _(pe):
            pe.wait_ge(scaled, 2)
            nc.tensor.transpose(onw_ps, onw[:, :], R["ident"][:, :])
            nc.tensor.transpose(whl_ps, whl[:, :], R["ident"][:, :]).then_inc(turned, 1)
            pe.wait_ge(cin_ready, 1)
            nc.tensor.transpose(back_ps, cin_t[:, 0:P], R["ident"][0:F, 0:F]).then_inc(cin_back, 1)

            def step(k):
                pe.wait_ge(h_ready, k + 1)
                pe.sem_inc(turn, 1)
                for j in range(JB):
                    last = nc.tensor.transpose(hT_ps[:, j // 4, (j % 4) * NP:(j % 4 + 1) * NP], hh[:, j, :], R["ident"][0:NP, 0:NP])
                last.then_inc(hT_in_ps, 1)
                pe.wait_ge(hT_ready, k + 1)
                wait(pe, sr_ready, k)
                for j in range(JB):
                    last = nc.tensor.matmul(pr_ps[:, j // 4, (j % 4) * P:(j % 4 + 1) * P], hT[:, j, :], R["wsr"][:, :], start=True, stop=True)
                last.then_inc(pr_in_ps, 1)

            step(0)
            with pe.Fori(1, NS) as k:
                step(k)

        @block.scalar
        def _(act):
            def root(var_ready, std_ready, n):
                act.wait_ge(var_ready, n + 1)
                nc.scalar.activation(std[:, :], st[:, :], ACT.Sqrt, bias=epst[:, :], scale=1.0 / F).then_inc(std_ready, 1)

            def step(k, more=True):
                root(var_h, std_h, k)
                if more:
                    root(var_x, std_x, k + 2)
                act.wait_ge(hT_in_ps, k + 1)
                for q, w in enumerate((4, 4, 2)):
                    nc.scalar.activation(hT[:, 4 * q:4 * q + w, :], hT_ps[:, q, 0:w * NP].rearrange("f (j n) -> f j n", n=NP), ACT.Copy)\
                        .then_inc(hT_part, 1)
                act.wait_ge(hT_part, k * 3 + 3)
                act.sem_inc(hT_ready, 1)

            act.wait_ge(scaled, 2)
            for k in range(2):
                root(var_x, std_x, k)
            with act.Fori(0, NS - 2) as k:
                step(k)
            for k in range(NS - 2, NS):
                step(k, more=False)

        @block.vector
        def _(dve):
            do = Order(dve, chain)
            wide = [NP, JB, F]
            do(nc.vector.memset(epst[:, :], EPS))
            nc.vector.tensor_scalar(onw[:, :], R["state"][:, 0:F], R["onward"][:, :], None, ALU.mult).then_inc(scaled, 1)
            nc.vector.tensor_copy(whl[:, :], R["whole"][:, :].to_broadcast([P, F])).then_inc(scaled, 1)
            do(nc.vector.memset(cin_t[:, 0:1], 0.0))
            dve.wait_ge(turned, 1)
            do(nc.vector.tensor_copy(whl_t[:, :], whl_ps))
            nc.vector.tensor_tensor_scan(cin_t[:, 1:P + 1], whl_t[:, :], onw_ps, 0.0, ALU.mult, ALU.add).then_inc(cin_ready, 1)
            nc.vector.memset(R["src"][96:P, LAST * T:RUN], 0).then_inc(padded, 1)
            dve.wait_ge(cin_back, 1)
            dve.wait_ge(got_in, 16)
            nc.vector.tensor_tensor(got[:, :], got[:, :], back_ps, ALU.add).then_inc(mended, 1)

            def stage(k, b):
                nc.vector.tensor_copy(ends[b][:, :], R["end"][:, bass.ds(k * JB, JB)]).then_inc(staged, 1)

            def normalize(do, src, var_ready, std_ready, n):
                do(nc.vector.tensor_reduce(st[:, :], src, AX, ALU.add))
                do(nc.vector.tensor_scalar(st[:, :], st[:, :], 1.0 / F, None, ALU.mult))
                do(nc.vector.tensor_tensor(xc[:, :, :], src, st[:, :].unsqueeze(2).to_broadcast(wide), ALU.subtract))
                do(nc.vector.tensor_tensor(sq[:, :, :], xc[:, :, :], xc[:, :, :], ALU.mult))
                nc.vector.tensor_reduce(st[:, :], sq[:, :, :], AX, ALU.add).then_inc(var_ready, 1)
                dve.wait_ge(std_ready, n + 1)
                do(nc.vector.reciprocal(st[:, :], std[:, :]))
                do(nc.vector.tensor_tensor(xc[:, :, :], xc[:, :, :], st[:, :].unsqueeze(2).to_broadcast(wide), ALU.mult))

            def first_part(do, i, b):
                dve.wait_ge(x_in[b], i * 16 + 16)
                normalize(do, x[b][:, :, :], var_x, std_x, i * 2 + b)
                do(nc.vector.scalar_tensor_tensor(R["base"][:, bass.ds((i * 2 + b) * JB, JB), :], xc[:, :, :], 0.0, x[b][:, :, :],
                                                  ALU.max, ALU.add))
                dve.sem_inc(base_ready, 1)

            def step(i, b, count, first=False, last=False):
                k = i * 2 + b
                do = Order(dve, chain, count)
                cols = bass.ds(k * JB, JB)
                base = R["base"][:, cols, :]
                dve.wait_ge(gathered[b], i * 16 * JB + 16 * JB)
                do(nc.vector.tensor_tensor(agg[b][:, :, :], agg[b][:, :, :], half[:, cols].unsqueeze(2).to_broadcast(wide), ALU.mult))
                do(nc.vector.tensor_tensor(base, base, agg[b][:, :, :], ALU.add))
                if not last:
                    stage(k + 2, b)
                normalize(do, base, var_h, std_h, k)
                nc.vector.tensor_scalar(hh[:, :, :], xc[:, :, :], 0.0, None, ALU.max).then_inc(h_ready, 1)
                if not last:
                    dve.wait_ge(h_ready, k + 1)
                    first_part(do, i + 1, b)
                if not first:
                    dve.wait_ge(scattered[b], i * 16 * JB)
                    dve.wait_ge(tabled[b], i * 32)
                do(nc.vector.tensor_copy(starts[b][:, :], R["start"][:, cols]))
                dve.wait_ge(pr_in_ps, k + 1)
                for q, w in enumerate((4, 4, 2)):
                    do(nc.vector.tensor_tensor(sr[b][:, 4 * q:4 * q + w, :], pr_ps[:, q, 0:w * P].rearrange("n (j c) -> n j c", c=P),
                                               R["bsr"][0:NP, :].unsqueeze(1).to_broadcast([NP, w, 2 * F]), ALU.add))
                dve.sem_inc(sr_ready, 1)
                assert do.n == (12 if last else STEP), do.n

            STEP = 19
            do(nc.vector.tensor_scalar(half[:, :], R["pres"][:, :], 0.5, None, ALU.mult))
            stage(0, 0)
            stage(1, 1)
            for b in range(2):
                first_part(do, 0, b)
            done = do.n
            for b in range(2):
                step(0, b, done + b * STEP, first=True)
            with dve.Fori(1, HALF - 1) as i:
                for b in range(2):
                    step(i, b, i * (2 * STEP) + (done + b * STEP))
            for b in range(2):
                step(HALF - 1, b, done + (NS - 2) * STEP + 12 * b, last=True)


def attention(nc, R, A, D):
    with ExitStack() as ctx:
        def sb(name, shape, dt=f32):
            return ctx.enter_context(nc.sbuf_tensor(name, shape, dt))

        def sem(name):
            return ctx.enter_context(nc.semaphore(name))

        U = 4
        idx = [sb(f"idx{u}", [P, T], i32) for u in range(U)]
        se = [sb(f"se{u}", [P, T, F]) for u in range(U)]
        rs = [sb(f"rs{b}", [P, T, F]) for b in range(2)]
        keepf = [sb(f"akeepf{b}", [P, F, T]) for b in range(2)]
        rnew = sb("rnew", [P, F, T])
        rneg = sb("rneg", [P, F, T])
        z = [sb(f"z{b}", [P, F, T]) for b in range(2)]
        t1 = sb("t1", [P, F, T])
        t2 = sb("t2", [P, F, T])
        decf = sb("decf", [P, F, T])
        wse = sb("wse", [P, F, T])
        num = sb("num", [P, F, T])
        lg = sb("lg", [P, H, T])
        kneg = sb("kneg", [P, T])
        mx = sb("mx", [P, H, T + 1])
        den = sb("den", [P, H, T + 1])
        exin = sb("exin", [P, 2, H, T])
        ex = sb("ex", [P, 2, H, T])
        dec = sb("dec", [P, H, T])
        tmp = sb("tmp", [P, F])
        heads = sb("heads", [P, F])
        rows = [sb(f"arows{b}", [P, T, ROW]) for b in range(2)]

        heads_in = sem("heads_in")
        heads_out = sem("heads_out")
        inited = sem("inited")
        idx_ready = sem("idx_ready")
        turn = sem("turn")
        gathered = [sem(f"agathered{u}") for u in range(U)]
        rs_in = [sem(f"rs_in{b}") for b in range(2)]
        rnew_ready = sem("rnew_ready")
        chain = sem("chain")
        keepf_ready = sem("keepf_ready")
        carried = sem("carried")
        held = sem("held")
        z_ready = sem("z_ready")
        expz_ready = sem("expz_ready")
        bounded = sem("bounded")
        softplus_ready = sem("softplus_ready")
        tanh_ready = sem("tanh_ready")
        exin_ready = sem("exin_ready")
        ex_ready = sem("ex_ready")
        dec_ready = sem("dec_ready")
        decf_ready = sem("decf_ready")
        se_used = sem("se_used")
        summed = sem("summed")
        rows_ready = sem("rows_ready")
        stored = [sem(f"astored{b}") for b in range(2)]
        block = ctx.enter_context(nc.Block())
        NI = CH // U
        rs_d = D["sums"][0:P * RUN, :].rearrange("(p c k) f -> p c (k f)", p=P, c=CH)
        st_d = D["states"][0:P * RUN, :].rearrange("(p c k) f -> p c (k f)", p=P, c=CH)

        @block.sync
        def _(sp):
            def load(c, b):
                sp.dma_start(rs[b][:, :, :].rearrange("p k f -> p (k f)").unsqueeze(1), rs_d[:, bass.ds(c, 1), :]).then_inc(rs_in[b], 16)

            def store(c, b):
                sp.wait_ge(rows_ready, (c + 1) * 3)
                sp.dma_start(st_d[:, bass.ds(c, 1), :], rows[b][:, :, :].rearrange("p k f -> p (k f)").unsqueeze(1)).then_inc(stored[b], 16)

            def body(i, first=False, last=False):
                for u in range(U):
                    c = i * U + u
                    if not (last and u + 2 >= U):
                        sp.wait_ge(rnew_ready, c + 1)
                        load(c + 2, u % 2)
                    if not (first and u == 0):
                        store(c - 1, 1 - u % 2)

            sp.wait_ge(heads_in, 16)
            sp.dma_start(D["sums"][0:P * RUN, :].rearrange("(p k) f -> p k f", p=P)[:, 0:1, :], heads[:, :].unsqueeze(1)).then_inc(heads_out, 16)
            load(1, 1)
            sp.wait_ge(heads_out, 16)
            load(0, 0)
            body(0, first=True)
            with sp.Fori(1, NI - 1) as i:
                body(i)
            body(NI - 1, last=True)
            store(CH - 1, 1)
            for b in range(2):
                sp.wait_ge(stored[b], 16 * CH // 2)

        @block.gpsimd
        def _(pool):
            def gather(i, u, first=False):
                c = i * U + u
                if not first:
                    pool.wait_ge(se_used, c - U + 1)
                    pool.wait_ge(idx_ready, c - U + 1)
                    pool.sem_inc(turn, 1)
                node = R["src"][:, u * T:(u + 1) * T] if first else idx[u][:, :]
                for k in range(T):
                    pool.indirect_dma_start(out=se[u][:, k, :], out_offset=None, in_=D["s_proj"],
                                            in_offset=bass.IndirectOffsetOnAxis(ap=node[:, k:k + 1], axis=0)).then_inc(gathered[u], 16)

            pool.indirect_dma_start(out=heads[:, :], out_offset=None, in_=D["r_proj"],
                                    in_offset=bass.IndirectOffsetOnAxis(ap=R["first"][:, :], axis=0)).then_inc(heads_in, 16)
            for u in range(U):
                gather(0, u, first=True)
            with pool.Fori(1, NI) as i:
                for u in range(U):
                    gather(i, u)
            for u in range(U):
                pool.wait_ge(gathered[u], 16 * T * NI)

        @block.scalar
        def _(act):
            def spread(c, b):
                src = R["keep"][:, bass.ds(c * T + 1, T - 1)].unsqueeze(1).to_broadcast([P, F, T - 1])
                nc.scalar.activation(keepf[b][:, :, 1:T], src, ACT.Copy).then_inc(keepf_ready, 1)

            def index(c, u):
                nc.scalar.activation(idx[u][:, :], R["src"][:, bass.ds(c * T, T)], ACT.Copy).then_inc(idx_ready, 1)

            def body(i, first=False, last=False):
                for u in range(U):
                    b = u % 2
                    c = i * U + u
                    act.wait_ge(z_ready, c + 1)
                    nc.scalar.activation(t1[:, :, :], z[b][:, :, :], ACT.Exp).then_inc(expz_ready, 1)
                    act.wait_ge(bounded, c + 1)
                    nc.scalar.activation(t1[:, :, :], t1[:, :, :], ACT.Ln, bias=1.0).then_inc(softplus_ready, 1)
                    act.wait_ge(softplus_ready, c + 1)
                    nc.scalar.activation(t2[:, :, :], t1[:, :, :], ACT.Tanh).then_inc(tanh_ready, 1)
                    if not (last and u + 2 >= U):
                        wait(act, held, c + 1)
                        spread(c + 2, b)
                    if not last:
                        act.wait_ge(gathered[u], i * 16 * T + 16 * T)
                        index(c + U, u)
                    act.wait_ge(exin_ready, c + 1)
                    nc.scalar.activation(ex[:, :, :, :], exin[:, :, :, :], ACT.Exp).then_inc(ex_ready, 1)
                    act.wait_ge(dec_ready, c + 1)
                    nc.scalar.activation(decf[:, :, 1:T].rearrange("p (h d) t -> p h d t", h=H),
                                         dec[:, :, 1:T].unsqueeze(2).to_broadcast([P, H, HD, T - 1]), ACT.Copy).then_inc(decf_ready, 1)
                    act.wait_ge(summed, (c + 1) * 2)
                    if not (first and u < 2):
                        act.wait_ge(stored[b], (i * (U // 2) + u // 2) * 16)
                    nc.scalar.activation(rows[b][:, :, 0:F], num[:, :, :].rearrange("p f t -> p t f"), ACT.Copy).then_inc(rows_ready, 1)
                    nc.scalar.activation(rows[b][:, :, F:F + H], den[:, :, 1:T + 1].rearrange("p h t -> p t h"), ACT.Copy).then_inc(rows_ready, 1)
                    nc.scalar.activation(rows[b][:, :, F + H:ROW], mx[:, :, 1:T + 1].rearrange("p h t -> p t h"), ACT.Copy).then_inc(rows_ready, 1)

            act.wait_ge(inited, 7)
            for b in range(2):
                spread(b, b)
            body(0, first=True)
            with act.Fori(1, NI - 1) as i:
                body(i)
            body(NI - 1, last=True)

        @block.vector
        def _(dve):
            flat = lambda x: x.rearrange("p f t -> p (f t)")
            STEP = 19

            def receivers(i, u):
                i, u = i + u // U, u % U
                c, b = i * U + u, u % 2
                kp = R["keep"][:, bass.ds(c * T, T)].unsqueeze(1).to_broadcast([P, F, T])
                dve.wait_ge(rs_in[b], (i * (U // 2) + u // 2) * 16 + 16)
                nc.vector.scalar_tensor_tensor(rnew[:, :, :], kp, 1.0, rs[b][:, :, :].rearrange("p k f -> p f k"),
                                               ALU.subtract, ALU.mult).then_inc(rnew_ready, 1)
                dve.wait_ge(rnew_ready, c + 1)
                wait(dve, held, c)
                nc.vector.scalar_tensor_tensor(rnew[:, :, 0], rneg[:, :, T - 1], R["keep"][:, bass.ds(c * T, 1)], rnew[:, :, 0],
                                               ALU.mult, ALU.add).then_inc(carried, 1)
                dve.wait_ge(carried, c + 1)
                dve.wait_ge(keepf_ready, c + 1)
                nc.vector.tensor_tensor_scan(flat(rneg[:, :, :]), flat(keepf[b][:, :, :]), flat(rnew[:, :, :]), 0.0, ALU.mult, ALU.add)\
                    .then_inc(held, 1)

            def edge_inputs(i, u):
                i, u = i + u // U, u % U
                c, b = i * U + u, u % 2
                dve.wait_ge(held, c + 1)
                dve.wait_ge(gathered[u], i * 16 * T + 16 * T)
                nc.vector.tensor_tensor(z[b][:, :, :], se[u][:, :, :].rearrange("p k f -> p f k"), rneg[:, :, :], ALU.subtract)\
                    .then_inc(z_ready, 1)

            def body(i, last=False):
                for u in range(U):
                    c, b = i * U + u, u % 2
                    do = Order(dve, chain, c * STEP)
                    dve.wait_ge(expz_ready, c + 1)
                    nc.vector.tensor_scalar(t1[:, :, :], t1[:, :, :], 2.0 ** 60, None, ALU.min).then_inc(bounded, 1)
                    more = not (last and u + 1 >= U)
                    if more:
                        receivers(i, u + 1)
                        if not last:
                            edge_inputs(i, u + 1)
                    kp = R["keep"][:, bass.ds(c * T, T)]
                    do(nc.vector.tensor_scalar(kneg[:, :], kp, -1.0, BIG, ALU.add, ALU.mult))
                    dve.wait_ge(tanh_ready, c + 1)
                    do(nc.vector.tensor_tensor(t2[:, :, :], z[b][:, :, :], t2[:, :, :], ALU.mult))
                    do(nc.vector.tensor_tensor(t2[:, :, :], t2[:, :, :], R["aw"][:, :].unsqueeze(2).to_broadcast([P, F, T]), ALU.mult))
                    do(nc.vector.tensor_reduce(lg[:, :, :], t2[:, :, :].rearrange("p (h d) t -> p h t d", h=H), AX, ALU.add))
                    do(nc.vector.tensor_scalar(lg[:, :, :], lg[:, :, :], R["ab"][:, :], None, ALU.add))
                    wait(dve, rows_ready, c * 3)
                    for h in range(H):
                        do(nc.vector.tensor_tensor_scan(mx[:, h, 1:T + 1], kneg[:, :], lg[:, h, :], mx[:, h, 0:1], ALU.add, ALU.max))
                    do(nc.vector.tensor_tensor(exin[:, 0, :, :], mx[:, :, 0:T], mx[:, :, 1:T + 1], ALU.subtract))
                    do(nc.vector.tensor_scalar(exin[:, 0, :, :], exin[:, 0, :, :], 0.0, None, ALU.min))
                    nc.vector.tensor_tensor(exin[:, 1, :, :], lg[:, :, :], mx[:, :, 1:T + 1], ALU.subtract).then_inc(exin_ready, 1)
                    do(nc.vector.tensor_copy(mx[:, :, 0], mx[:, :, T]))
                    dve.wait_ge(ex_ready, c + 1)
                    nc.vector.tensor_tensor(dec[:, :, :], ex[:, 0, :, :], kp.unsqueeze(1).to_broadcast([P, H, T]), ALU.mult).then_inc(dec_ready, 1)
                    nc.vector.tensor_tensor(wse[:, :, :].rearrange("p (h d) t -> p h d t", h=H),
                                            se[u][:, :, :].rearrange("p k (h d) -> p h d k", h=H),
                                            ex[:, 1, :, :].unsqueeze(2).to_broadcast([P, H, HD, T]), ALU.mult).then_inc(se_used, 1)
                    dve.wait_ge(dec_ready, c + 1)
                    for h in range(H):
                        do(nc.vector.tensor_tensor_scan(den[:, h, 1:T + 1], dec[:, h, :], ex[:, 1, h, :], den[:, h, 0:1], ALU.mult, ALU.add))
                    do(nc.vector.tensor_copy(den[:, :, 0], den[:, :, T]))
                    do(nc.vector.tensor_tensor(tmp[:, :].rearrange("p (h d) -> p h d", h=H), num[:, :, T - 1].rearrange("p (h d) -> p h d", h=H),
                                               dec[:, :, 0:1].to_broadcast([P, H, HD]), ALU.mult))
                    dve.wait_ge(se_used, c + 1)
                    do(nc.vector.tensor_tensor(wse[:, :, 0], wse[:, :, 0], tmp[:, :], ALU.add))
                    dve.wait_ge(decf_ready, c + 1)
                    nc.vector.tensor_tensor_scan(flat(num[:, :, :]), flat(decf[:, :, :]), flat(wse[:, :, :]), 0.0, ALU.mult, ALU.add)\
                        .then_inc(summed, 1)
                    dve.wait_ge(summed, c * 2 + 1)
                    dve.sem_inc(summed, 1)
                    assert do.n == STEP, do.n
                    if more and last:
                        edge_inputs(i, u + 1)

            for tile, value in ((keepf[0], 0.0), (keepf[1], 0.0), (decf, 0.0), (rneg, 0.0), (num, 0.0), (mx, -BIG), (den, 0.0)):
                nc.vector.memset(tile[:, :, :], value).then_inc(inited, 1)
            dve.wait_ge(inited, 7)
            receivers(0, 0)
            edge_inputs(0, 0)
            body(0)
            with dve.Fori(1, NI - 1) as i:
                body(i)
            body(NI - 1, last=True)
            nc.vector.tensor_copy(R["state"][:, 0:F], num[:, :, T - 1]).then_inc(inited, 1)
            nc.vector.tensor_copy(R["state"][:, F:F + H], den[:, :, T]).then_inc(inited, 1)
            nc.vector.tensor_copy(R["state"][:, F + H:ROW], mx[:, :, T]).then_inc(inited, 1)


def finish(nc, R, A, D, out, ABW=F + H):
    with ExitStack() as ctx:
        def sb(name, shape, dt=f32):
            return ctx.enter_context(nc.sbuf_tensor(name, shape, dt))

        def ps(name, shape):
            return ctx.enter_context(nc.psum_tensor(name, shape, f32))

        def sem(name):
            return ctx.enter_context(nc.semaphore(name))

        drop = sb("drop", [P, H])
        drop_t = sb("drop_t", [H, P])
        mx_t = sb("mx_t", [H, P + 1])
        mio = sb("mio", [P, 2, H])
        e = sb("e", [P, 2, H])
        add = sb("add", [P, ABW])
        mul = sb("mul", [P, ABW])
        mul_t = sb("mul_t", [ABW, P])
        cin_t = sb("fcin_t", [ABW, P + 1])
        cin = sb("cin", [P, ABW])
        got = sb("fgot", [P, ROW])
        mt = sb("mt", [P, H])
        ends = [sb(f"fends{b}", [NP, JB], i32) for b in range(2)]
        q = [sb(f"q{b}", [NP, JB, ROW]) for b in range(2)]
        inv = sb("inv", [NP, JB, H])
        res = [sb(f"res{b}", [NP, JB, F]) for b in range(2)]
        a_ps, b_ps = ps("a_ps", [P, 512]), ps("b_ps", [P, 512])

        chain = sem("chain")
        pe_do = [sem(f"pe_do{k}") for k in range(4)]
        pe_did = [sem(f"pe_did{k}") for k in range(4)]
        act_do = [sem(f"act_do{k}") for k in range(2)]
        act_did = [sem(f"act_did{k}") for k in range(2)]
        got_in = sem("got_in")
        mended = sem("mended")
        mended_out = sem("mended_out")
        staged = sem("staged")
        turn = sem("turn")
        gathered = [sem(f"fgathered{b}") for b in range(2)]
        res_ready = sem("res_ready")
        out_done = [sem(f"out_done{b}") for b in range(2)]
        block = ctx.enter_context(nc.Block())
        out_v = out.rearrange("(p j) f -> p j f", p=NP)

        @block.sync
        def _(sp):
            with sp.Fori(0, NS // 2) as i:
                for b in range(2):
                    sp.wait_ge(res_ready, i * 2 + b + 1)
                    sp.dma_start(out_v[:, bass.ds((i * 2 + b) * JB, JB), :], res[b][:, :, :]).then_inc(out_done[b], 16)
            for b in range(2):
                sp.wait_ge(out_done[b], 16 * NS // 2)

        @block.gpsimd
        def _(pool):
            at = lambda ap: bass.IndirectOffsetOnAxis(ap=ap, axis=0)
            pool.indirect_dma_start(out=got[:, :], out_offset=None, in_=D["states"], in_offset=at(R["mend"][:, :])).then_inc(got_in, 16)
            pool.wait_ge(mended, 1)
            pool.indirect_dma_start(out=D["states"], out_offset=at(R["mend"][:, :]), in_=got[:, :], in_offset=None).then_inc(mended_out, 16)
            pool.wait_ge(mended_out, 16)
            with pool.Fori(0, NS // 2) as i:
                for b in range(2):
                    pool.wait_ge(staged, i * 2 + b + 1)
                    pool.sem_inc(turn, 1)
                    for m in range(JB):
                        pool.indirect_dma_start(out=q[b][:, m, :], out_offset=None, in_=D["states"], in_offset=at(ends[b][:, m:m + 1]))\
                            .then_inc(gathered[b], 16)

        @block.tensor
        def _(pe):
            ident = R["ident"]
            pe.wait_ge(pe_do[0], 1)
            nc.tensor.transpose(a_ps[0:H, 0:P], R["state"][:, F + H:ROW], ident[:, :])
            nc.tensor.transpose(b_ps[0:H, 0:P], drop[:, :], ident[:, :]).then_inc(pe_did[0], 1)
            pe.wait_ge(pe_do[1], 1)
            nc.tensor.transpose(a_ps[:, 0:H], mx_t[:, 0:P], ident[0:H, 0:H])
            nc.tensor.transpose(b_ps[:, 0:H], mx_t[:, 1:P + 1], ident[0:H, 0:H]).then_inc(pe_did[1], 1)
            pe.wait_ge(pe_do[2], 1)
            nc.tensor.transpose(a_ps[0:ABW, 0:P], add[:, :], ident[:, :])
            nc.tensor.transpose(b_ps[0:ABW, 0:P], mul[:, :], ident[:, :]).then_inc(pe_did[2], 1)
            pe.wait_ge(pe_do[3], 1)
            nc.tensor.transpose(a_ps[:, 0:ABW], cin_t[:, 0:P], ident[0:ABW, 0:ABW]).then_inc(pe_did[3], 1)

        @block.scalar
        def _(act):
            for k in range(2):
                act.wait_ge(act_do[k], 1)
                nc.scalar.activation(e[:, :, :], e[:, :, :], ACT.Exp).then_inc(act_did[k], 1)

        @block.vector
        def _(dve):
            do = Order(dve, chain)

            def heads_wide(x):
                return x.unsqueeze(2).to_broadcast([P, H, HD])

            def by_head(x):
                return x.rearrange("p (h d) -> p h d", h=H)

            do(nc.vector.memset(mx_t[:, 0:1], -BIG))
            do(nc.vector.memset(cin_t[:, 0:1], 0.0))
            nc.vector.tensor_scalar(drop[:, :], R["whole"][:, :].to_broadcast([P, H]), -1.0, BIG, ALU.add, ALU.mult).then_inc(pe_do[0], 1)
            dve.wait_ge(pe_did[0], 1)
            do(nc.vector.tensor_copy(drop_t[:, :], b_ps[0:H, 0:P]))
            nc.vector.tensor_tensor_scan(mx_t[:, 1:P + 1], drop_t[:, :], a_ps[0:H, 0:P], -BIG, ALU.add, ALU.max).then_inc(pe_do[1], 1)
            dve.wait_ge(pe_did[1], 1)
            do(nc.vector.tensor_copy(mio[:, 0, :], a_ps[:, 0:H]))
            do(nc.vector.tensor_copy(mio[:, 1, :], b_ps[:, 0:H]))
            do(nc.vector.tensor_tensor(e[:, 0, :], mio[:, 0, :], mio[:, 1, :], ALU.subtract))
            do(nc.vector.tensor_scalar(e[:, 0, :], e[:, 0, :], 0.0, None, ALU.min))
            nc.vector.tensor_tensor(e[:, 1, :], R["state"][:, F + H:ROW], mio[:, 1, :], ALU.subtract).then_inc(act_do[0], 1)
            dve.wait_ge(act_did[0], 1)
            do(nc.vector.tensor_scalar(e[:, 0, :], e[:, 0, :], R["whole"][:, :], None, ALU.mult))
            do(nc.vector.tensor_scalar(e[:, 1, :], e[:, 1, :], R["onward"][:, :], None, ALU.mult))
            do(nc.vector.tensor_copy(by_head(mul[:, 0:F]), heads_wide(e[:, 0, :])))
            do(nc.vector.tensor_copy(mul[:, F:ABW], e[:, 0, :]))
            do(nc.vector.tensor_tensor(by_head(add[:, 0:F]), by_head(R["state"][:, 0:F]), heads_wide(e[:, 1, :]), ALU.mult))
            nc.vector.tensor_tensor(add[:, F:ABW], R["state"][:, F:F + H], e[:, 1, :], ALU.mult).then_inc(pe_do[2], 1)
            dve.wait_ge(pe_did[2], 1)
            do(nc.vector.tensor_copy(mul_t[:, :], b_ps[0:ABW, 0:P]))
            nc.vector.tensor_tensor_scan(cin_t[:, 1:P + 1], mul_t[:, :], a_ps[0:ABW, 0:P], 0.0, ALU.mult, ALU.add).then_inc(pe_do[3], 1)
            dve.wait_ge(pe_did[3], 1)
            do(nc.vector.tensor_copy(cin[:, :], a_ps[:, 0:ABW]))
            dve.wait_ge(got_in, 16)
            do(nc.vector.tensor_tensor(mt[:, :], got[:, F + H:ROW], mio[:, 0, :], ALU.max))
            do(nc.vector.tensor_tensor(e[:, 0, :], got[:, F + H:ROW], mt[:, :], ALU.subtract))
            nc.vector.tensor_tensor(e[:, 1, :], mio[:, 0, :], mt[:, :], ALU.subtract).then_inc(act_do[1], 1)
            dve.wait_ge(act_did[1], 1)
            do(nc.vector.tensor_scalar(e[:, 1, :], e[:, 1, :], R["cont"][:, :], None, ALU.mult))
            do(nc.vector.tensor_tensor(by_head(got[:, 0:F]), by_head(got[:, 0:F]), heads_wide(e[:, 0, :]), ALU.mult))
            do(nc.vector.tensor_tensor(got[:, F:ABW], got[:, F:ABW], e[:, 0, :], ALU.mult))
            do(nc.vector.tensor_tensor(by_head(cin[:, 0:F]), by_head(cin[:, 0:F]), heads_wide(e[:, 1, :]), ALU.mult))
            do(nc.vector.tensor_tensor(cin[:, F:ABW], cin[:, F:ABW], e[:, 1, :], ALU.mult))
            nc.vector.tensor_tensor(got[:, 0:ABW], got[:, 0:ABW], cin[:, :], ALU.add).then_inc(mended, 1)

            def stage(k, b):
                nc.vector.tensor_copy(ends[b][:, :], R["end"][:, bass.ds(k * JB, JB)]).then_inc(staged, 1)

            def step(i, b, first=False, more=True):
                k = i * 2 + b
                do = Order(dve, chain, base + k * 3)
                cols = bass.ds(k * JB, JB)
                dve.wait_ge(gathered[b], i * 16 * JB + 16 * JB)
                do(nc.vector.reciprocal(inv[:, :, :], q[b][:, :, F:F + H]))
                do(nc.vector.tensor_tensor(inv[:, :, :], inv[:, :, :], R["pres"][:, cols].unsqueeze(2).to_broadcast([NP, JB, H]), ALU.mult))
                if not first:
                    dve.wait_ge(out_done[b], i * 16)
                do(nc.vector.tensor_tensor(res[b][:, :, :].rearrange("n j (h d) -> n j h d", h=H),
                                           q[b][:, :, 0:F].rearrange("n j (h d) -> n j h d", h=H),
                                           inv[:, :, :].unsqueeze(3).to_broadcast([NP, JB, H, HD]), ALU.mult))
                nc.vector.tensor_tensor(res[b][:, :, :], res[b][:, :, :], R["base"][:, cols, :], ALU.add).then_inc(res_ready, 1)
                if more:
                    stage(k + 2, b)

            base = do.n
            stage(0, 0)
            stage(1, 1)
            for b in range(2):
                step(0, b, first=True)
            with dve.Fori(1, NS // 2 - 1) as i:
                for b in range(2):
                    step(i, b)
            for b in range(2):
                step(NS // 2 - 1, b, more=False)


def gnn_program(nc, A, out):
    D = {
        "samples": nc.dram_tensor("samples", [SB], i32).ap(),
        "sums": nc.dram_tensor("sums", [P * RUN + N, F], f32).ap(),
        "states": nc.dram_tensor("states", [P * RUN, ROW], f32).ap(),
        "s_proj": nc.dram_tensor("s_proj", [N, F], f32).ap(),
        "r_proj": nc.dram_tensor("r_proj", [N, F], f32).ap(),
    }
    with ExitStack() as ctx:
        shapes = {
            "base": ([NP, NJ, F], f32), "src": ([P, RUN], i32), "keep": ([P, RUN], f32), "ident": ([P, P], f32),
            "w1g1": ([P, 2 * F], f32), "w2g2": ([P, 2 * F], f32), "b1g1": ([P, 1], f32),
            "b2g2": ([P, 2 * F], f32),
            "wsr": ([F, 2 * F], f32), "bsr": ([P, 2 * F], f32), "aw": ([P, F], f32), "ab": ([P, 1], f32),
            "pres": ([NP, NJ], f32), "end": ([NP, NJ], f32), "start": ([NP, NJ], f32),
            "first": ([P, 1], i32), "mend": ([P, 1], i32), "cont": ([P, 1], f32), "onward": ([P, 1], f32),
            "whole": ([P, 1], f32), "state": ([P, ROW], f32),
        }
        R = {k: ctx.enter_context(nc.sbuf_tensor(f"r_{k}", s, d)) for k, (s, d) in shapes.items()}
        edge_mlp(nc, R, A, D)
        update_nodes(nc, R, A, D)
        attention(nc, R, A, D)
        finish(nc, R, A, D, out)


_INS = ["x", "src", "dst", "edge_attr_64", "L0_gnn_W1", "L0_gnn_b1", "L0_gnn_W2", "L0_gnn_b2", "L0_gnn_G1", "L0_gnn_g1",
        "L0_gnn_G2", "L0_gnn_g2", "L1_gnn_Ws", "L1_gnn_bs", "L1_gnn_Wr", "L1_gnn_br", "L1_gnn_aw", "L1_gnn_ab"]


def kernel(**inputs):
    import numpy as np
    import concourse.bacc as bacc
    from concourse.bass_utils import run_bass_kernel_spmd

    nc = bacc.Bacc("TRN2", target_bir_lowering=False, num_devices=1)
    arrays, args = {}, {}
    for name in _INS:
        a = np.ascontiguousarray(inputs[name])
        arrays[f"in_{name}"] = a
        args[name] = nc.dram_tensor(f"in_{name}", a.shape, mybir.dt.from_np(a.dtype), kind="ExternalInput").ap()
    out = nc.dram_tensor("out_0", (N, F), f32, kind="ExternalOutput").ap()
    gnn_program(nc, args, out)
    return run_bass_kernel_spmd(nc, [arrays], core_ids=[0]).results[0]["out_0"]
```
